# Optimizing a Trainium2 kernel written in Bass

```python
import numpy as np
import jax
import jax.numpy as jnp

def _softmax(x, axis=-1):
    return jax.nn.softmax(x, axis=axis)

def _gelu(x):
    return jax.nn.gelu(x, approximate=True)

def _silu(x):
    return jax.nn.silu(x)

def _sigmoid(x):
    return jax.nn.sigmoid(x)

def _layernorm(x, axis=-1, eps=1e-05):
    m = jnp.mean(x, axis=axis, keepdims=True)
    v = jnp.var(x, axis=axis, keepdims=True)
    return (x - m) / jnp.sqrt(v + eps)

def _scatter_add(tgt, idx, src, axis=0):
    return tgt.at[idx].add(src)

def _segment_sum(src, seg, n):
    return jax.ops.segment_sum(src, seg, n)
kernel_name = 'mk_recurrent_d1_jaxref_r8_96dd47'

def setup_inputs(seed: int=0):
    np.random.seed(seed)
    _w = jnp.asarray

    def _L0_attn_setup():
        import jax, jax.numpy as jnp
        import numpy as np
        H_SIZE = 256
        N_HEADS = 32
        D_HEAD = 64
        D_STATE = 64
        D_CONV = 4
        N_GROUPS = 1
        INTER = 1024
        D_INNER = N_HEADS * D_HEAD
        D_BC = N_GROUPS * D_STATE
        XBC_LEN = D_INNER + 2 * D_BC
        PROJ = D_INNER + XBC_LEN + N_HEADS
        EPS = 1e-05

        def rmsnorm(x, w):
            var = jnp.mean(x * x, axis=-1, keepdims=True)
            return w * (x * jax.lax.rsqrt(var + EPS))

        def mamba2(xn, in_proj_w, conv_w, conv_b, A_log, D_param, dt_bias, mnorm_w, out_proj_w):
            B, L, _ = xn.shape
            xz = xn @ in_proj_w.T
            z = xz[..., :D_INNER]
            xBC = xz[..., D_INNER:D_INNER + XBC_LEN]
            dt_proj = xz[..., D_INNER + XBC_LEN:]
            xc = jnp.transpose(xBC, (0, 2, 1))
            xc = jax.lax.conv_general_dilated(xc, conv_w, window_strides=(1,), padding=[(D_CONV - 1, 0)], dimension_numbers=('NCH', 'OIH', 'NCH'), feature_group_count=XBC_LEN)
            xc = jax.nn.silu(xc + conv_b[None, :, None])
            xc = jnp.transpose(xc, (0, 2, 1))
            x_conv = xc[..., :D_INNER]
            B_proj = xc[..., D_INNER:D_INNER + D_BC]
            C_proj = xc[..., D_INNER + D_BC:]
            dt = jax.nn.softplus(dt_proj + dt_bias)
            A = -jnp.exp(A_log)
            x_heads = x_conv.reshape(B, L, N_HEADS, D_HEAD)
            xs = jnp.moveaxis(x_heads, 1, 0)
            dts = jnp.moveaxis(dt, 1, 0)
            Bs = jnp.moveaxis(B_proj, 1, 0)
            Cs = jnp.moveaxis(C_proj, 1, 0)
            h0 = jnp.zeros((B, N_HEADS, D_HEAD, D_STATE), xn.dtype)

            def step(h, inp):
                x_t, dt_t, B_t, C_t = inp
                dA = jnp.exp(A[None, :] * dt_t)
                dBx = dt_t[..., None, None] * x_t[..., None] * B_t[:, None, None, :]
                h = dA[..., None, None] * h + dBx
                y = jnp.einsum('bhps,bs->bhp', h, C_t) + D_param[None, :, None] * x_t
                return (h, y)
            _, ys = jax.lax.scan(step, h0, (xs, dts, Bs, Cs))
            y = jnp.moveaxis(ys, 0, 1).reshape(B, L, D_INNER)
            y = y * jax.nn.silu(z)
            y = rmsnorm(y, mnorm_w)
            return y @ out_proj_w.T
        key = jax.random.key(seed)
        ks = jax.random.split(key, 10)
        s = 0.02
        B, L = (1, 128)
        return {'x': jax.random.normal(ks[0], (B, L, H_SIZE), jnp.float32), 'ln1_w': jnp.ones((H_SIZE,), jnp.float32), 'in_proj_w': jax.random.normal(ks[1], (PROJ, H_SIZE), jnp.float32) * s, 'conv_w': jax.random.normal(ks[2], (XBC_LEN, 1, D_CONV), jnp.float32) * 0.2, 'conv_b': jnp.zeros((XBC_LEN,), jnp.float32), 'A_log': jax.random.uniform(ks[3], (N_HEADS,), jnp.float32, 0.0, 1.0), 'D_param': jnp.ones((N_HEADS,), jnp.float32), 'dt_bias': jax.random.normal(ks[4], (N_HEADS,), jnp.float32) * s, 'mnorm_w': jnp.ones((D_INNER,), jnp.float32), 'out_proj_w': jax.random.normal(ks[5], (H_SIZE, D_INNER), jnp.float32) * s, 'ln2_w': jnp.ones((H_SIZE,), jnp.float32), 'mlp_in_w': jax.random.normal(ks[6], (2 * INTER, H_SIZE), jnp.float32) * s, 'mlp_out_w': jax.random.normal(ks[7], (H_SIZE, INTER), jnp.float32) * s}
    _L0_attn_in = _L0_attn_setup()

    def _L0_ffn_setup():
        import jax, jax.numpy as jnp
        import numpy as np
        HIDDEN = 256
        N_EXPERTS = 8
        N_SHARED = 2
        TOP_K = 2
        MOE_FF = 176
        SHARED_FF = N_SHARED * MOE_FF
        SCALE = 2.5
        BATCH, SEQ = (2, 128)
        key = jax.random.key(seed)
        ks = jax.random.split(key, 8)
        s = 0.02
        return {'hidden_states': jax.random.normal(ks[0], (BATCH, SEQ, HIDDEN), jnp.float32), 'gate_w': jax.random.normal(ks[1], (N_EXPERTS, HIDDEN), jnp.float32) * s, 'shared_wg': jax.random.normal(ks[2], (SHARED_FF, HIDDEN), jnp.float32) * s, 'shared_wu': jax.random.normal(ks[3], (SHARED_FF, HIDDEN), jnp.float32) * s, 'shared_wd': jax.random.normal(ks[4], (HIDDEN, SHARED_FF), jnp.float32) * s, 'exp_wg': jax.random.normal(ks[5], (N_EXPERTS, MOE_FF, HIDDEN), jnp.float32) * s, 'exp_wu': jax.random.normal(ks[6], (N_EXPERTS, MOE_FF, HIDDEN), jnp.float32) * s, 'exp_wd': jax.random.normal(ks[7], (N_EXPERTS, HIDDEN, MOE_FF), jnp.float32) * s}
    _L0_ffn_in = _L0_ffn_setup()
    _d = {'L0_attn_x': _L0_attn_in['x'], 'L0_attn_ln1_w': _L0_attn_in['ln1_w'], 'L0_attn_in_proj_w': _L0_attn_in['in_proj_w'], 'L0_attn_conv_w': _L0_attn_in['conv_w'], 'L0_attn_conv_b': _L0_attn_in['conv_b'], 'L0_attn_A_log': _L0_attn_in['A_log'], 'L0_attn_D_param': _L0_attn_in['D_param'], 'L0_attn_dt_bias': _L0_attn_in['dt_bias'], 'L0_attn_mnorm_w': _L0_attn_in['mnorm_w'], 'L0_attn_out_proj_w': _L0_attn_in['out_proj_w'], 'L0_attn_ln2_w': _L0_attn_in['ln2_w'], 'L0_attn_mlp_in_w': _L0_attn_in['mlp_in_w'], 'L0_attn_mlp_out_w': _L0_attn_in['mlp_out_w'], 'L0_ffn_gate_w': _L0_ffn_in['gate_w'], 'L0_ffn_shared_wg': _L0_ffn_in['shared_wg'], 'L0_ffn_shared_wu': _L0_ffn_in['shared_wu'], 'L0_ffn_shared_wd': _L0_ffn_in['shared_wd'], 'L0_ffn_exp_wg': _L0_ffn_in['exp_wg'], 'L0_ffn_exp_wu': _L0_ffn_in['exp_wu'], 'L0_ffn_exp_wd': _L0_ffn_in['exp_wd']}
    _x0 = _d['L0_attn_x']
    _d['L0_attn_x'] = jax.random.normal(jax.random.fold_in(jax.random.key(seed), 1), (4, 256, 256), dtype=_x0.dtype)
    del _x0
    return _d

def reference(L0_attn_x, L0_attn_ln1_w, L0_attn_in_proj_w, L0_attn_conv_w, L0_attn_conv_b, L0_attn_A_log, L0_attn_D_param, L0_attn_dt_bias, L0_attn_mnorm_w, L0_attn_out_proj_w, L0_attn_ln2_w, L0_attn_mlp_in_w, L0_attn_mlp_out_w, L0_ffn_gate_w, L0_ffn_shared_wg, L0_ffn_shared_wu, L0_ffn_shared_wd, L0_ffn_exp_wg, L0_ffn_exp_wu, L0_ffn_exp_wd):

    def _L0_attn_ref(x, ln1_w, in_proj_w, conv_w, conv_b, A_log, D_param, dt_bias, mnorm_w, out_proj_w, ln2_w, mlp_in_w, mlp_out_w):
        import jax, jax.numpy as jnp
        import numpy as np
        H_SIZE = 256
        N_HEADS = 32
        D_HEAD = 64
        D_STATE = 64
        D_CONV = 4
        N_GROUPS = 1
        INTER = 1024
        D_INNER = N_HEADS * D_HEAD
        D_BC = N_GROUPS * D_STATE
        XBC_LEN = D_INNER + 2 * D_BC
        PROJ = D_INNER + XBC_LEN + N_HEADS
        EPS = 1e-05

        def rmsnorm(x, w):
            var = jnp.mean(x * x, axis=-1, keepdims=True)
            return w * (x * jax.lax.rsqrt(var + EPS))

        def mamba2(xn, in_proj_w, conv_w, conv_b, A_log, D_param, dt_bias, mnorm_w, out_proj_w):
            B, L, _ = xn.shape
            xz = xn @ in_proj_w.T
            z = xz[..., :D_INNER]
            xBC = xz[..., D_INNER:D_INNER + XBC_LEN]
            dt_proj = xz[..., D_INNER + XBC_LEN:]
            xc = jnp.transpose(xBC, (0, 2, 1))
            xc = jax.lax.conv_general_dilated(xc, conv_w, window_strides=(1,), padding=[(D_CONV - 1, 0)], dimension_numbers=('NCH', 'OIH', 'NCH'), feature_group_count=XBC_LEN)
            xc = jax.nn.silu(xc + conv_b[None, :, None])
            xc = jnp.transpose(xc, (0, 2, 1))
            x_conv = xc[..., :D_INNER]
            B_proj = xc[..., D_INNER:D_INNER + D_BC]
            C_proj = xc[..., D_INNER + D_BC:]
            dt = jax.nn.softplus(dt_proj + dt_bias)
            A = -jnp.exp(A_log)
            x_heads = x_conv.reshape(B, L, N_HEADS, D_HEAD)
            xs = jnp.moveaxis(x_heads, 1, 0)
            dts = jnp.moveaxis(dt, 1, 0)
            Bs = jnp.moveaxis(B_proj, 1, 0)
            Cs = jnp.moveaxis(C_proj, 1, 0)
            h0 = jnp.zeros((B, N_HEADS, D_HEAD, D_STATE), xn.dtype)

            def step(h, inp):
                x_t, dt_t, B_t, C_t = inp
                dA = jnp.exp(A[None, :] * dt_t)
                dBx = dt_t[..., None, None] * x_t[..., None] * B_t[:, None, None, :]
                h = dA[..., None, None] * h + dBx
                y = jnp.einsum('bhps,bs->bhp', h, C_t) + D_param[None, :, None] * x_t
                return (h, y)
            _, ys = jax.lax.scan(step, h0, (xs, dts, Bs, Cs))
            y = jnp.moveaxis(ys, 0, 1).reshape(B, L, D_INNER)
            y = y * jax.nn.silu(z)
            y = rmsnorm(y, mnorm_w)
            return y @ out_proj_w.T
        h = mamba2(rmsnorm(x, ln1_w), in_proj_w, conv_w, conv_b, A_log, D_param, dt_bias, mnorm_w, out_proj_w)
        x = x + h
        hh = rmsnorm(x, ln2_w) @ mlp_in_w.T
        gate, up = (hh[..., :INTER], hh[..., INTER:])
        h2 = jax.nn.silu(gate) * up @ mlp_out_w.T
        return x + h2

    def _L0_ffn_ref(hidden_states, gate_w, shared_wg, shared_wu, shared_wd, exp_wg, exp_wu, exp_wd):
        import jax, jax.numpy as jnp
        import numpy as np
        HIDDEN = 256
        N_EXPERTS = 8
        N_SHARED = 2
        TOP_K = 2
        MOE_FF = 176
        SHARED_FF = N_SHARED * MOE_FF
        SCALE = 2.5
        BATCH, SEQ = (2, 128)
        B, S, D = hidden_states.shape
        T = B * S
        xf = hidden_states.reshape(T, D)
        scores = jax.nn.sigmoid(xf @ gate_w.T)
        topk_w, topk_idx = jax.lax.top_k(scores, TOP_K)
        topk_w = topk_w / (topk_w.sum(axis=-1, keepdims=True) + 1e-20)
        topk_w = topk_w * SCALE
        shared_out = jax.nn.silu(xf @ shared_wg.T) * (xf @ shared_wu.T) @ shared_wd.T
        h = jax.nn.silu(jnp.einsum('td,efd->etf', xf, exp_wg)) * jnp.einsum('td,efd->etf', xf, exp_wu)
        all_out = jnp.einsum('etf,edf->etd', h, exp_wd)
        picked = all_out[topk_idx, jnp.arange(T)[:, None]]
        routed_out = (topk_w[..., None] * picked).sum(axis=1)
        return (shared_out + routed_out).reshape(B, S, D)
    x = L0_attn_x
    xn = _layernorm(x, axis=-1)
    s = _L0_attn_ref(xn, L0_attn_ln1_w, L0_attn_in_proj_w, L0_attn_conv_w, L0_attn_conv_b, L0_attn_A_log, L0_attn_D_param, L0_attn_dt_bias, L0_attn_mnorm_w, L0_attn_out_proj_w, L0_attn_ln2_w, L0_attn_mlp_in_w, L0_attn_mlp_out_w)
    g = _silu(_L0_ffn_ref(xn, L0_ffn_gate_w, L0_ffn_shared_wg, L0_ffn_shared_wu, L0_ffn_shared_wd, L0_ffn_exp_wg, L0_ffn_exp_wu, L0_ffn_exp_wd))
    x = x + s * g
    return x

_drawn_inputs = setup_inputs


def setup_inputs(seed=0):
    import zlib

    import numpy as np

    out = dict(_drawn_inputs(seed))
    spreads = {'L0_attn_ln1_w': (1.0, 0.6),
     'L0_attn_conv_b': (0.0, 0.8),
     'L0_attn_D_param': (1.0, 0.6),
     'L0_attn_mnorm_w': (1.0, 0.6),
     'L0_attn_ln2_w': (1.0, 0.6)}
    factors = {'L0_attn_in_proj_w': 3.862,
     'L0_attn_conv_w': 4.776,
     'L0_attn_A_log': 8.0,
     'L0_attn_dt_bias': 8.0,
     'L0_attn_out_proj_w': 3.836,
     'L0_attn_mlp_in_w': 8.0,
     'L0_attn_mlp_out_w': 8.0,
     'L0_ffn_gate_w': 3.84,
     'L0_ffn_shared_wg': 4.202,
     'L0_ffn_shared_wu': 4.154,
     'L0_ffn_shared_wd': 4.172,
     'L0_ffn_exp_wg': 3.379,
     'L0_ffn_exp_wu': 3.337,
     'L0_ffn_exp_wd': 3.319}
    for name, (base, spread) in spreads.items():
        noise = np.random.default_rng([zlib.crc32(name.encode()), seed]).standard_normal(out[name].shape)
        drawn = base * np.exp(spread * noise) if base else spread * noise
        out[name] = jnp.asarray(drawn.astype(out[name].dtype))
    for name, factor in factors.items():
        out[name] = (out[name] * factor).astype(out[name].dtype)
    return out
```

```python
from contextlib import ExitStack

import concourse.bass as bass
from concourse import mybir
from concourse.alu_op_type import AluOpType as ALU

ACT = mybir.ActivationFunctionType
F32 = mybir.dt.float32
BF16 = mybir.dt.bfloat16
U32 = mybir.dt.uint32
AX_X = mybir.AxisListType.X

P = 128
BATCH, SEQ, HID = 4, 256, 256
TOK = BATCH * SEQ
TT = TOK // P
KH = HID // P
HEADS, HD, NST, TAPS = 32, 64, 64, 4
DIN = HEADS * HD
CT = DIN // P
PAIRS = CT // 2
INTER = 1024
NE, FF, SFF = 8, 176, 352
FT = -(-(NE * FF + SFF) // P)
MT = INTER // P
FFP = FT * P
ROUTED_SCALE = 2.5
EPS = 1e-5
SPLIT = 3
GT = 4
GROUPS = TT // GT
CREDIT = 4

RING = (0, 1, 2)
BC0A, BC0B, BC1, YB, OPB = 3, 4, 5, 6, 7

SETUP = ([(("xr", q), q) for q in range(4)] + [(("dt", 0), 6)] + [(("xn", q), 4 + q) for q in range(4)]
         + [(("gate", 0), 7), (("decay", 0), 0), (("decay", 1), 1), (("comb", 0), 3), (("comb", 1), 4)])


def first_projection():
    return [(("xp", p), RING[p % 3]) for p in range(PAIRS + 1)]


def sequence_items(last):
    keys = [("s", 0)]
    for i in range(PAIRS + 3):
        if i < PAIRS:
            keys += [("xtr", i), ("z", i)]
        if 2 <= i < PAIRS + 2 and not last:
            keys.append(("xp", i - 2))
        if i == PAIRS + 2:
            keys += ([] if last else [("xp", PAIRS)]) + [("ssq", 0)]
    items = [(k, RING[n % 3]) for n, k in enumerate(keys)]
    for i in range(PAIRS):
        items += [(("bc0a", i), BC0A), (("bc0b", i), BC0B), (("bc1", i), BC1), (("y", i), YB)]
    return items + [(("op", 0), OPB)]


def group_items():
    items = []
    for m in range(FT + MT):
        items += [(("gate", m), m % 2), (("up", m), 2 + m % 2)]
        if m < FT:
            items.append((("comb", m), 4))
    return items + [(("x1t", k), 5) for k in range(KH)] + [(("acc", a, h), 6 + h) for a in range(2) for h in range(2)]


class Banks:

    def __init__(self):
        self.base = [0] * 8

    def phase(self, items, times=1):
        base, seen, table = list(self.base), [0] * 8, {}
        for key, bank in items:
            table[key] = (bank, base[bank], seen[bank])
            seen[bank] += 1
        self.base = [b + times * n for b, n in zip(self.base, seen)]
        return {k: (bank, b0, seen[bank], n) for k, (bank, b0, n) in table.items()}


BANKS = Banks()
IN_SETUP = BANKS.phase(SETUP)
IN_FIRST = BANKS.phase(first_projection())
IN_SEQ = BANKS.phase(sequence_items(False), BATCH - 1)
IN_LAST = BANKS.phase(sequence_items(True))
IN_GROUP = BANKS.phase(group_items(), GROUPS)


def fills(table, key, it=0):
    bank, base, per, n = table[key]
    return bank, it * per + (base + n)


def build(nc, x, wx, wz, wdt, wo, wgu, wd, wmi, wmo, wgate, conv_w, conv_b, a_log, dt_bias, d_col,
          mnorm, ln1, ln2, ident_in, eye_in, sel_head_in, sel_exp_in, iota_in, out):
    with ExitStack() as ctx:
        def sb(name, shape, dt=F32):
            return ctx.enter_context(nc.sbuf_tensor(name, shape, dt))

        def sem(name):
            return ctx.enter_context(nc.semaphore(name))

        wx_sb = sb("wx_sb", [P, KH * (DIN + 2 * NST)])
        wz_sb = sb("wz_sb", [P, KH * DIN])
        wo_sb = sb("wo_sb", [P, CT, HID])
        wgu_sb = sb("wgu_sb", [P, KH, 2, FFP])
        wmo_sb = sb("wmo_sb", [P, MT, HID])
        wdt_sb = sb("wdt_sb", [P, KH, HEADS])
        wgate_sb = sb("wgate_sb", [P, KH, NE])
        wx_v = wx_sb[:, :].rearrange("p (k n) -> p k n", k=KH)
        wz_v = wz_sb[:, :].rearrange("p (k n) -> p k n", k=KH)
        wd_v = wx_sb[:, 0:FT * HID].rearrange("p (m n) -> p m n", m=FT)
        wmi_v = wz_sb[:, 0:KH * 2 * INTER].rearrange("p (k g n) -> p k g n", k=KH, g=2)
        cw = sb("cw", [P, CT + 1, TAPS])
        cb = sb("cb", [P, CT + 1])
        arow = sb("arow", [P, HEADS])
        dtb = sb("dtb", [P, HEADS])
        dcol = sb("dcol", [P, CT])
        mn = sb("mn", [P, CT])
        ln1_sb = sb("ln1_sb", [P, KH])
        ln2_sb = sb("ln2_sb", [P, KH])
        ident = sb("ident", [P, P])
        eye = sb("eye", [P, 2, 512])
        sel_head = sb("sel_head", [SPLIT * HEADS, HEADS], BF16)
        sel_exp = sb("sel_exp", [SPLIT * 32, FFP], BF16)
        iota = sb("iota", [P, TT, NE])
        ones = sb("ones", [P, 1])
        power = sb("power", [P, TT])
        xn_all = sb("xn_all", [P, TT, HID])
        xnT = sb("xnT", [P, KH, TOK])
        xrT = sb("xrT", [P, KH, TOK])
        dt_tok = sb("dt_tok", [P, TT, HEADS])
        decay0 = sb("decay0", [SPLIT * HEADS, TOK], BF16)
        decay1 = sb("decay1", [SPLIT * HEADS, BATCH * P], BF16)
        comb_split = sb("comb_split", [SPLIT * 32, TOK], BF16)
        xsT = sb("xsT", [P, CT * SEQ])
        xsT_v = xsT[:, :].rearrange("p (j t) -> p j t", j=CT)
        bT = sb("bT", [NST, SEQ])
        cT = sb("cT", [NST, SEQ])
        acc = sb("acc", [P, 2, 2, SEQ])
        xtok = sb("xtok", [P, 2, 2, 256])
        xdt = sb("xdt", [P, 2, 2, 256])
        sz = sb("sz", [P, 2, 512])
        m0 = sb("m0", [P, 2, 4, SEQ])
        m1 = sb("m1", [P, 2, 4, P])
        y_sb = sb("y_sb", [P, 2, 512])
        gT = sb("gT", [P, 4, 512])
        sq = sb("sq", [P, 2, 512])
        gsq = sb("gsq", [P, 512])
        s_sb = sb("s_sb", [P, SEQ + P])
        var_g = sb("var_g", [P, 2])
        rstd_g = sb("rstd_g", [P, 2])
        sg = sb("sg", [P, 2, 512])
        hid = sb("hid", [P, 2, 512])
        ssq_x1 = sb("ssq_x1", [P, GT])
        var_x1 = sb("var_x1", [P, GT])
        rstd_x1 = sb("rstd_x1", [P, GT])
        x1r = xsT[:, 0:1024].rearrange("p (q n) -> p q n", q=GT)
        res = xsT[:, 1024:2048].rearrange("p (q n) -> p q n", q=GT)
        gm = xsT[:, 2048:3072].rearrange("p (q n) -> p q n", q=GT)
        xf = xsT[:, 3072:4096].rearrange("p (q n) -> p q n", q=GT)
        x1T = m0[:, 0, :, :].rearrange("p (k q) t -> p k (q t)", k=KH)
        x_all = m0[:, :, :, :].rearrange("p a b c -> p (a b) c")
        xr_all = gT[:, :, :].rearrange("p a (b c) -> p (a b) c", b=2)
        junk = xsT[:, 2048:4096].rearrange("p (t n) -> p t n", t=TT)
        st = sb("st", [P, 6, TT])
        wk = xsT[:, :].rearrange("p (n t h) -> p n t h", n=16, t=TT)
        decT = xsT[0:HEADS, 2048:3072]
        part = xsT[0:HEADS, 3072:4096]
        mid = m1[0:HEADS, :, :, :].rearrange("p a b c -> p (a b c)").bitcast(BF16)
        rk = y_sb[:, :, :].rearrange("p a b -> p (a b)")
        score, prob, top, mask0, mask1, wsc = (rk[:, 64 * n:64 * n + 64].rearrange("p (t e) -> p t e", t=TT)
                                               for n in range(6))
        topi = rk[:, 384:448].bitcast(U32).rearrange("p (t e) -> p t e", t=TT)
        topf = rk[:, 448:512].rearrange("p (t e) -> p t e", t=TT)
        wsum = rk[:, 512:520]
        wnorm = rk[:, 520:528]
        combx = rk[:, 576:576 + TT * (NE + 1)].rearrange("p (t e) -> p t e", t=TT)
        combT = acc[0:32, :, :, :].rearrange("p a b c -> p (a b c)")
        cpart = xtok[0:32, :, :, :].rearrange("p a b c -> p (a b c)")
        cmid = xdt[0:32, :, :, :].rearrange("p a b c -> p (a b c)").bitcast(BF16)

        bank = [ctx.enter_context(nc.psum_tensor(f"bank{n}", [P, 512], F32)) for n in range(8)]
        bank_full = [sem(f"bank_full{n}") for n in range(8)]
        bank_free = [sem(f"bank_free{n}") for n in range(8)]

        loaded = {n: sem(f"loaded_{n}") for n in
                  ("x", "small", "wx", "wz", "wo", "wgu", "wmo", "wd", "wmi", "xf")}
        v_step, a_step, p_step = sem("v_step"), sem("a_step"), sem("p_step")
        names = ("xtok_ready", "xdt_ready", "sz_ready", "scan_step", "m0_step", "m1_ready", "y_ready", "g_ready",
                 "sq_ready", "gsq_ready", "tap_ready", "conv_step", "xs_ready", "s_ready", "op_done",
                 "var_ready", "rstd_ready", "x1_ready",
                 "sg_ready", "hid_step", "hid_ready", "down_done", "ssq_ready", "var1_ready", "rstd1_ready", "x1r_ready",
                 "x1t_ready", "gm_ready", "res_ready", "prod_ready", "sum_ready")
        S = {n: sem(n) for n in names}
        stored = sem("stored")
        block = ctx.enter_context(nc.Block())

        def await_full(eng, table, key, it=0):
            b, n = fills(table, key, it)
            eng.wait_ge(bank_full[b], n + 1)
            return bank[b]

        def await_free(eng, table, key, it=0):
            b, n = fills(table, key, it)
            if not (isinstance(n, int) and n == 0):
                eng.wait_ge(bank_free[b], n)
            return bank[b]

        def is_full(ins, table, key):
            ins.then_inc(bank_full[table[key][0]], 1)

        def is_free(ins, table, key):
            ins.then_inc(bank_free[table[key][0]], 1)

        def reached(eng, name, n):
            eng.wait_ge(S[name], n + CREDIT)

        def sequences(eng):
            with eng.Fori(0, BATCH - 1) as b:
                yield b, IN_SEQ, False
            yield BATCH - 1, IN_LAST, True

        def at(b, n, size=1):
            return bass.ds(b * n, size) if not isinstance(b, int) else slice(b * n, b * n + size)

        UNITS = PAIRS + 1
        CONV = PAIRS * 6 + 3

        @block.sync
        def _(sp):
            sp.sem_inc(stored, 16)
            sp.dma_start(x_all, x).then_inc(loaded["x"], 16)
            small = [(ident, ident_in), (ln1_sb, ln1), (wdt_sb, wdt), (dtb, dt_bias), (arow, a_log),
                     (wgate_sb, wgate), (iota, iota_in), (cw, conv_w), (cb, conv_b), (dcol, d_col), (mn, mnorm),
                     (ln2_sb, ln2), (eye, eye_in), (sel_head, sel_head_in), (sel_exp, sel_exp_in)]
            for dst, src in small:
                sp.dma_start(dst[:], src).then_inc(loaded["small"], 16)
            sp.dma_start(wx_sb[:, :], wx).then_inc(loaded["wx"], 16)
            sp.dma_start(wz_sb[:, :], wz).then_inc(loaded["wz"], 16)
            sp.dma_start(wo_sb[:], wo).then_inc(loaded["wo"], 16)
            sp.dma_start(wgu_sb[:], wgu).then_inc(loaded["wgu"], 16)
            sp.dma_start(wmo_sb[:], wmo).then_inc(loaded["wmo"], 16)
            reached(sp, "conv_step", BATCH * CONV)
            sp.dma_start(wx_sb[:, 0:FT * HID], wd).then_inc(loaded["wd"], 16)
            reached(sp, "sz_ready", BATCH * PAIRS)
            sp.dma_start(wz_sb[:, :], wmi).then_inc(loaded["wmi"], 16)
            reached(sp, "y_ready", BATCH * PAIRS)
            with sp.Fori(0, GROUPS) as g:
                reached(sp, "sum_ready", g)
                sp.dma_start(xf, x[:, bass.ds(g * GT, GT), :]).then_inc(loaded["xf"], 16)
                reached(sp, "sum_ready", g + 1)
                sp.dma_start(out[:, bass.ds(g * GT, GT), :], res).then_inc(stored, 16)
            sp.wait_ge(stored, 16 * (GROUPS + 1))

        SMALL = 15 * 16

        @block.vector
        def _(dve):
            steps = [0]

            def step(ins):
                steps[0] += 1
                ins.then_inc(v_step, 1)
                dve.wait_ge(v_step, steps[0])

            for n in ("scan_step", "m0_step", "y_ready", "conv_step", "var_ready", "x1_ready", "hid_step", "hid_ready",
                      "var1_ready", "x1r_ready", "res_ready"):
                dve.sem_inc(S[n], CREDIT)
            dve.memset(power[:], -0.5)
            dve.memset(ones[:], 1.0)
            step(dve.memset(comb_split[:], 0.0))
            dve.wait_ge(loaded["x"], 16)
            step(dve.reduce_sum(st[:, 0, :], x_all, AX_X))
            step(dve.tensor_scalar(st[:, 1, :], st[:, 0, :], 1.0 / HID, None, ALU.mult))
            step(dve.tensor_tensor(xn_all[:], x_all, st[:, 1, :].unsqueeze(2).to_broadcast([P, TT, HID]), ALU.subtract))
            CENTRED = steps[0]
            assert CENTRED == V_CENTRED
            dve.wait_ge(a_step, A_SQUARES)
            step(dve.tensor_scalar(st[:, 2, :], st[:, 2, :], 1.0 / HID, None, ALU.mult))
            step(dve.tensor_scalar(st[:, 3, :], st[:, 2, :], EPS, None, ALU.add))
            assert steps[0] == V_VAR
            dve.wait_ge(p_step, 1)
            step(dve.tensor_tensor(st[:, 5, :], st[:, 4, :], st[:, 4, :], ALU.mult))
            step(dve.tensor_tensor(st[:, 5, :], st[:, 5, :], st[:, 2, :], ALU.mult))
            step(dve.tensor_scalar(st[:, 5, :], st[:, 5, :], EPS, None, ALU.add))
            assert steps[0] == V_VARN
            step(dve.tensor_tensor(xn_all[:], xn_all[:], st[:, 4, :].unsqueeze(2).to_broadcast([P, TT, HID]), ALU.mult))
            assert steps[0] == V_XN
            dve.wait_ge(p_step, 2)
            step(dve.tensor_tensor(xr_all, xn_all[:], st[:, 5, :].unsqueeze(2).to_broadcast([P, TT, HID]), ALU.mult))
            assert steps[0] == V_XR
            dve.wait_ge(loaded["small"], SMALL)
            pb = await_full(dve, IN_SETUP, ("dt", 0))
            v, q, e, lnu, d, r = (wk[:, n] for n in (0, 1, 2, 3, 4, 5))
            ins = dve.tensor_tensor(v, pb[:, 0:TT * HEADS].rearrange("p (t h) -> p t h", t=TT),
                                    dtb[:, :].unsqueeze(1).to_broadcast([P, TT, HEADS]), ALU.add)
            is_free(ins, IN_SETUP, ("dt", 0))
            dve.wait_ge(bank_free[6], 1)
            step(dve.tensor_scalar(q, v, 0.0, None, ALU.max))
            assert steps[0] == V_V
            dve.wait_ge(a_step, A_LN)
            step(dve.tensor_scalar(d, e, 1.0, -1.0, ALU.add, ALU.add))
            step(dve.tensor_scalar(r, d, 1e-30, None, ALU.max))
            step(dve.reciprocal(r, r))
            step(dve.tensor_tensor(lnu, lnu, r, ALU.mult))
            step(dve.tensor_scalar(d, d, 0.0, None, ALU.is_equal))
            step(dve.tensor_tensor(lnu, lnu, d, ALU.add))
            step(dve.tensor_tensor(lnu, lnu, e, ALU.mult))
            step(dve.tensor_tensor(dt_tok[:], q, lnu, ALU.add))
            step(dve.tensor_tensor(d, dt_tok[:], arow[:, :].unsqueeze(1).to_broadcast([P, TT, HEADS]), ALU.mult))
            assert steps[0] == V_LOGA
            pb = await_full(dve, IN_SETUP, ("gate", 0))
            dve.wait_ge(a_step, A_GATE)
            step(dve.tensor_scalar(score, prob, 1.0, None, ALU.add))
            step(dve.reciprocal(score, score))
            for t in range(TT):
                dve.max(top[:, t, :], score[:, t, :]).then_inc(v_step, 1)
            steps[0] += TT
            dve.wait_ge(v_step, steps[0])
            for t in range(TT):
                dve.max_index(topi[:, t, :], top[:, t, :], score[:, t, :]).then_inc(v_step, 1)
            steps[0] += TT
            dve.wait_ge(v_step, steps[0])
            step(dve.tensor_copy(topf, topi))
            step(dve.tensor_tensor(mask0, iota[:], topf[:, :, 0:1].to_broadcast([P, TT, NE]), ALU.is_equal))
            step(dve.tensor_tensor(mask1, iota[:], topf[:, :, 1:2].to_broadcast([P, TT, NE]), ALU.is_equal))
            step(dve.tensor_tensor(mask0, mask0, mask1, ALU.add))
            step(dve.tensor_tensor(wsc, mask0, score, ALU.mult))
            step(dve.reduce_sum(wsum, wsc, AX_X))
            step(dve.tensor_scalar(wsum, wsum, 1e-20, None, ALU.add))
            step(dve.reciprocal(wnorm, wsum))
            step(dve.memset(combx, 1.0))
            step(dve.tensor_tensor(wsc, wsc, wnorm.unsqueeze(2).to_broadcast([P, TT, NE]), ALU.mult))
            step(dve.tensor_scalar(combx[:, :, 0:NE], wsc, ROUTED_SCALE, None, ALU.mult))
            assert steps[0] == V_COMB, steps[0]
            for n in range(2):
                pb = await_full(dve, IN_SETUP, ("decay", n))
                ins = dve.tensor_copy(decT[:, 512 * n:512 * n + 512], pb[0:HEADS, :])
                is_free(ins, IN_SETUP, ("decay", n))
            dve.wait_ge(bank_free[0], 2)
            dve.wait_ge(bank_free[1], 2)
            dec_c = decT.rearrange("h (b c t) -> h b c t", b=BATCH, c=2)
            step(dve.memset(decT.rearrange("h (b t) -> h b t", b=BATCH)[:, :, 0:1], 0.0))
            step(dve.tensor_copy(decay0[0:HEADS, :], decT))
            step(dve.tensor_tensor(part, decT, decay0[0:HEADS, :], ALU.subtract))
            step(dve.tensor_copy(mid[:, 0:TOK], part))
            step(dve.tensor_copy(decay0[HEADS:2 * HEADS, :], mid[:, 0:TOK]))
            step(dve.tensor_tensor(decay0[2 * HEADS:3 * HEADS, :], part, mid[:, 0:TOK], ALU.subtract))
            step(dve.tensor_copy(decay1[:, :].rearrange("h (b t) -> h b t", b=BATCH),
                                 decay0[:, :].rearrange("h (b c t) -> h b c t", b=BATCH, c=2)[:, :, 1, :]))
            step(dve.memset(decay1[:, :].rearrange("h (b t) -> h b t", b=BATCH)[:, :, 0:1], 0.0))
            assert steps[0] == V_DECAY, steps[0]
            NR = NE + 1
            for n in range(2):
                pb = await_full(dve, IN_SETUP, ("comb", n))
                ins = dve.tensor_copy(combT[0:NR, 512 * n:512 * n + 512], pb[0:NR, :])
                is_free(ins, IN_SETUP, ("comb", n))
            dve.wait_ge(bank_free[3], 2)
            dve.wait_ge(bank_free[4], 2)
            step(dve.tensor_copy(comb_split[0:NR, :], combT[0:NR, :]))
            step(dve.tensor_tensor(cpart[0:NR, :], combT[0:NR, :], comb_split[0:NR, :], ALU.subtract))
            step(dve.tensor_copy(cmid[0:NR, 0:TOK], cpart[0:NR, :]))
            step(dve.tensor_copy(comb_split[32:32 + NR, :], cmid[0:NR, 0:TOK]))
            step(dve.tensor_tensor(comb_split[64:64 + NR, :], cpart[0:NR, :], cmid[0:NR, 0:TOK], ALU.subtract))
            assert steps[0] == V_SPLIT, steps[0]

            def convolve(unit, table, key, it, it_units):
                pb = await_full(dve, table, key, it)
                reached(dve, "tap_ready", it_units * UNITS + unit + 1)
                tiles = 2 if unit < PAIRS else 1
                at0 = it_units * CONV + unit * 6
                for s in range(1, TAPS):
                    for jj in range(tiles):
                        if s > 1:
                            reached(dve, "conv_step", at0 + (s - 2) * tiles + jj + 1)
                        a = acc[:, unit % 2, jj, s:SEQ]
                        ins = dve.scalar_tensor_tensor(a, pb[:, jj * SEQ:jj * SEQ + SEQ - s],
                                                       cw[:, 2 * unit + jj, TAPS - 1 - s:TAPS - s], a, ALU.mult, ALU.add)
                        ins.then_inc(S["conv_step"], 1)
                reached(dve, "conv_step", at0 + 3 * tiles)
                dve.sem_inc(bank_free[table[key][0]], 1)

            for unit in range(UNITS):
                convolve(unit, IN_FIRST, ("xp", unit), 0, 0)
            dve.wait_ge(loaded["wo"], 16)
            for j in range(CT):
                ins = dve.tensor_scalar(wo_sb[:, j, :], wo_sb[:, j, :], mn[:, j:j + 1], None, ALU.mult)
            ins.then_inc(v_step, 1)
            assert steps[0] + 1 == V_WO

            for b, table, last in sequences(dve):
                for i in range(PAIRS + 3):
                    if i < PAIRS:
                        r = i % 2
                        n3 = (b * PAIRS + i) * 3
                        b6, f6 = fills(table, ("y", i), b if not last else 0)
                        dve.wait_ge(bank_full[b6], f6 - 1)
                        pa = await_full(dve, table, ("bc0a", i), b if not last else 0)
                        ins = dve.tensor_tensor_scan(m0[:, r, 0:2, :].rearrange("p h t -> p (h t)"), pa[:, :], eye[:, 0, :],
                                                     0.0, ALU.mult, ALU.add)
                        ins.then_inc(S["scan_step"], 1)
                        pc = await_full(dve, table, ("bc0b", i), b if not last else 0)
                        ins = dve.tensor_tensor_scan(m0[:, r, 2:4, :].rearrange("p h t -> p (h t)"), pc[:, :], eye[:, 0, :],
                                                     0.0, ALU.mult, ALU.add)
                        ins.then_inc(S["scan_step"], 1)
                        pd = await_full(dve, table, ("bc1", i), b if not last else 0)
                        ins = dve.tensor_tensor_scan(m1[:, r, :, :].rearrange("p h t -> p (h t)"), pd[:, :], eye[:, 1, :],
                                                     0.0, ALU.mult, ALU.add)
                        ins.then_inc(S["scan_step"], 1)
                        if i == 0:
                            reached(dve, "s_ready", b + 1)
                        for half in range(2):
                            reached(dve, "scan_step", n3 + 1 + half)
                            mm = m0[:, r, 2 * half:2 * half + 2, :]
                            ins = dve.tensor_tensor(mm, mm, s_sb[:, 0:SEQ].unsqueeze(1).to_broadcast([P, 2, SEQ]), ALU.mult)
                            ins.then_inc(S["m0_step"], 1)
                        is_three = [BC0A, BC0B, BC1]
                        reached(dve, "scan_step", n3 + 3)
                        for bk in is_three:
                            dve.sem_inc(bank_free[bk], 1)
                    if 1 <= i < PAIRS + 1:
                        h = i - 1
                        pb = await_full(dve, table, ("y", h), b if not last else 0)
                        reached(dve, "g_ready", b * PAIRS + (h - 1))
                        for jj in range(2):
                            j = 2 * h + jj
                            ins = dve.scalar_tensor_tensor(y_sb[:, h % 2, jj * SEQ:jj * SEQ + SEQ], xsT_v[:, j, :],
                                                           dcol[:, j:j + 1], pb[:, jj * SEQ:jj * SEQ + SEQ],
                                                           ALU.mult, ALU.add)
                        ins.then_inc(S["y_ready"], 1)
                        reached(dve, "y_ready", b * PAIRS + h + 1)
                        dve.sem_inc(bank_free[YB], 1)
                    if 2 <= i < PAIRS + 2 and not last:
                        convolve(i - 2, table, ("xp", i - 2), b, b + 1)
                    if i == PAIRS + 2:
                        if not last:
                            convolve(PAIRS, table, ("xp", PAIRS), b, b + 1)
                        pb = await_full(dve, table, ("ssq", 0), b if not last else 0)
                        ins = dve.tensor_scalar(var_g[:], pb[:, 0:2], 1.0 / DIN, EPS, ALU.mult, ALU.add)
                        ins.then_inc(S["var_ready"], 1)
                        reached(dve, "var_ready", b + 1)
                        dve.sem_inc(bank_free[table[("ssq", 0)][0]], 1)
                        pb = await_full(dve, table, ("op", 0), b if not last else 0)
                        reached(dve, "rstd_ready", b + 1)
                        for c in range(2):
                            xc = xn_all[:, at(b, 2, 2), :][:, c, :]
                            ins = dve.scalar_tensor_tensor(xc, pb[:, c * HID:c * HID + HID], rstd_g[:, c:c + 1], xc,
                                                           ALU.mult, ALU.add)
                        ins.then_inc(S["x1_ready"], 1)
                        reached(dve, "x1_ready", b + 1)
                        dve.sem_inc(bank_free[OPB], 1)

            with dve.Fori(0, GROUPS) as g:
                reached(dve, "ssq_ready", g + 1)
                ins = dve.tensor_scalar(var_x1[:], ssq_x1[:], 1.0 / HID, EPS, ALU.mult, ALU.add)
                ins.then_inc(S["var1_ready"], 1)
                reached(dve, "rstd1_ready", g + 1)
                b5, f5 = fills(IN_GROUP, ("x1t", 0), g)
                dve.wait_ge(bank_full[b5], f5)
                for q in range(GT):
                    ins = dve.tensor_scalar(x1r[:, q, :], xn_all[:, bass.ds(g * GT, GT), :][:, q, :], rstd_x1[:, q:q + 1],
                                            None, ALU.mult)
                ins.then_inc(S["x1r_ready"], 1)
                for m in range(FT + MT):
                    n = g * (FT + MT) + m
                    pb = await_full(dve, IN_GROUP, ("up", m), g)
                    reached(dve, "sg_ready", n + 1)
                    reached(dve, "down_done", n - 1)
                    ins = dve.tensor_tensor(hid[:, m % 2, :], sg[:, m % 2, :], pb[:, :], ALU.mult)
                    is_free(ins, IN_GROUP, ("up", m))
                    if m < FT:
                        pc = await_full(dve, IN_GROUP, ("comb", m), g)
                        b_, f_ = fills(IN_GROUP, ("up", m), g)
                        dve.wait_ge(bank_free[b_], f_ + 1)
                        ins = dve.tensor_tensor(hid[:, m % 2, :], hid[:, m % 2, :], pc[:, :], ALU.mult)
                        ins.then_inc(S["hid_ready"], 1)
                        reached(dve, "hid_ready", n + 1)
                        dve.sem_inc(bank_free[4], 1)
                    else:
                        b_, f_ = fills(IN_GROUP, ("up", m), g)
                        dve.wait_ge(bank_free[b_], f_ + 1)
                        dve.sem_inc(S["hid_ready"], 1)
                dve.wait_ge(stored, (g + 1) * 16)
                for h in range(2):
                    pb = await_full(dve, IN_GROUP, ("acc", 1, h), g)
                    ins = dve.tensor_tensor(res[:, 2 * h:2 * h + 2, :],
                                            xn_all[:, bass.ds(g * GT, GT), :][:, 2 * h:2 * h + 2, :],
                                            pb[:, :].rearrange("p (q n) -> p q n", q=2), ALU.add)
                    is_free(ins, IN_GROUP, ("acc", 1, h))
                b_, f_ = fills(IN_GROUP, ("acc", 1, 1), g)
                dve.wait_ge(bank_free[b_], f_ + 1)
                dve.sem_inc(S["res_ready"], 1)

        @block.scalar
        def _(act):
            for n in ("xtok_ready", "sz_ready", "sq_ready", "tap_ready", "xs_ready", "s_ready", "sg_ready", "ssq_ready",
                      "x1t_ready", "gm_ready"):
                act.sem_inc(S[n], CREDIT)
            act.wait_ge(v_step, V_CENTRED)
            for t in range(TT):
                ins = act.activation(junk[:, t, :], xn_all[:, t, :], ACT.Square, accum_out=st[:, 2, t:t + 1])
                ins.then_inc(a_step, 1)
            act.wait_ge(loaded["small"], SMALL)
            for q in range(4):
                pb = await_full(act, IN_SETUP, ("xr", q))
                for k in range(KH):
                    ins = act.activation(xrT[:, k, 256 * q:256 * q + 256], pb[:, 256 * k:256 * k + 256], ACT.Copy,
                                         scale=ln1_sb[:, k:k + 1])
                is_free(ins, IN_SETUP, ("xr", q))
            act.wait_ge(v_step, V_V)
            ins = act.activation(wk[:, 6], wk[:, 0], ACT.Abs)
            ins.then_inc(a_step, 1)
            act.activation(arow[:], arow[:], ACT.Exp).then_inc(a_step, 1)
            act.wait_ge(a_step, TT + 2)
            act.activation(wk[:, 2], wk[:, 6], ACT.Exp, scale=-1.0).then_inc(a_step, 1)
            act.mul(arow[:], arow[:], -1.0).then_inc(a_step, 1)
            act.wait_ge(a_step, TT + 4)
            act.activation(wk[:, 3], wk[:, 2], ACT.Ln, bias=1.0).then_inc(a_step, 1)
            assert TT + 5 == A_LN
            for q in range(4):
                pb = await_full(act, IN_SETUP, ("xn", q))
                ins = act.activation(xnT[:, :, 256 * q:256 * q + 256], pb[:, :].rearrange("p (k t) -> p k t", k=KH), ACT.Copy)
                is_free(ins, IN_SETUP, ("xn", q))
            pb = await_full(act, IN_SETUP, ("gate", 0))
            ins = act.activation(prob, pb[:, 0:TT * NE].rearrange("p (t e) -> p t e", t=TT), ACT.Exp, scale=-1.0)
            ins.then_inc(a_step, 1)
            act.wait_ge(a_step, A_GATE)
            act.sem_inc(bank_free[7], 1)
            act.wait_ge(v_step, V_LOGA)
            act.activation(wk[:, 7], wk[:, 4], ACT.Exp).then_inc(a_step, 1)

            def first_tap(unit, table, key, it, it_units):
                pb = await_full(act, table, key, it)
                reached(act, "xs_ready", it_units * UNITS + max(unit - 1, 0))
                tiles = 2 if unit < PAIRS else 1
                for jj in range(tiles):
                    ins = act.activation(acc[:, unit % 2, jj, :], pb[:, jj * SEQ:jj * SEQ + SEQ], ACT.Identity,
                                         bias=cb[:, 2 * unit + jj:2 * unit + jj + 1],
                                         scale=cw[:, 2 * unit + jj, TAPS - 1:TAPS])
                ins.then_inc(S["tap_ready"], 1)

            def silu_conv(unit, it_units):
                if unit < PAIRS:
                    reached(act, "conv_step", it_units * CONV + unit * 6 + 6)
                    ins = act.activation(xsT_v[:, 2 * unit:2 * unit + 2, :], acc[:, unit % 2, :, :], ACT.Silu)
                else:
                    reached(act, "conv_step", it_units * CONV + CONV)
                    act.activation(bT[:], acc[0:NST, unit % 2, 0, :], ACT.Silu)
                    ins = act.activation(cT[:], acc[NST:P, unit % 2, 0, :], ACT.Silu)
                ins.then_inc(S["xs_ready"], 1)

            act.wait_ge(v_step, V_SPLIT)
            for unit in range(UNITS):
                first_tap(unit, IN_FIRST, ("xp", unit), 0, 0)
                if unit:
                    silu_conv(unit - 1, 0)
            silu_conv(PAIRS, 0)

            for b, table, last in sequences(act):
                it = b if not last else 0
                for i in range(PAIRS + 3):
                    if i == 0:
                        pb = await_full(act, table, ("s", 0), it)
                        reached(act, "m0_step", b * PAIRS * 2)
                        reached(act, "m1_ready", b * PAIRS)
                        ins = act.activation(s_sb[:], pb[:, 0:SEQ + P], ACT.Copy)
                        ins.then_inc(S["s_ready"], 1)
                        reached(act, "s_ready", b + 1)
                        act.sem_inc(bank_free[table[("s", 0)][0]], 1)
                    if i < PAIRS:
                        pb = await_full(act, table, ("xtr", i), it)
                        reached(act, "xdt_ready", b * PAIRS + i - 1)
                        ins = act.activation(xtok[:, i % 2, :, :].rearrange("p c n -> p (c n)"), pb[:, :], ACT.Copy)
                        ins.then_inc(S["xtok_ready"], 1)
                        reached(act, "xtok_ready", b * PAIRS + i + 1)
                        act.sem_inc(bank_free[table[("xtr", i)][0]], 1)
                        pb = await_full(act, table, ("z", i), it)
                        reached(act, "g_ready", b * PAIRS + i - 1)
                        ins = act.activation(sz[:, i % 2, :], pb[:, :], ACT.Silu)
                        ins.then_inc(S["sz_ready"], 1)
                        reached(act, "sz_ready", b * PAIRS + i + 1)
                        act.sem_inc(bank_free[table[("z", i)][0]], 1)
                    if 2 <= i < PAIRS + 2 and not last:
                        first_tap(i - 2, table, ("xp", i - 2), it, b + 1)
                    if 2 <= i < PAIRS + 2:
                        h = i - 2
                        reached(act, "g_ready", b * PAIRS + h + 1)
                        if h == 0:
                            bs, fs = fills(IN_SEQ, ("ssq", 0), b)
                            act.wait_ge(bank_full[bs], fs + 1 - IN_SEQ[("ssq", 0)][2])
                            dst = gsq[:, :]
                        else:
                            reached(act, "gsq_ready", b * (PAIRS - 1) + max(h - 2, 0))
                            dst = sq[:, h % 2, :]
                        act.activation(dst, gT[:, h % 4, :], ACT.Square).then_inc(S["sq_ready"], 1)
                    if 3 <= i < PAIRS + 3 and not last:
                        reached(act, "y_ready", b * PAIRS + (i - 3) + 1)
                        silu_conv(i - 3, b + 1)
                    if i == PAIRS + 2 and not last:
                        first_tap(PAIRS, table, ("xp", PAIRS), it, b + 1)
                        silu_conv(PAIRS, b + 1)

            with act.Fori(0, GROUPS) as g:
                reached(act, "x1_ready", BATCH)
                reached(act, "var1_ready", g)
                reached(act, "hid_ready", g * (FT + MT))
                for q in range(GT):
                    ins = act.activation(sg[:, q // 2, (q % 2) * HID:(q % 2) * HID + HID], xn_all[:, bass.ds(g * GT, GT), :][:, q, :], ACT.Square,
                                         accum_out=ssq_x1[:, q:q + 1])
                ins.then_inc(S["ssq_ready"], 1)
                reached(act, "ssq_ready", g + 1)
                for m in range(FT + MT):
                    n = g * (FT + MT) + m
                    pb = await_full(act, IN_GROUP, ("gate", m), g)
                    reached(act, "hid_ready", n - 1)
                    ins = act.activation(sg[:, m % 2, :], pb[:, :], ACT.Silu)
                    ins.then_inc(S["sg_ready"], 1)
                    reached(act, "sg_ready", n + 1)
                    act.sem_inc(bank_free[m % 2], 1)
                    if m in (2, 3):
                        k = m - 2
                        pb = await_full(act, IN_GROUP, ("x1t", k), g)
                        reached(act, "hid_ready", g * (FT + MT))
                        ins = act.activation(x1T[:, k, :], pb[:, :], ACT.Copy, scale=ln2_sb[:, k:k + 1])
                        ins.then_inc(S["x1t_ready"], 1)
                        reached(act, "x1t_ready", g * KH + k + 1)
                        act.sem_inc(bank_free[5], 1)
                    if m == FT:
                        reached(act, "prod_ready", g)
                        for h in range(2):
                            pb = await_full(act, IN_GROUP, ("acc", 0, h), g)
                            ins = act.activation(gm[:, 2 * h:2 * h + 2, :], pb[:, :].rearrange("p (q n) -> p q n", q=2),
                                                 ACT.Silu)
                            is_free(ins, IN_GROUP, ("acc", 0, h))
                        b_, f_ = fills(IN_GROUP, ("acc", 0, 1), g)
                        act.wait_ge(bank_free[b_], f_ + 1)
                        act.sem_inc(S["gm_ready"], 1)

        @block.gpsimd
        def _(pool):
            for n in ("xdt_ready", "m1_ready", "g_ready", "gsq_ready", "rstd_ready", "rstd1_ready", "prod_ready",
                      "sum_ready"):
                pool.sem_inc(S[n], CREDIT)
            pool.wait_ge(v_step, V_VAR)
            pool.tensor_tensor(st[:, 4, :], st[:, 3, :], power[:], ALU.pow).then_inc(p_step, 1)
            pool.wait_ge(v_step, V_VARN)
            pool.tensor_tensor(st[:, 5, :], st[:, 5, :], power[:], ALU.pow).then_inc(p_step, 1)
            pool.wait_ge(v_step, V_SPLIT)
            for b, table, last in sequences(pool):
                it = b if not last else 0
                for i in range(PAIRS + 3):
                    if i < PAIRS:
                        r = i % 2
                        reached(pool, "xtok_ready", b * PAIRS + i + 1)
                        b6, f6 = fills(table, ("y", i), it)
                        pool.wait_ge(bank_full[b6], f6 - 1)
                        for c in range(2):
                            dt_c = dt_tok[:, at(b, 2, 2), 4 * i:4 * i + 4][:, c, :]
                            ins = pool.tensor_tensor(xdt[:, r, c, :].rearrange("p (h d) -> p h d", h=4),
                                                     xtok[:, r, c, :].rearrange("p (h d) -> p h d", h=4),
                                                     dt_c.unsqueeze(2).to_broadcast([P, 4, HD]), ALU.mult)
                        ins.then_inc(S["xdt_ready"], 1)
                        reached(pool, "scan_step", (b * PAIRS + i) * 3 + 3)
                        if i == 0:
                            reached(pool, "s_ready", b + 1)
                        ins = pool.tensor_tensor(m1[:, r, :, :], m1[:, r, :, :],
                                                 s_sb[:, SEQ:SEQ + P].unsqueeze(1).to_broadcast([P, 4, P]), ALU.mult)
                        ins.then_inc(S["m1_ready"], 1)
                    if 1 <= i < PAIRS + 1:
                        h = i - 1
                        reached(pool, "y_ready", b * PAIRS + h + 1)
                        reached(pool, "sz_ready", b * PAIRS + h + 1)
                        reached(pool, "op_done", b * PAIRS + h - 3)
                        reached(pool, "sq_ready", b * PAIRS + h - 3)
                        ins = pool.tensor_tensor(gT[:, h % 4, :], y_sb[:, h % 2, :], sz[:, h % 2, :], ALU.mult)
                        ins.then_inc(S["g_ready"], 1)
                    if 3 <= i < PAIRS + 2:
                        h = i - 2
                        reached(pool, "sq_ready", b * PAIRS + h + 1)
                        if h > 1:
                            reached(pool, "gsq_ready", b * (PAIRS - 1) + h - 1)
                        pool.tensor_tensor(gsq[:], gsq[:], sq[:, h % 2, :], ALU.add).then_inc(S["gsq_ready"], 1)
                    if i == PAIRS + 2:
                        reached(pool, "var_ready", b + 1)
                        pool.tensor_tensor(rstd_g[:], var_g[:], power[:, 0:2], ALU.pow).then_inc(S["rstd_ready"], 1)
            with pool.Fori(0, GROUPS) as g:
                reached(pool, "var1_ready", g + 1)
                pool.tensor_tensor(rstd_x1[:], var_x1[:], power[:, 0:GT], ALU.pow).then_inc(S["rstd1_ready"], 1)
                reached(pool, "res_ready", g + 1)
                reached(pool, "gm_ready", g + 1)
                pool.tensor_tensor(res, res, gm, ALU.mult).then_inc(S["prod_ready"], 1)
                reached(pool, "prod_ready", g + 1)
                pool.wait_ge(loaded["xf"], g * 16 + 16)
                pool.tensor_tensor(res, res, xf, ALU.add).then_inc(S["sum_ready"], 1)

        @block.tensor
        def _(pe):
            for n in ("op_done", "down_done"):
                pe.sem_inc(S[n], CREDIT)
            pe.wait_ge(loaded["small"], SMALL)

            def transposes(kind, src, q):
                pb = await_free(pe, IN_SETUP, (kind, q))
                for k in range(KH):
                    for c in range(2):
                        ins = pe.transpose(pb[:, 256 * k + P * c:256 * k + P * c + P], src[:, 2 * q + c, k * P:k * P + P],
                                           ident[:])
                is_full(ins, IN_SETUP, (kind, q))

            pe.wait_ge(v_step, V_XR)
            for q in range(4):
                transposes("xr", xr_all, q)
            pb = await_free(pe, IN_SETUP, ("dt", 0))
            for t in range(TT):
                if t % 2 == 0:
                    pe.wait_ge(bank_free[t // 2], 1)
                for k in range(KH):
                    ins = pe.matmul(pb[:, t * HEADS:t * HEADS + HEADS], xrT[:, k, t * P:t * P + P], wdt_sb[:, k, :],
                                    start=(k == 0), stop=(k == KH - 1))
            is_full(ins, IN_SETUP, ("dt", 0))
            for q in range(4):
                transposes("xn", xn_all, q)
            pb = await_free(pe, IN_SETUP, ("gate", 0))
            for t in range(TT):
                if t % 2 == 0:
                    pe.wait_ge(bank_free[4 + t // 2], IN_SETUP[("xn", t // 2)][3] + 1)
                for k in range(KH):
                    ins = pe.matmul(pb[:, t * NE:t * NE + NE], xnT[:, k, t * P:t * P + P], wgate_sb[:, k, :],
                                    start=(k == 0), stop=(k == KH - 1))
            is_full(ins, IN_SETUP, ("gate", 0))
            pe.wait_ge(a_step, A_DECAY)
            for n in range(2):
                pb = await_free(pe, IN_SETUP, ("decay", n))
                for t in range(4):
                    ins = pe.transpose(pb[0:HEADS, t * P:t * P + P], wk[:, 7, 4 * n + t, :], ident[:])
                is_full(ins, IN_SETUP, ("decay", n))
            pe.wait_ge(v_step, V_COMB)
            for n in range(2):
                pb = await_free(pe, IN_SETUP, ("comb", n))
                for t in range(4):
                    ins = pe.transpose(pb[0:NE + 1, t * P:t * P + P], combx[:, 4 * n + t, :], ident[:])
                is_full(ins, IN_SETUP, ("comb", n))

            def project_x(unit, table, key, it, tokens):
                pb = await_free(pe, table, key, it)
                tiles = 2 if unit < PAIRS else 1
                for jj in range(tiles):
                    for k in range(KH):
                        ins = pe.matmul(pb[:, jj * SEQ:jj * SEQ + SEQ], wx_v[:, k, (2 * unit + jj) * P:(2 * unit + jj + 1) * P],
                                        xrT[:, k, tokens], start=(k == 0), stop=(k == KH - 1))
                is_full(ins, table, key)

            pe.wait_ge(loaded["wx"], 16)
            for unit in range(UNITS):
                project_x(unit, IN_FIRST, ("xp", unit), 0, slice(0, SEQ))
            pe.wait_ge(loaded["wz"], 16)
            pe.wait_ge(v_step, V_WO)

            for b, table, last in sequences(pe):
                it = b if not last else 0
                toks = at(b, SEQ, SEQ)
                nxt = None if last else bass.ds(b * SEQ + SEQ, SEQ)
                for i in range(PAIRS + 3):
                    if i == 0:
                        reached(pe, "xs_ready", b * UNITS + UNITS)
                        pb = await_free(pe, table, ("s", 0), it)
                        pe.matmul(pb[:, 0:SEQ], bT[:, 0:P], cT[:, :], start=True, stop=True)
                        ins = pe.matmul(pb[:, SEQ:SEQ + P], bT[:, P:SEQ], cT[:, P:SEQ], start=True, stop=True)
                        is_full(ins, table, ("s", 0))
                    if i < PAIRS:
                        pb = await_free(pe, table, ("xtr", i), it)
                        for c in range(2):
                            for jj in range(2):
                                ins = pe.transpose(pb[:, c * 256 + jj * P:c * 256 + jj * P + P],
                                                   xsT_v[:, 2 * i + jj, c * P:c * P + P], ident[:])
                        is_full(ins, table, ("xtr", i))
                        for n, name in enumerate(("bc0a", "bc0b")):
                            pb = await_free(pe, table, (name, i), it)
                            for hh in range(2):
                                h = 4 * i + 2 * n + hh
                                ins = pe.matmul(pb[:, hh * SEQ:hh * SEQ + SEQ], sel_head[:, h:h + 1].to_broadcast([SPLIT * HEADS, P]),
                                                decay0[:, toks], start=True, stop=True)
                            is_full(ins, table, (name, i))
                        pb = await_free(pe, table, ("bc1", i), it)
                        for hh in range(4):
                            h = 4 * i + hh
                            ins = pe.matmul(pb[:, hh * P:hh * P + P], sel_head[:, h:h + 1].to_broadcast([SPLIT * HEADS, P]),
                                            decay1[:, at(b, P, P)], start=True, stop=True)
                        is_full(ins, table, ("bc1", i))
                        pb = await_free(pe, table, ("z", i), it)
                        for jj in range(2):
                            for k in range(KH):
                                ins = pe.matmul(pb[:, jj * SEQ:jj * SEQ + SEQ], wz_v[:, k, (2 * i + jj) * P:(2 * i + jj + 1) * P],
                                                xrT[:, k, toks], start=(k == 0), stop=(k == KH - 1))
                        is_full(ins, table, ("z", i))
                    if 1 <= i < PAIRS + 1:
                        h, r = i - 1, (i - 1) % 2
                        pb = await_free(pe, table, ("y", h), it)
                        reached(pe, "xdt_ready", b * PAIRS + h + 1)
                        reached(pe, "m0_step", (b * PAIRS + h) * 2 + 2)
                        reached(pe, "m1_ready", b * PAIRS + h + 1)
                        for jj in range(2):
                            for hh in range(2):
                                n = 2 * jj + hh
                                rows = slice(HD * hh, HD * hh + HD)
                                pe.matmul(pb[rows, jj * SEQ:jj * SEQ + SEQ], xdt[:, r, 0, n * HD:n * HD + HD], m0[:, r, n, :],
                                          start=True, stop=False)
                                ins = pe.matmul(pb[rows, jj * SEQ + P:jj * SEQ + SEQ], xdt[:, r, 1, n * HD:n * HD + HD],
                                                m1[:, r, n, :], start=False, stop=True)
                        is_full(ins, table, ("y", h))
                    if 2 <= i < PAIRS + 2 and not last:
                        project_x(i - 2, table, ("xp", i - 2), it, nxt)
                    if i == PAIRS + 2 and not last:
                        project_x(PAIRS, table, ("xp", PAIRS), it, nxt)
                    if 3 <= i < PAIRS + 3:
                        h = i - 3
                        if h == 0:
                            po = await_free(pe, table, ("op", 0), it)
                        reached(pe, "g_ready", b * PAIRS + h + 1)
                        for jj in range(2):
                            for c in range(2):
                                ins = pe.matmul(po[:, c * HID:c * HID + HID], gT[:, h % 4, jj * SEQ + c * P:jj * SEQ + c * P + P],
                                                wo_sb[:, 2 * h + jj, :], start=(h == 0 and jj == 0 and c == 0),
                                                stop=(h == PAIRS - 1 and jj == 1), skip_group_check=True)
                        ins.then_inc(S["op_done"], 1)
                    if i == PAIRS + 2:
                        reached(pe, "op_done", b * PAIRS + PAIRS)
                        pe.sem_inc(bank_full[OPB], 1)
                        pb = await_free(pe, table, ("ssq", 0), it)
                        reached(pe, "gsq_ready", b * (PAIRS - 1) + PAIRS - 1)
                        for c in range(2):
                            for jj in range(2):
                                ins = pe.matmul(pb[:, c:c + 1], gsq[:, jj * SEQ + c * P:jj * SEQ + c * P + P], ones[:],
                                                start=(jj == 0), stop=(jj == 1))
                        is_full(ins, table, ("ssq", 0))

            pe.wait_ge(loaded["wgu"], 16)
            with pe.Fori(0, GROUPS) as g:
                toks = bass.ds(g * GT * P, GT * P)

                def down(m):
                    a = 0 if m < FT else 1
                    if m in (0, FT):
                        for h in range(2):
                            await_free(pe, IN_GROUP, ("acc", a, h), g)
                    if m == 0:
                        pe.wait_ge(loaded["wd"], 16)
                    if m == FT:
                        pe.wait_ge(loaded["wmo"], 16)
                    n = g * (FT + MT) + m
                    reached(pe, "hid_ready", n + 1)
                    w = wd_v[:, m, :] if m < FT else wmo_sb[:, m - FT, :]
                    for q in range(GT):
                        ins = pe.matmul(bank[6 + q // 2][:, (q % 2) * HID:(q % 2) * HID + HID], hid[:, m % 2, q * P:q * P + P],
                                        w, start=(m in (0, FT) and q % 2 == 0), stop=(m in (FT - 1, FT + MT - 1)),
                                        skip_group_check=True)
                    ins.then_inc(S["down_done"], 1)
                    if m in (FT - 1, FT + MT - 1):
                        reached(pe, "down_done", n + 1)
                        for h in range(2):
                            pe.sem_inc(bank_full[6 + h], 1)

                for m in range(FT + MT):
                    if m == FT:
                        pe.wait_ge(loaded["wmi"], 16)
                        reached(pe, "x1t_ready", g * KH + KH)
                    for n, name in enumerate(("gate", "up")):
                        pb = await_free(pe, IN_GROUP, (name, m), g)
                        for k in range(KH):
                            if m < FT:
                                ins = pe.matmul(pb[:, :], wgu_sb[:, k, n, m * P:m * P + P], xnT[:, k, toks],
                                                start=(k == 0), stop=(k == KH - 1))
                            else:
                                ins = pe.matmul(pb[:, :], wmi_v[:, k, n, (m - FT) * P:(m - FT) * P + P], x1T[:, k, :],
                                                start=(k == 0), stop=(k == KH - 1))
                        is_full(ins, IN_GROUP, (name, m))
                    if m < FT:
                        pb = await_free(pe, IN_GROUP, ("comb", m), g)
                        ins = pe.matmul(pb[:, :], sel_exp[:, m * P:m * P + P], comb_split[:, toks], start=True, stop=True)
                        is_full(ins, IN_GROUP, ("comb", m))
                    if m in (2, 3):
                        k = m - 2
                        reached(pe, "x1r_ready", g + 1)
                        pb = await_free(pe, IN_GROUP, ("x1t", k), g)
                        for q in range(GT):
                            ins = pe.transpose(pb[:, q * P:q * P + P], x1r[:, q, k * P:k * P + P], ident[:])
                        is_full(ins, IN_GROUP, ("x1t", k))
                    if m > 0:
                        down(m - 1)
                down(FT + MT - 1)


A_SQUARES, A_LN, A_GATE, A_DECAY = TT, TT + 5, TT + 6, TT + 7
V_CENTRED, V_VAR, V_VARN, V_XN, V_XR, V_V = 4, 6, 9, 10, 11, 12
V_LOGA = V_V + 9
V_COMB = V_LOGA + 2 + 2 * TT + 11
V_DECAY = V_COMB + 8
V_SPLIT = V_DECAY + 5
V_WO = V_SPLIT + 1


def kernel(**inputs):
    import numpy as np
    import concourse.bacc as bacc
    from concourse.bass_utils import run_bass_kernel_spmd
    import ml_dtypes

    a = {k: np.asarray(v) for k, v in inputs.items()}
    f32, bf16 = np.float32, ml_dtypes.bfloat16

    def rows(w, k):
        return w.reshape(k, P, -1).transpose(1, 0, 2)

    proj = a["L0_attn_in_proj_w"]
    gate_rows = np.concatenate([a["L0_ffn_exp_wg"].reshape(NE * FF, HID), a["L0_ffn_shared_wg"]])
    up_rows = np.concatenate([a["L0_ffn_exp_wu"].reshape(NE * FF, HID), a["L0_ffn_shared_wu"]])
    down_rows = np.concatenate([a["L0_ffn_exp_wd"].transpose(0, 2, 1).reshape(NE * FF, HID), a["L0_ffn_shared_wd"].T])
    pad = FFP - gate_rows.shape[0]
    gate_rows, up_rows, down_rows = (np.pad(w, ((0, pad), (0, 0))) for w in (gate_rows, up_rows, down_rows))
    owner = np.minimum(np.arange(FFP) // FF, NE)
    sel_exp = np.zeros((SPLIT * 32, FFP), bf16)
    sel_head = np.zeros((SPLIT * HEADS, HEADS), bf16)
    for s in range(SPLIT):
        sel_exp[32 * s + owner, np.arange(FFP)] = 1
        sel_head[HEADS * s + np.arange(HEADS), np.arange(HEADS)] = 1
    eye = np.zeros((P, 2, 512), f32)
    for h in range(2):
        eye[np.arange(P), 0, h * SEQ + np.arange(P)] = 1
    for h in range(4):
        eye[np.arange(P), 1, h * P + np.arange(P)] = 1
    arrays = {
        "x": a["L0_attn_x"].reshape(TT, P, HID).transpose(1, 0, 2),
        "wx": rows(proj[DIN:2 * DIN + 2 * NST].T, KH).reshape(P, -1),
        "wz": rows(proj[:DIN].T, KH).reshape(P, -1),
        "wdt": rows(proj[2 * DIN + 2 * NST:].T, KH),
        "wo": rows(a["L0_attn_out_proj_w"].T, CT),
        "wgu": np.stack([rows(gate_rows.T, KH), rows(up_rows.T, KH)], 2),
        "wd": rows(down_rows, FT).reshape(P, -1),
        "wmi": rows(a["L0_attn_mlp_in_w"].T, KH).reshape(P, -1),
        "wmo": rows(a["L0_attn_mlp_out_w"].T, MT),
        "wgate": rows(a["L0_ffn_gate_w"].T, KH),
        "conv_w": a["L0_attn_conv_w"].reshape(CT + 1, P, TAPS).transpose(1, 0, 2),
        "conv_b": a["L0_attn_conv_b"].reshape(CT + 1, P).T,
        "a_log": np.broadcast_to(a["L0_attn_A_log"], (P, HEADS)),
        "dt_bias": np.broadcast_to(a["L0_attn_dt_bias"], (P, HEADS)),
        "d_col": np.repeat(a["L0_attn_D_param"], HD).reshape(CT, P).T,
        "mnorm": a["L0_attn_mnorm_w"].reshape(CT, P).T,
        "ln1": a["L0_attn_ln1_w"].reshape(KH, P).T,
        "ln2": a["L0_attn_ln2_w"].reshape(KH, P).T,
        "ident": np.eye(P, dtype=f32),
        "eye": eye,
        "sel_head": sel_head,
        "sel_exp": sel_exp,
        "iota": np.broadcast_to(np.arange(NE, dtype=f32), (P, TT, NE)),
    }
    nc = bacc.Bacc("TRN2", target_bir_lowering=False, num_devices=1)
    args, feed = [], {}
    for name, arr in arrays.items():
        arr = np.ascontiguousarray(arr)
        feed[f"in_{name}_dram"] = arr
        args.append(nc.dram_tensor(f"in_{name}_dram", arr.shape, mybir.dt.from_np(arr.dtype), kind="ExternalInput").ap())
    out = nc.dram_tensor("out_0_dram", (P, TT, HID), F32, kind="ExternalOutput").ap()
    build(nc, *args, out)
    r = run_bass_kernel_spmd(nc, [feed], core_ids=[0])
    got = r.results[0]["out_0_dram"]
    return np.ascontiguousarray(got.transpose(1, 0, 2).reshape(BATCH, SEQ, HID))
```

```python
from contextlib import ExitStack

import concourse.bass as bass
from concourse import mybir
from concourse.alu_op_type import AluOpType as ALU

ACT = mybir.ActivationFunctionType
F32 = mybir.dt.float32
F32R = mybir.dt.float32r
BF16 = mybir.dt.bfloat16
U32 = mybir.dt.uint32
AX_X = mybir.AxisListType.X

P = 128
BATCH, SEQ, HID = 4, 256, 256
TOK = BATCH * SEQ
TT = TOK // P
KH = HID // P
HEADS, HD, NST, TAPS = 32, 64, 64, 4
DIN = HEADS * HD
XCH = DIN + 2 * NST
CT = DIN // P
PAIRS = CT // 2
UNITS = PAIRS + 1
INTER = 1024
NE, FF, SFF = 8, 176, 352
FT = -(-(NE * FF + SFF) // P)
MT = INTER // P
FFP = FT * P
ROUTED_SCALE = 2.5
EPS = 1e-5
SPLIT = 3
NR = NE + 1
HALF = TOK // 2
CREDIT = 4
CONV = PAIRS * 4 + 2

RING = (0, 1, 2)
BC0A, BC0B, BC1, YB, OPB = 3, 4, 5, 6, 7
GATE, UP, COMB, ACC = 0, 2, 3, 4

WX_CHUNKS = [(0, 512), (512, 512), (1024, 512), (1536, XCH - 1536)]
NCH = 4
SLOT = KH * (XCH - 1536)

SETUP = [(("xr", 0), 6), (("xr", 1), 3), (("xr", 2), 4), (("xr", 3), 5), (("dt", 0), 6), (("dt", 1), 3),
         (("dtt", 0), 7)]


ROUTE_STEP, COMB_STEP = 6, 8
XN_AT = {3: (0, 1), 5: (2, 3)}
ORDER = (0, 1, 2, 3, PAIRS, 4, 5, 6, 7)


def place(unit):
    return ORDER.index(unit)


def units_at(i, prev, last):
    if i < 2:
        return [PAIRS - 2 + i] if prev else []
    if last or i >= PAIRS:
        return []
    return ([PAIRS] if i == PAIRS - 2 else []) + [i - 2]


def convolved_at(i, prev, last):
    if i == 0:
        return [PAIRS - 3] if prev else []
    return units_at(i - 1, prev, last)


def in_step(i, lag, prev):
    h = i - lag
    return h if (0 <= h < PAIRS or (h < 0 and prev)) else None


def first_projection():
    return [(("xp", u), RING[n % 3]) for n, u in enumerate(ORDER)]


def sequence_items(prev, last):
    keys, ys = [], []
    for i in range(PAIRS + 3 if last else PAIRS):
        if i < PAIRS:
            keys += [("xtr", i), ("z", i)]
        if i == 0:
            keys.append(("s", 0))
        if i == 2 and prev:
            keys.append(("ssq", -1))
        keys += [("xp", u) for u in units_at(i, prev, last)]
        if last:
            keys += [("xn", q) for q in XN_AT.get(i, ())]
        if last and i == ROUTE_STEP:
            keys.append(("gate", 0))
        if last and i == COMB_STEP:
            keys += [("comb", 0), ("comb", 1)]
        if i == PAIRS + 2:
            keys.append(("ssq", 0))
        h = in_step(i, 1, prev)
        if h is not None:
            ys.append((("y", h), YB))
    items = [(k, RING[n % 3]) for n, k in enumerate(keys)]
    for i in range(PAIRS):
        items += [(("bc0a", i), BC0A), (("bc0b", i), BC0B), (("bc1", i), BC1)]
    return items + ys + ([(("op", -1), OPB)] if prev else []) + ([(("op", 0), OPB)] if last else [])


MOE_ITEMS = [(("gate", u), GATE + u) for u in range(2)] + [(("up", u), UP) for u in range(2)] + [
    (("comb", u), COMB) for u in range(2)]
MLP_ITEMS = MOE_ITEMS[:4]


class Banks:

    def __init__(self):
        self.base = [0] * 8

    def phase(self, items, times=1, carried=None):
        base, seen, table = list(self.base), [0] * 8, {}
        for key, bank in items:
            table[key] = (bank, base[bank], seen[bank])
            seen[bank] += 1
        self.base = [b + times * n for b, n in zip(self.base, seen)]
        if carried is not None:
            key, bank = carried
            table[key] = (bank, base[bank], -1)
        return {k: (bank, b0, seen[bank], n) for k, (bank, b0, n) in table.items()}


BANKS = Banks()
IN_SETUP = BANKS.phase(SETUP)
IN_FIRST = BANKS.phase(first_projection())
IN_BEGIN = BANKS.phase(sequence_items(False, False))
CARRIED = (("carried", PAIRS - 3), RING[2])
assert all([k for k, b in sequence_items(prev, False) if b == RING[2]][-1] == ("xp", PAIRS - 3) for prev in (False, True))
IN_SEQ = BANKS.phase(sequence_items(True, False), BATCH - 2, CARRIED)
IN_LAST = BANKS.phase(sequence_items(True, True), 1, CARRIED)
IN_MOE = BANKS.phase(MOE_ITEMS, FT)
IN_MOE_ACC = BANKS.phase([(("acc", n), ACC + n) for n in range(4)])
IN_X1T = BANKS.phase([(("x1t", n), n) for n in range(4)])
IN_MLP = BANKS.phase(MLP_ITEMS, MT)
IN_MLP_ACC = BANKS.phase([(("acc", n), ACC + n) for n in range(4)])


def fills(table, key, it=0):
    bank, base, per, n = table[key]
    return bank, it * per + (base + n)


LN_GROUPS = ((0, 2), (2, TT))
P_RSTD = 8
V_CENTRED = [1 + 2 + 2, 1 + 4 + 4 + TT]
V_XR = [V_CENTRED[0] + 2, V_CENTRED[1] + TT - 2]
V_WDT = V_XR[1] + (TT - 2) + 2
V_NEG = V_WDT + BATCH + 1
V_U = V_NEG + 1
V_DT = V_U + 7
V_RESET = V_DT + 1
V_PART = V_RESET + 1
V_DECAY = V_PART + BATCH + 1 + 2 * BATCH + 2
A_SQUARES = [2, TT]
A_NEGA = TT + 2
A_EXP = A_NEGA + 1
A_LN = A_EXP + 1
A_DEC = A_LN + 1
A_HI = A_DEC + 1
A_MID = A_HI + 1

PACK_A = (("ident", P), ("ln1", KH), ("conv_w", (CT + 1) * TAPS), ("conv_b", CT + 1))
PACK_B = (("wdt", KH * P), ("wgate", KH * NE), ("iota", TT * NE), ("d_col", CT), ("mnorm", CT), ("ln2", KH),
          ("dt_bias", 1), ("a_log", 1))
R_COMB = 2 + 2 * TT + 4 + 7
R_PART = R_COMB + 1
R_SPLIT = R_PART + 1
RA_HI, RA_MID = 1, 3

def build(nc, x, wx, wz, wo, wgu, wd, pack_a_in, pack_b_in, eye_in, sel_head_in, sel_exp_in, out):
    with ExitStack() as ctx:
        def sb(name, shape, dt=F32):
            return ctx.enter_context(nc.sbuf_tensor(name, shape, dt))

        def sem(name):
            return ctx.enter_context(nc.semaphore(name))

        wx_r = sb("wx_r", [P, 2, KH * XCH], F32R)
        wz_r = sb("wz_r", [P, 2, KH * DIN], F32R)
        wo_r = sb("wo_r", [P, 2, CT * HID], F32R)
        xrT = sb("xrT", [P, 2, KH, TOK], F32R)
        g_r = sb("g_r", [P, 2, 2, 512], F32R)
        wdt_r = sb("wdt_r", [P, 2, KH, P], F32R)
        wgate_r = sb("wgate_r", [P, 2, KH, NE], F32R)
        wx_v = wx_r[:, :, :].rearrange("p s (k n) -> p s k n", k=KH)
        wz_v = wz_r[:, :, :].rearrange("p s (k n) -> p s k n", k=KH)
        wo_v = wo_r[:, :, :].rearrange("p s (j n) -> p s j n", j=CT)
        flat_x = wx_r[:, :, :].rearrange("p s n -> p (s n)")
        flat_z = wz_r[:, :, :].rearrange("p s n -> p (s n)")
        xnT = flat_x[:, 0:2 * KH * TOK].rearrange("p (s k t) -> p s k t", s=2, k=KH)
        x1T = flat_x[:, 2 * KH * TOK:4 * KH * TOK].rearrange("p (s k t) -> p s k t", s=2, k=KH)
        hid = flat_z[:, 0:4096].rearrange("p (r s t) -> p r s t", r=2, s=2)
        wgu_r = flat_z[:, 4096:6144].rearrange("p (r s k g n) -> p r s k g n", r=2, s=2, k=KH, g=2)
        wd_r = flat_z[:, 6144:7168].rearrange("p (r s n) -> p r s n", r=2, s=2)
        pack_a = sb("pack_a", [P, sum(n for _, n in PACK_A)])
        pack_b = sb("pack_b", [P, sum(n for _, n in PACK_B)])
        small = {}
        for whole, parts in ((pack_a, PACK_A), (pack_b, PACK_B)):
            col = 0
            for name, n in parts:
                small[name] = whole[:, col:col + n]
                col += n
        ident, ln1_sb, cb = small["ident"], small["ln1"], small["conv_b"]
        cw = small["conv_w"].rearrange("p (j s) -> p j s", s=TAPS)
        wdt_sb = small["wdt"].rearrange("p (k n) -> p k n", k=KH)
        wgate_sb = small["wgate"].rearrange("p (k n) -> p k n", k=KH)
        iota = small["iota"].rearrange("p (t e) -> p t e", t=TT)
        dcol, mn, ln2_sb = small["d_col"], small["mnorm"], small["ln2"]
        dt_bias, neg_a = small["dt_bias"], small["a_log"]
        eye = sb("eye", [P, 2, 512])
        sel_head = sb("sel_head", [SPLIT * HEADS, HEADS], BF16)
        ones = sb("ones", [P, 1])
        power = sb("power", [P, TT])
        st = sb("st", [P, 6, TT])
        xn_all = sb("xn_all", [P, TT, HID])
        dt_tok = sb("dt_tok", [P, 2, BATCH * HEADS])
        decay0 = sb("decay0", [SPLIT * HEADS, TOK], BF16)
        decay1 = sb("decay1", [SPLIT * HEADS, BATCH * P], BF16)
        comb_split = sb("comb_split", [SPLIT * 32, TOK], BF16)
        rk = sb("rk", [P, 672])
        xsT = sb("xsT", [P, CT * SEQ])
        xsT_v = xsT[:, :].rearrange("p (j t) -> p j t", j=CT)
        bT = sb("bT", [NST, SEQ])
        cT = sb("cT", [NST, SEQ])
        acc = sb("acc", [P, 2, 2, SEQ])
        acc_bc = sb("acc_bc", [P, 1, SEQ])
        gsq = sb("gsq", [P, 512])
        s_sb = sb("s_sb", [P, SEQ + P])
        var_g = sb("var_g", [P, 2])
        rstd_g = sb("rstd_g", [P, 2])
        arena = sb("arena", [P, 8192])
        m0 = arena[:, 0:2048].rearrange("p (r h t) -> p r h t", r=2, h=4)
        m1 = arena[:, 2048:3072].rearrange("p (r h t) -> p r h t", r=2, h=4)
        xtok = arena[:, 3072:4096].rearrange("p (r c n) -> p r c n", r=2, c=2)
        xdt = arena[:, 4096:5120].rearrange("p (r c n) -> p r c n", r=2, c=2)
        sz = arena[:, 5120:6144].rearrange("p (r n) -> p r n", r=2)
        y_sb = arena[:, 6144:7168].rearrange("p (r n) -> p r n", r=2)
        sq = arena[:, 7168:8192].rearrange("p (r n) -> p r n", r=2)
        gm = arena[:, 0:2048].rearrange("p (q n) -> p q n", q=TT)
        xx = arena[:, 2048:4096].rearrange("p (q n) -> p q n", q=TT)
        x1r = arena[:, 4096:6144].rearrange("p (q n) -> p q n", q=TT)
        hraw = arena[:, 6144:7168].rearrange("p (r n) -> p r n", r=2)
        sg = arena[:, 7168:8192].rearrange("p (r n) -> p r n", r=2)
        ssq_x1 = sb("ssq_x1", [P, TT])
        var_x1 = sb("var_x1", [P, TT])
        rstd_x1 = sb("rstd_x1", [P, TT])
        raw = [arena[:, SLOT * n:SLOT * n + SLOT] for n in range(4)]
        v, q_, neg, e, u, lnu, d, c_, f, dtT, dec, part = (
            arena[:, 4 * SLOT + SEQ * n:4 * SLOT + SEQ * (n + 1)] for n in range(12))
        hi, mid, lo = (w.bitcast(BF16)[:, 0:SEQ] for w in (v, neg, e))
        xr_first = xsT[:, 3584:4096].rearrange("p (t n) -> p t n", t=2)
        xr_rest = xsT[:, 2048:3584].rearrange("p (t n) -> p t n", t=6)

        def xr_tile(t):
            return xr_first[:, t, :] if t < 2 else xr_rest[:, t - 2, :]

        junk = xsT[:, 0:2048].rearrange("p (t n) -> p t n", t=TT)
        prob, score, top, mask0, mask1, wsc, topf = (rk[:, 64 * n:64 * n + 64].rearrange("p (t e) -> p t e", t=TT)
                                                     for n in range(7))
        topi = rk[:, 448:512].bitcast(U32).rearrange("p (t e) -> p t e", t=TT)
        combx = rk[:, 512:512 + TT * NR].rearrange("p (t e) -> p t e", t=TT)
        wsum = rk[:, 584:592]
        wnorm = rk[:, 592:600]
        combT = xsT[0:32, 0:1024]
        cpart = acc[0:32, :, :, :].rearrange("p a b c -> p (a b c)")
        cmid = xsT[0:32, 1024:1536].bitcast(BF16)
        raw_gu = xsT[:, 1536:2560].rearrange("p (r n) -> p r n", r=2)
        raw_d = xsT[:, 2560:3072].rearrange("p (r n) -> p r n", r=2)
        sel_exp = xsT[0:SPLIT * 32, 3072:3072 + FFP // 2].bitcast(BF16)

        bank = [ctx.enter_context(nc.psum_tensor(f"bank{n}", [P, 512], F32)) for n in range(8)]
        bank_full = [sem(f"bank_full{n}") for n in range(8)]
        bank_free = [sem(f"bank_free{n}") for n in range(8)]

        loaded_x = [sem(f"loaded_x{n}") for n in range(2)]
        loaded_small = [sem(f"loaded_small{n}") for n in range(2)]
        loaded_raw = [sem(f"loaded_raw{n}") for n in range(4)]
        loaded_xq = [sem(f"loaded_xq{n}") for n in range(2)]
        loaded_gu = [sem(f"loaded_gu{n}") for n in range(2)]
        loaded_d = [sem(f"loaded_d{n}") for n in range(2)]
        loaded_sel, loaded_xx = sem("loaded_sel"), sem("loaded_xx")
        v_step, a_step, p_step = sem("v_step"), sem("a_step"), sem("p_step")
        r_step, ra_step = sem("r_step"), sem("ra_step")
        names = ("chunk_hi", "small_hi", "wx_split", "wx_rest_split", "wzo_split", "wo_scaled", "xr_hi",
                 "xdt_ready", "m0_step", "m1_ready", "g_ready", "g_hi", "g_split",
                 "sq_ready", "gsq_ready", "tap_ready", "conv_step", "xs_ready", "op_done", "rstd_ready",
                 "xq_normed", "xn_hi",
                 "gu_hi", "gu_split", "d_hi", "d_split", "h_ready", "h_hi", "h_split", "down_done",
                 "t_step", "ssq_ready", "var1_ready", "rstd1_ready", "x1r_ready", "x1t_hi", "xx_step",
                 "out_step", "out_ready")
        S = {n: sem(n) for n in names}
        stored = sem("stored")
        block = ctx.enter_context(nc.Block())

        def await_full(eng, table, key, it=0):
            b, n = fills(table, key, it)
            eng.wait_ge(bank_full[b], n + 1)
            return bank[b]

        def await_free(eng, table, key, it=0):
            b, n = fills(table, key, it)
            if not (isinstance(n, int) and n == 0):
                eng.wait_ge(bank_free[b], n)
            return bank[b]

        def await_read(eng, table, key, it=0):
            b, n = fills(table, key, it)
            eng.wait_ge(bank_free[b], n + 1)

        def is_full(ins, table, key):
            ins.then_inc(bank_full[table[key][0]], 1)

        def is_free(ins, table, key):
            ins.then_inc(bank_free[table[key][0]], 1)

        def reached(eng, name, n):
            eng.wait_ge(S[name], n + CREDIT)

        def sequences(eng):
            yield 0, IN_BEGIN, 0, False, False
            with eng.Fori(0, BATCH - 2) as it:
                yield it + 1, IN_SEQ, it, True, False
            yield BATCH - 1, IN_LAST, 0, True, True

        def steps_of(last):
            return range(PAIRS + 3 if last else PAIRS)

        def slot_free(eng, table, i, it):
            if ("y", i - 1) in table:
                b6, f6 = fills(table, ("y", i - 1), it)
                eng.wait_ge(bank_full[b6], f6)

        def sums(b, h):
            return b * (PAIRS - 1) + (h if h >= 0 else h + 1)

        def conv_place(unit):
            return acc[:, unit % 2, :, :] if unit < PAIRS else acc_bc

        def tiles(eng, count):
            yield 0, 0, True, False
            yield 1, 1, False, False
            with eng.Fori(1, count // 2 - 1) as n:
                yield n * 2, 0, False, False
                yield n * 2 + 1, 1, False, False
            yield count - 2, 0, False, False
            yield count - 1, 1, False, True

        def at(b, n, size):
            return slice(b * n, b * n + size) if isinstance(b, int) else bass.ds(b * n, size)

        def product(pe, dst, lhs, rhs, first, last):
            for n, (a, c) in enumerate(((0, 0), (0, 1), (1, 0))):
                ins = pe.matmul(dst, lhs(a), rhs(c), start=first and n == 0, stop=last and n == 2)
            return ins

        @block.sync
        def _(sp):
            sp.dma_start(xn_all[:, 0:2, :], x[:, 0:2, :]).then_inc(loaded_x[0], 16)

            def chunk(n):
                w, c = divmod(n, NCH)
                if w == 0:
                    at0, size = WX_CHUNKS[c]
                    src = wx[:, KH * at0:KH * (at0 + size)]
                else:
                    src = (wz, wo)[w - 1][:, 1024 * c:1024 * c + 1024]
                sp.dma_start(raw[n % 4][:, 0:src.shape[1]], src).then_inc(loaded_raw[n % 4], 16)

            sp.dma_start(pack_a[:], pack_a_in).then_inc(loaded_small[0], 16)
            chunk(0)
            chunk(1)
            sp.dma_start(xn_all[:, 2:TT, :], x[:, 2:TT, :]).then_inc(loaded_x[1], 16)
            for n in range(2, 4):
                chunk(n)
            for dst, src in ((pack_b, pack_b_in), (eye, eye_in), (sel_head, sel_head_in)):
                sp.dma_start(dst[:], src).then_inc(loaded_small[1], 16)
            for n in (4, 5, 6, 7, 8, 9, 10, 11):
                if n in (4, 5):
                    reached(sp, "wx_split", n - 3)
                elif n < 2 * NCH:
                    reached(sp, "wx_rest_split", n - 5)
                else:
                    reached(sp, "wzo_split", n - 2 * NCH + 1)
                chunk(n)
            for q in range(BATCH):
                if q < 2:
                    reached(sp, "xs_ready", BATCH * UNITS)
                else:
                    await_read(sp, IN_LAST, ("xn", q - 2))
                sp.dma_start(acc[:, q % 2, :, :], x[:, 2 * q:2 * q + 2, :]).then_inc(loaded_xq[q % 2], 16)

            def weights(m, r):
                reached(sp, "gu_split", m - 1)
                sp.dma_start(raw_gu[:, r, :], wgu[at(m, P, P), :]).then_inc(loaded_gu[r], 16)
                reached(sp, "d_split", m - 1)
                sp.dma_start(raw_d[:, r, :], wd[at(m, P, P), :]).then_inc(loaded_d[r], 16)

            b6, n6 = fills(IN_LAST, ("y", 5))
            sp.wait_ge(bank_free[b6], n6 + 1)
            weights(0, 0)
            weights(1, 1)
            b6, n6 = fills(IN_LAST, ("y", 7))
            sp.wait_ge(bank_free[b6], n6 + 1)
            sp.dma_start(sel_exp, sel_exp_in).then_inc(loaded_sel, 16)
            await_read(sp, IN_LAST, ("op", 0))
            sp.dma_start(xx, x).then_inc(loaded_xx, 16)
            with sp.Fori(1, (FT + MT) // 2) as n:
                weights(n * 2, 0)
                weights(n * 2 + 1, 1)
            for n in range(4):
                reached(sp, "out_ready", n + 1)
                sp.dma_start(out[:, 2 * n:2 * n + 2, :], xx[:, 2 * n:2 * n + 2, :]).then_inc(stored, 16)
            sp.wait_ge(stored, 16 * 4)

        SMALL = (16, 3 * 16)

        def split_wx(eng, c, name):
            a, size = WX_CHUNKS[c]
            reached(eng, "chunk_hi", c + 1)
            ins = eng.tensor_tensor(wx_v[:, 1, :, a:a + size], raw[c][:, 0:KH * size].rearrange("p (k n) -> p k n", k=KH),
                                    wx_v[:, 0, :, a:a + size].bitcast(F32), ALU.subtract)
            ins.then_inc(S[name], 1)

        @block.vector
        def _(dve):
            steps = [0]

            def step(ins):
                steps[0] += 1
                ins.then_inc(v_step, 1)
                dve.wait_ge(v_step, steps[0])

            def many(made):
                for ins in made:
                    steps[0] += 1
                    ins.then_inc(v_step, 1)
                dve.wait_ge(v_step, steps[0])

            for n in ("wx_split", "m0_step", "g_split", "conv_step", "xq_normed", "h_ready", "h_split",
                      "t_step", "var1_ready", "x1r_ready", "out_step", "out_ready"):
                dve.sem_inc(S[n], CREDIT)
            dve.memset(power[:], -0.5)
            dve.memset(ones[:], 1.0)
            step(dve.memset(comb_split[:], 0.0))

            def centre(g):
                a, b = LN_GROUPS[g]
                dve.wait_ge(loaded_x[g], 16)
                step(dve.reduce_sum(st[:, 0, a:b], xn_all[:, a:b, :], AX_X))
                step(dve.tensor_scalar(st[:, 1, a:b], st[:, 0, a:b], 1.0 / HID, None, ALU.mult))
                many([dve.tensor_scalar(xn_all[:, t, :], xn_all[:, t, :], st[:, 1, t:t + 1], None, ALU.subtract)
                      for t in range(a, b)])
                assert steps[0] == V_CENTRED[g], steps

            def norm_xr(g):
                a, b = LN_GROUPS[g]
                dve.wait_ge(p_step, P_RSTD * (g + 1))
                many([dve.tensor_scalar(xr_tile(t), xn_all[:, t, :], st[:, 5, t:t + 1], None, ALU.mult)
                      for t in range(a, b)])
                assert steps[0] == V_XR[g], steps

            def norm_xn(g):
                many([dve.tensor_scalar(xn_all[:, t, :], xn_all[:, t, :], st[:, 4, t:t + 1], None, ALU.mult)
                      for t in range(*LN_GROUPS[g])])

            def split_xr(q):
                pb = await_full(dve, IN_SETUP, ("xr", q))
                reached(dve, "xr_hi", q + 1)
                for k in range(KH):
                    toks = slice(SEQ * q, SEQ * q + SEQ)
                    ins = dve.scalar_tensor_tensor(xrT[:, 1, k, toks], pb[:, 256 * k:256 * k + 256], ln1_sb[:, k:k + 1],
                                                   xrT[:, 0, k, toks].bitcast(F32), ALU.mult, ALU.subtract)
                is_free(ins, IN_SETUP, ("xr", q))

            def convolve(unit, table, it, turn, name="xp"):
                key = (name, unit)
                pb = await_full(dve, table, key, it)
                n = place(unit)
                reached(dve, "tap_ready", turn * UNITS + n + 1)
                n_tiles = 2 if unit < PAIRS else 1
                at0 = turn * CONV + n * 4 - (2 if n > place(PAIRS) else 0)
                for s in range(1, TAPS):
                    for jj in range(n_tiles):
                        if s > 1:
                            reached(dve, "conv_step", at0 + (s - 2) * n_tiles + jj + 1)
                        a = conv_place(unit)[:, jj, s:SEQ]
                        ins = dve.scalar_tensor_tensor(a, pb[:, jj * SEQ:jj * SEQ + SEQ - s],
                                                       cw[:, 2 * unit + jj, TAPS - 1 - s:TAPS - s], a, ALU.mult, ALU.add)
                        if s < TAPS - 1:
                            ins.then_inc(S["conv_step"], 1)
                is_free(ins, table, key)

            centre(0)
            norm_xr(0)
            norm_xn(0)
            split_wx(dve, 0, "wx_split")
            split_xr(0)
            centre(1)
            convolve(ORDER[0], IN_FIRST, 0, 0)
            split_wx(dve, 1, "wx_split")
            convolve(ORDER[1], IN_FIRST, 0, 0)
            norm_xr(1)
            norm_xn(1)
            for q in range(1, BATCH):
                split_xr(q)
            reached(dve, "small_hi", 1)
            many([dve.tensor_tensor(wdt_r[:, 1], wdt_sb, wdt_r[:, 0].bitcast(F32), ALU.subtract),
                  dve.tensor_tensor(wgate_r[:, 1], wgate_sb, wgate_r[:, 0].bitcast(F32), ALU.subtract)])
            assert steps[0] == V_WDT, (steps, V_WDT)
            convolve(ORDER[2], IN_FIRST, 0, 0)
            made = []
            for b in range(BATCH):
                pb = await_full(dve, IN_SETUP, ("dt", b // 2))
                rows = slice(HEADS * b, HEADS * b + HEADS)
                made.append(dve.tensor_scalar(v[rows, :], pb[rows, (b % 2) * SEQ:(b % 2) * SEQ + SEQ], dt_bias[rows, :], None,
                                              ALU.add))
            many(made)
            for n in range(2):
                dve.sem_inc(bank_free[IN_SETUP[("dt", n)][0]], 1)
            step(dve.scalar_tensor_tensor(neg, v, -1.0, v, ALU.mult, ALU.min))
            assert steps[0] == V_NEG
            convolve(ORDER[3], IN_FIRST, 0, 0)
            dve.wait_ge(a_step, A_EXP)
            step(dve.tensor_scalar(u, e, 1.0, None, ALU.add))
            assert steps[0] == V_U
            many([dve.tensor_scalar(d, u, -1.0, None, ALU.add), dve.tensor_scalar(f, e, -1.0, 1.0, ALU.mult, ALU.add),
                  dve.tensor_scalar(q_, v, 0.0, None, ALU.max)])
            step(dve.tensor_tensor(c_, e, d, ALU.subtract))
            step(dve.tensor_tensor(c_, c_, f, ALU.mult))
            dve.wait_ge(a_step, A_LN)
            step(dve.tensor_tensor(c_, c_, lnu, ALU.add))
            step(dve.tensor_tensor(dtT, q_, c_, ALU.add))
            assert steps[0] == V_DT
            convolve(ORDER[4], IN_FIRST, 0, 0)
            dve.wait_ge(a_step, A_DEC)
            step(dve.memset(dec[:, 0:1], 0.0))
            assert steps[0] == V_RESET
            convolve(ORDER[5], IN_FIRST, 0, 0)
            dve.wait_ge(a_step, A_HI)
            step(dve.tensor_tensor(part, dec, hi, ALU.subtract))
            assert steps[0] == V_PART

            def by_head(s, whole):
                return [dve.tensor_copy(decay0[HEADS * s:HEADS * s + HEADS, SEQ * b:SEQ * b + SEQ],
                                        whole[HEADS * b:HEADS * b + HEADS, :]) for b in range(BATCH)]

            many(by_head(0, hi))
            convolve(ORDER[6], IN_FIRST, 0, 0)
            dve.wait_ge(a_step, A_MID)
            step(dve.tensor_tensor(lo, part, mid, ALU.subtract))
            many(by_head(1, mid) + by_head(2, lo))
            step(dve.tensor_copy(decay1[:, :].rearrange("h (b t) -> h b t", b=BATCH),
                                 decay0[:, :].rearrange("h (b c t) -> h b c t", b=BATCH, c=2)[:, :, 1, :]))
            step(dve.memset(decay1[:, :].rearrange("h (b t) -> h b t", b=BATCH)[:, :, 0:1], 0.0))
            assert steps[0] == V_DECAY, (steps, V_DECAY)
            convolve(ORDER[7], IN_FIRST, 0, 0)
            convolve(ORDER[8], IN_FIRST, 0, 0)
            reached(dve, "wzo_split", 2 * NCH)

            r_steps = [0]

            def route(made):
                for ins in made:
                    r_steps[0] += 1
                    ins.then_inc(r_step, 1)
                dve.wait_ge(r_step, r_steps[0])

            def variance(key, table, it):
                pb = await_full(dve, table, key, it)
                ins = dve.tensor_scalar(var_g[:], pb[:, 0:2], 1.0 / DIN, EPS, ALU.mult, ALU.add)
                is_free(ins, table, key)

            def residual(key, seq, table, it):
                pb = await_full(dve, table, key, it)
                reached(dve, "rstd_ready", seq + 1)
                for c in range(2):
                    xc = xn_all[:, at(seq, 2, 2), :][:, c, :]
                    ins = dve.scalar_tensor_tensor(xc, pb[:, c * HID:c * HID + HID], rstd_g[:, c:c + 1], xc,
                                                   ALU.mult, ALU.add)
                is_free(ins, table, key)

            for b, table, it, prev, last in sequences(dve):
                for i in steps_of(last):
                    for unit in convolved_at(i, prev, last):
                        convolve(unit, table, it, b if i < 3 else b + 1, "xp" if i > 0 else "carried")
                    if i < PAIRS:
                        r = i % 2
                        slot_free(dve, table, i, it)
                        scans = (("bc0a", m0[:, r, 0:2, :], 0), ("bc0b", m0[:, r, 2:4, :], 0), ("bc1", m1[:, r, :, :], 1))
                        for name, dst, e_ in scans:
                            pa = await_full(dve, table, (name, i), it)
                            ins = dve.tensor_tensor_scan(dst.rearrange("p h t -> p (h t)"), pa[:, :], eye[:, e_, :],
                                                         0.0, ALU.mult, ALU.add)
                            is_free(ins, table, (name, i))
                        if i == 0:
                            await_read(dve, table, ("s", 0), it)
                        for half in range(2):
                            await_read(dve, table, (("bc0a", "bc0b")[half], i), it)
                            mm = m0[:, r, 2 * half:2 * half + 2, :]
                            ins = dve.tensor_tensor(mm, mm, s_sb[:, 0:SEQ].unsqueeze(1).to_broadcast([P, 2, SEQ]), ALU.mult)
                            ins.then_inc(S["m0_step"], 1)
                    if last:
                        for q in XN_AT.get(i, ()):
                            dve.wait_ge(loaded_xq[q % 2], 16 * (q // 2 + 1))
                            for t in range(2):
                                tt = 2 * q + t
                                ins = dve.tensor_scalar(acc[:, q % 2, t, :], acc[:, q % 2, t, :], st[:, 1, tt:tt + 1],
                                                        st[:, 4, tt:tt + 1], ALU.subtract, ALU.mult)
                            ins.then_inc(S["xq_normed"], 1)
                    if i == 3 and prev:
                        residual(("op", -1), b - 1, table, it)
                    h = in_step(i, 1, prev)
                    if h is not None:
                        pb = await_full(dve, table, ("y", h), it)
                        reached(dve, "g_hi", b * PAIRS + h - 1)
                        reached(dve, "g_split", b * PAIRS + h - 1)
                        for jj in range(2):
                            j = 2 * (h % PAIRS) + jj
                            ins = dve.scalar_tensor_tensor(y_sb[:, h % 2, jj * SEQ:jj * SEQ + SEQ], xsT_v[:, j, :],
                                                           dcol[:, j:j + 1], pb[:, jj * SEQ:jj * SEQ + SEQ],
                                                           ALU.mult, ALU.add)
                        is_free(ins, table, ("y", h))
                    if i == 2 and prev:
                        variance(("ssq", -1), table, it)
                    h = in_step(i, 2, prev)
                    if h is not None:
                        reached(dve, "g_hi", b * PAIRS + h + 1)
                        dve.tensor_tensor(g_r[:, 1, h % 2, :], y_sb[:, h % 2, :], g_r[:, 0, h % 2, :].bitcast(F32),
                                          ALU.subtract).then_inc(S["g_split"], 1)
                    if last:
                        for q in XN_AT.get(i, ()):
                            pb = await_full(dve, table, ("xn", q), it)
                            reached(dve, "xn_hi", q + 1)
                            toks = slice(SEQ * q, SEQ * q + SEQ)
                            ins = dve.tensor_tensor(xnT[:, 1, :, toks], pb[:, :].rearrange("p (k t) -> p k t", k=KH),
                                                    xnT[:, 0, :, toks].bitcast(F32), ALU.subtract)
                            is_free(ins, table, ("xn", q))
                    if last and i == ROUTE_STEP + 1:
                        await_read(dve, table, ("gate", 0), it)
                        route([dve.tensor_scalar(score, prob, 1.0, None, ALU.add)])
                        route([dve.reciprocal(score, score)])
                        route([dve.max(top[:, t, :], score[:, t, :]) for t in range(TT)])
                        route([dve.max_index(topi[:, t, :], top[:, t, :], score[:, t, :]) for t in range(TT)])
                        route([dve.tensor_copy(topf, topi), dve.memset(combx, 1.0)])
                        route([dve.tensor_tensor(mask0, iota, topf[:, :, 0:1].to_broadcast([P, TT, NE]), ALU.is_equal),
                               dve.tensor_tensor(mask1, iota, topf[:, :, 1:2].to_broadcast([P, TT, NE]), ALU.is_equal)])
                        route([dve.tensor_tensor(mask0, mask0, mask1, ALU.add)])
                        route([dve.tensor_tensor(wsc, mask0, score, ALU.mult)])
                        route([dve.reduce_sum(wsum, wsc, AX_X)])
                        route([dve.tensor_scalar(wsum, wsum, 1e-20, None, ALU.add)])
                        route([dve.reciprocal(wnorm, wsum)])
                        route([dve.tensor_tensor(wsc, wsc, wnorm.unsqueeze(2).to_broadcast([P, TT, NE]), ALU.mult)])
                        route([dve.tensor_scalar(combx[:, :, 0:NE], wsc, ROUTED_SCALE, None, ALU.mult)])
                        assert r_steps[0] == R_COMB, r_steps
                    if last and i == COMB_STEP + 1:
                        dve.wait_ge(ra_step, RA_HI)
                        route([dve.tensor_tensor(cpart[0:NR, :], combT[0:NR, :], comb_split[0:NR, :], ALU.subtract)])
                        assert r_steps[0] == R_PART
                        dve.wait_ge(ra_step, RA_MID)
                        route([dve.tensor_tensor(comb_split[64:64 + NR, :], cpart[0:NR, :], cmid[0:NR, 0:TOK], ALU.subtract)])
                        assert r_steps[0] == R_SPLIT
                    if i == PAIRS + 2:
                        variance(("ssq", 0), table, it)
                        residual(("op", 0), b, table, it)

            def split_hidden(n):
                reached(dve, "h_hi", n["count"])
                u, r = n["u"], n["slot"]
                dve.tensor_tensor(hid[:, r, 1, u * HALF:u * HALF + HALF], hraw[:, u, :],
                                  hid[:, r, 0, u * HALF:u * HALF + HALF].bitcast(F32), ALU.subtract).then_inc(S["h_split"], 1)

            def hidden(base, count, table, routed):
                for m, r, first, last in tiles(dve, count):
                    for u in range(2):
                        n = (m + base) * 2 + u
                        if not (first and u == 0):
                            split_hidden({"count": n, "u": 1 - u, "slot": r if u else 1 - r})
                        if routed and first and u == 0:
                            reached(dve, "g_split", BATCH * PAIRS)
                            dve.wait_ge(loaded_sel, 16)
                        pb = await_full(dve, table, ("up", u), m)
                        await_read(dve, table, ("gate", u), m)
                        reached(dve, "h_split", n - 1)
                        dst = hraw[:, u, :]
                        ins = dve.tensor_tensor(dst, sg[:, u, :], pb[:, :], ALU.mult)
                        is_free(ins, table, ("up", u))
                        if routed:
                            pc = await_full(dve, table, ("comb", u), m)
                            await_read(dve, table, ("up", u), m)
                            ins = dve.tensor_tensor(dst, dst, pc[:, :], ALU.mult)
                            is_free(ins, table, ("comb", u))
                    if routed and first:
                        reached(dve, "ssq_ready", 1)
                        dve.tensor_scalar(var_x1[:], ssq_x1[:], 1.0 / HID, EPS, ALU.mult, ALU.add).then_inc(S["var1_ready"], 1)
                    if last:
                        split_hidden({"count": n + 1, "u": 1, "slot": r})
                    if routed and last:
                        reached(dve, "rstd1_ready", 1)
                        for q in range(TT):
                            ins = dve.tensor_scalar(x1r[:, q, :], xn_all[:, q, :], rstd_x1[:, q:q + 1], None, ALU.mult)
                        ins.then_inc(S["x1r_ready"], 1)

            hidden(0, FT, IN_MOE, True)
            for q in range(4):
                pb = await_full(dve, IN_X1T, ("x1t", q))
                reached(dve, "x1t_hi", q + 1)
                for k in range(KH):
                    toks = slice(SEQ * q, SEQ * q + SEQ)
                    ins = dve.scalar_tensor_tensor(x1T[:, 1, k, toks], pb[:, 256 * k:256 * k + 256], ln2_sb[:, k:k + 1],
                                                   x1T[:, 0, k, toks].bitcast(F32), ALU.mult, ALU.subtract)
                is_free(ins, IN_X1T, ("x1t", q))
            hidden(FT, MT, IN_MLP, False)
            for n in range(4):
                pb = await_full(dve, IN_MLP_ACC, ("acc", n))
                prod = x1r[:, 2 * n:2 * n + 2, :]
                ins = dve.tensor_tensor(prod, gm[:, 2 * n:2 * n + 2, :], pb[:, :].rearrange("p (q n) -> p q n", q=2), ALU.mult)
                ins.then_inc(S["out_step"], 1)
                if n == 0:
                    reached(dve, "xx_step", 2)
                reached(dve, "out_step", n + 1)
                dst = xx[:, 2 * n:2 * n + 2, :]
                dve.tensor_tensor(dst, dst, prod, ALU.add).then_inc(S["out_ready"], 1)

        @block.scalar
        def _(act):
            for n in ("chunk_hi", "wo_scaled", "small_hi", "xr_hi", "g_hi", "sq_ready", "tap_ready", "xs_ready", "xn_hi", "gu_hi", "d_hi", "h_hi",
                      "ssq_ready", "x1t_hi"):
                act.sem_inc(S[n], CREDIT)

            def squares(g):
                act.wait_ge(v_step, V_CENTRED[g])
                for t in range(*LN_GROUPS[g]):
                    ins = act.activation(junk[:, t, :], xn_all[:, t, :], ACT.Square, accum_out=st[:, 2, t:t + 1])
                    ins.then_inc(a_step, 1)

            def hi_xr(q):
                pb = await_full(act, IN_SETUP, ("xr", q))
                for k in range(KH):
                    ins = act.activation(xrT[:, 0, k, SEQ * q:SEQ * q + SEQ], pb[:, 256 * k:256 * k + 256], ACT.Copy,
                                         scale=ln1_sb[:, k:k + 1])
                ins.then_inc(S["xr_hi"], 1)

            def hi_chunk(n):
                w, c = divmod(n, NCH)
                act.wait_ge(loaded_raw[n % 4], 16 * (n // 4 + 1))
                if w == 0:
                    a, size = WX_CHUNKS[c]
                    ins = act.activation(wx_v[:, 0, :, a:a + size], raw[c][:, 0:KH * size].rearrange("p (k n) -> p k n", k=KH),
                                         ACT.Copy)
                elif w == 1:
                    ins = act.activation(wz_v[:, 0, :, 512 * c:512 * c + 512],
                                         raw[n % 4][:, 0:1024].rearrange("p (k n) -> p k n", k=KH), ACT.Copy)
                else:
                    for j in range(4):
                        part_j = raw[n % 4][:, HID * j:HID * j + HID]
                        ins = act.activation(part_j, part_j, ACT.Copy, scale=mn[:, 4 * c + j:4 * c + j + 1])
                    ins.then_inc(S["wo_scaled"], 1)
                    reached(act, "wo_scaled", c + 1)
                    ins = act.activation(wo_r[:, 0, 1024 * c:1024 * c + 1024], raw[n % 4][:, 0:1024], ACT.Copy)
                ins.then_inc(S["chunk_hi"], 1)

            def first_tap(unit, table, it, turn, name="xp"):
                pb = await_full(act, table, (name, unit), it)
                if unit == PAIRS:
                    gone = place(PAIRS) + 1 - UNITS
                else:
                    gone = place(unit - 2) + 1 if unit > 1 else unit - 1
                if not (isinstance(turn, int) and turn == 0 and gone <= 0):
                    reached(act, "xs_ready", turn * UNITS + gone)
                for jj in range(2 if unit < PAIRS else 1):
                    ins = act.activation(conv_place(unit)[:, jj, :], pb[:, jj * SEQ:jj * SEQ + SEQ], ACT.Identity,
                                         bias=cb[:, 2 * unit + jj:2 * unit + jj + 1],
                                         scale=cw[:, 2 * unit + jj, TAPS - 1:TAPS])
                ins.then_inc(S["tap_ready"], 1)

            def silu_conv(unit, table, it, name="xp"):
                await_read(act, table, (name, unit), it)
                if unit < PAIRS:
                    ins = act.activation(xsT_v[:, 2 * unit:2 * unit + 2, :], conv_place(unit), ACT.Silu)
                else:
                    act.activation(bT[:], acc_bc[0:NST, 0, :], ACT.Silu)
                    ins = act.activation(cT[:], acc_bc[NST:P, 0, :], ACT.Silu)
                ins.then_inc(S["xs_ready"], 1)

            squares(0)
            hi_chunk(0)
            act.wait_ge(loaded_small[0], SMALL[0])
            hi_xr(0)
            hi_chunk(1)
            hi_chunk(2)
            hi_chunk(3)
            first_tap(ORDER[0], IN_FIRST, 0, 0)
            squares(1)
            first_tap(ORDER[1], IN_FIRST, 0, 0)
            hi_chunk(4)
            for q in range(1, BATCH):
                hi_xr(q)
            act.wait_ge(loaded_small[1], SMALL[1])
            act.activation(wdt_r[:, 0], wdt_sb, ACT.Copy)
            act.activation(wgate_r[:, 0], wgate_sb, ACT.Copy).then_inc(S["small_hi"], 1)
            act.wait_ge(a_step, A_SQUARES[1])
            silu_conv(ORDER[0], IN_FIRST, 0)
            first_tap(ORDER[2], IN_FIRST, 0, 0)
            hi_chunk(5)
            silu_conv(ORDER[1], IN_FIRST, 0)
            first_tap(ORDER[3], IN_FIRST, 0, 0)
            hi_chunk(6)
            silu_conv(ORDER[2], IN_FIRST, 0)
            first_tap(ORDER[4], IN_FIRST, 0, 0)
            act.activation(neg_a, neg_a, ACT.Exp).then_inc(a_step, 1)
            act.wait_ge(a_step, A_SQUARES[1] + 1)
            act.mul(neg_a, neg_a, -1.0).then_inc(a_step, 1)
            act.wait_ge(v_step, V_NEG)
            act.activation(e, neg, ACT.Exp).then_inc(a_step, 1)
            act.wait_ge(v_step, V_U)
            act.activation(lnu, u, ACT.Ln).then_inc(a_step, 1)
            hi_chunk(7)
            silu_conv(ORDER[3], IN_FIRST, 0)
            act.wait_ge(v_step, V_DT)
            act.wait_ge(a_step, A_NEGA)
            act.activation(dec, dtT, ACT.Exp, scale=neg_a).then_inc(a_step, 1)
            first_tap(ORDER[5], IN_FIRST, 0, 0)
            pb = await_full(act, IN_SETUP, ("dtt", 0))
            is_free(act.activation(dt_tok[:, :, :].rearrange("p c n -> p (c n)"), pb[:, 0:2 * P], ACT.Copy), IN_SETUP,
                    ("dtt", 0))
            hi_chunk(8)
            silu_conv(ORDER[4], IN_FIRST, 0)
            act.wait_ge(v_step, V_RESET)
            act.activation(hi, dec, ACT.Copy).then_inc(a_step, 1)
            first_tap(ORDER[6], IN_FIRST, 0, 0)
            silu_conv(ORDER[5], IN_FIRST, 0)
            hi_chunk(9)
            act.wait_ge(v_step, V_PART)
            act.activation(mid, part, ACT.Copy).then_inc(a_step, 1)
            first_tap(ORDER[7], IN_FIRST, 0, 0)
            silu_conv(ORDER[6], IN_FIRST, 0)
            hi_chunk(10)
            first_tap(ORDER[8], IN_FIRST, 0, 0)
            silu_conv(ORDER[7], IN_FIRST, 0)
            hi_chunk(11)
            silu_conv(ORDER[8], IN_FIRST, 0)
            reached(act, "wzo_split", 2 * NCH)

            def hi_gu(m, r):
                act.wait_ge(loaded_gu[r], (m - r) * 8 + 16)
                act.activation(wgu_r[:, r, 0].rearrange("p k g n -> p (k g n)"), raw_gu[:, r, :], ACT.Copy)\
                   .then_inc(S["gu_hi"], 1)

            def hi_d(m, r):
                act.wait_ge(loaded_d[r], (m - r) * 8 + 16)
                act.activation(wd_r[:, r, 0, :], raw_d[:, r, :], ACT.Copy).then_inc(S["d_hi"], 1)

            for b, table, it, prev, last in sequences(act):
                for i in steps_of(last):
                    for unit in convolved_at(i, prev, last):
                        first_tap(unit, table, it, b if i < 3 else b + 1, "xp" if i > 0 else "carried")
                    if i < PAIRS:
                        pb = await_full(act, table, ("xtr", i), it)
                        reached(act, "xdt_ready", b * PAIRS + i - 1)
                        ins = act.activation(xtok[:, i % 2, :, :].rearrange("p c n -> p (c n)"), pb[:, :], ACT.Copy)
                        is_free(ins, table, ("xtr", i))
                        pb = await_full(act, table, ("z", i), it)
                        reached(act, "g_ready", b * PAIRS + i - 1)
                        ins = act.activation(sz[:, i % 2, :], pb[:, :], ACT.Silu)
                        is_free(ins, table, ("z", i))
                    if i == 0:
                        pb = await_full(act, table, ("s", 0), it)
                        reached(act, "m0_step", b * PAIRS * 2)
                        reached(act, "m1_ready", b * PAIRS)
                        ins = act.activation(s_sb[:], pb[:, 0:SEQ + P], ACT.Copy)
                        is_free(ins, table, ("s", 0))
                    for q in XN_AT.get(i, ()) if last else ():
                        pb = await_full(act, table, ("xn", q), it)
                        ins = act.activation(xnT[:, 0, :, SEQ * q:SEQ * q + SEQ], pb[:, :].rearrange("p (k t) -> p k t", k=KH),
                                             ACT.Copy)
                        ins.then_inc(S["xn_hi"], 1)
                    if last and i == ROUTE_STEP:
                        pb = await_full(act, table, ("gate", 0), it)
                        ins = act.activation(prob, pb[:, 0:TT * NE].rearrange("p (t e) -> p t e", t=TT), ACT.Exp, scale=-1.0)
                        is_free(ins, table, ("gate", 0))
                    h = in_step(i, 2, prev)
                    if h is not None:
                        reached(act, "g_ready", b * PAIRS + h + 1)
                        if h == 0:
                            if prev:
                                await_full(act, table, ("ssq", -1), it)
                            dst = gsq[:, :]
                        else:
                            if h != 1 or prev:
                                reached(act, "gsq_ready", sums(b, h - 2 if h != 1 else -1))
                            dst = sq[:, h % 2, :]
                        act.activation(dst, y_sb[:, h % 2, :], ACT.Square).then_inc(S["sq_ready"], 1)
                        reached(act, "op_done", b * PAIRS + h - 1)
                        act.activation(g_r[:, 0, h % 2, :], y_sb[:, h % 2, :], ACT.Copy).then_inc(S["g_hi"], 1)
                    for unit in convolved_at(i, prev, last):
                        own = i < 3
                        if unit < PAIRS:
                            await_read(act, table, ("y", -1 if own else unit), it)
                        silu_conv(unit, table, it, "xp" if i > 0 else "carried")
                    if last and i == COMB_STEP:
                        for n in range(2):
                            pb = await_full(act, table, ("comb", n), it)
                            ins = act.activation(combT[0:NR, 512 * n:512 * n + 512], pb[0:NR, :], ACT.Copy)
                            is_free(ins, table, ("comb", n))
                        await_read(act, table, ("comb", 0), it)
                        await_read(act, table, ("comb", 1), it)
                        act.activation(comb_split[0:NR, :], combT[0:NR, :], ACT.Copy).then_inc(ra_step, 1)
                    if last and i == COMB_STEP + 1:
                        act.wait_ge(r_step, R_PART)
                        act.activation(cmid[0:NR, 0:TOK], cpart[0:NR, :], ACT.Copy).then_inc(ra_step, 1)
                        act.wait_ge(ra_step, RA_HI + 1)
                        act.activation(comb_split[32:32 + NR, :], cmid[0:NR, 0:TOK], ACT.Copy).then_inc(ra_step, 1)
                        hi_gu(0, 0)

            def hidden(base, count, table, routed):
                made = ("comb" if routed else "up")
                for m, r, first, last in tiles(act, count):
                    for u in range(2):
                        n = (m + base) * 2 + u
                        if not (first and u == 0):
                            high_half(table, made, m if u else m - 1, 1 - u, r if u else 1 - r, n)
                        pb = await_full(act, table, ("gate", u), m)
                        b2, n2 = fills(table, ("up", u), m)
                        act.wait_ge(bank_free[b2], n2 - 1)
                        if routed and first and u == 0:
                            reached(act, "gsq_ready", BATCH * (PAIRS - 1))
                        ins = act.activation(sg[:, u, :], pb[:, :], ACT.Silu)
                        is_free(ins, table, ("gate", u))
                        if u == 0:
                            if routed or not last:
                                hi_gu(m + (base + 1), 1 - r)
                            hi_d(m + base, r)
                    if routed and first:
                        await_read(act, IN_LAST, ("op", 0))
                        for q in range(TT):
                            ins = act.activation(x1r[:, q, :], xn_all[:, q, :], ACT.Square, accum_out=ssq_x1[:, q:q + 1])
                        ins.then_inc(S["ssq_ready"], 1)
                    if last:
                        high_half(table, made, m, 1, r, n + 1)

            def high_half(table, made, m, u, r, n):
                await_read(act, table, (made, u), m)
                reached(act, "down_done", n - 4)
                act.activation(hid[:, r, 0, u * HALF:u * HALF + HALF], hraw[:, u, :], ACT.Copy).then_inc(S["h_hi"], 1)

            hidden(0, FT, IN_MOE, True)
            for q in range(4):
                pb = await_full(act, IN_X1T, ("x1t", q))
                for k in range(KH):
                    ins = act.activation(x1T[:, 0, k, SEQ * q:SEQ * q + SEQ], pb[:, 256 * k:256 * k + 256], ACT.Copy,
                                         scale=ln2_sb[:, k:k + 1])
                ins.then_inc(S["x1t_hi"], 1)
            for n in range(4):
                pb = await_full(act, IN_MOE_ACC, ("acc", n))
                ins = act.activation(gm[:, 2 * n:2 * n + 2, :], pb[:, :].rearrange("p (q n) -> p q n", q=2), ACT.Silu)
                is_free(ins, IN_MOE_ACC, ("acc", n))
            hidden(FT, MT, IN_MLP, False)

        @block.gpsimd
        def _(pool):
            for n in ("wx_rest_split", "wzo_split", "xdt_ready", "m1_ready", "g_ready", "gsq_ready", "rstd_ready", "gu_split",
                      "d_split", "rstd1_ready", "xx_step"):
                pool.sem_inc(S[n], CREDIT)
            steps = [0]

            def step(ins):
                steps[0] += 1
                ins.then_inc(p_step, 1)
                pool.wait_ge(p_step, steps[0])

            for g, (a, b) in enumerate(LN_GROUPS):
                pool.wait_ge(a_step, A_SQUARES[g])
                var, rstd, both = st[:, 2, a:b], st[:, 4, a:b], st[:, 5, a:b]
                step(pool.tensor_scalar(var, var, 1.0 / HID, None, ALU.mult))
                step(pool.tensor_scalar(rstd, var, EPS, None, ALU.add))
                step(pool.tensor_tensor(rstd, rstd, power[:, a:b], ALU.pow))
                step(pool.tensor_tensor(both, rstd, rstd, ALU.mult))
                step(pool.tensor_tensor(both, both, var, ALU.mult))
                step(pool.tensor_scalar(both, both, EPS, None, ALU.add))
                step(pool.tensor_tensor(both, both, power[:, a:b], ALU.pow))
                step(pool.tensor_tensor(both, both, rstd, ALU.mult))
                assert steps[0] == P_RSTD * (g + 1)
                if g == 0:
                    for c in range(2, NCH):
                        split_wx(pool, c, "wx_rest_split")
            pool.wait_ge(loaded_small[1], SMALL[1])
            for n in range(NCH, 3 * NCH):
                w, c = divmod(n, NCH)
                chunk = raw[n % 4][:, 0:1024]
                reached(pool, "chunk_hi", n + 1)
                if w == 1:
                    dst, hi = (wz_v[:, s, :, 512 * c:512 * c + 512] for s in (1, 0))
                    src = chunk.rearrange("p (k n) -> p k n", k=KH)
                else:
                    dst, hi = (wo_r[:, s, 1024 * c:1024 * c + 1024] for s in (1, 0))
                    src = chunk
                pool.tensor_tensor(dst, src, hi.bitcast(F32), ALU.subtract).then_inc(S["wzo_split"], 1)
            await_read(pool, IN_SETUP, ("dtt", 0))

            def split_gu(n, r):
                reached(pool, "gu_hi", n + 1)
                hi, lo = (wgu_r[:, r, s].rearrange("p k g n -> p (k g n)") for s in (0, 1))
                pool.tensor_tensor(lo, raw_gu[:, r, :], hi.bitcast(F32), ALU.subtract).then_inc(S["gu_split"], 1)

            def split_d(n, r):
                reached(pool, "d_hi", n + 1)
                pool.tensor_tensor(wd_r[:, r, 1, :], raw_d[:, r, :], wd_r[:, r, 0, :].bitcast(F32), ALU.subtract)\
                    .then_inc(S["d_split"], 1)

            def root(key, table, it):
                await_read(pool, table, key, it)
                pool.tensor_tensor(rstd_g[:], var_g[:], power[:, 0:2], ALU.pow).then_inc(S["rstd_ready"], 1)

            for b, table, it, prev, last in sequences(pool):
                for i in steps_of(last):
                    if i < PAIRS:
                        r = i % 2
                        await_read(pool, table, ("xtr", i), it)
                        slot_free(pool, table, i, it)
                        for c in range(2):
                            dt_c = dt_tok[:, c, at(b, HEADS, HEADS)][:, 4 * i:4 * i + 4]
                            ins = pool.tensor_tensor(xdt[:, r, c, :].rearrange("p (h d) -> p h d", h=4),
                                                     xtok[:, r, c, :].rearrange("p (h d) -> p h d", h=4),
                                                     dt_c.unsqueeze(2).to_broadcast([P, 4, HD]), ALU.mult)
                        ins.then_inc(S["xdt_ready"], 1)
                        await_read(pool, table, ("bc1", i), it)
                        if i == 0:
                            await_read(pool, table, ("s", 0), it)
                        ins = pool.tensor_tensor(m1[:, r, :, :], m1[:, r, :, :],
                                                 s_sb[:, SEQ:SEQ + P].unsqueeze(1).to_broadcast([P, 4, P]), ALU.mult)
                        ins.then_inc(S["m1_ready"], 1)
                    if i == 2 and prev:
                        root(("ssq", -1), table, it)
                    h = in_step(i, 1, prev)
                    if h is not None:
                        await_read(pool, table, ("y", h), it)
                        if h >= 0:
                            await_read(pool, table, ("z", h), it)
                        yv = y_sb[:, h % 2, :]
                        pool.tensor_tensor(yv, yv, sz[:, h % 2, :], ALU.mult).then_inc(S["g_ready"], 1)
                    h = in_step(i, 2, prev)
                    if h is not None and h != 0:
                        reached(pool, "sq_ready", b * PAIRS + h + 1)
                        if h != 1:
                            reached(pool, "gsq_ready", sums(b, h) - 1)
                        pool.tensor_tensor(gsq[:], gsq[:], sq[:, h % 2, :], ALU.add).then_inc(S["gsq_ready"], 1)
                    if i == PAIRS + 2:
                        split_gu(0, 0)
                        root(("ssq", 0), table, it)

            for base, count, routed in ((0, FT, True), (FT, MT, False)):
                if not routed:
                    for n in range(4):
                        await_read(pool, IN_MOE_ACC, ("acc", n))
                for m, r, first, last in tiles(pool, count):
                    if routed or not last:
                        split_gu(m + (base + 1), 1 - r)
                    split_d(m + base, r)
                    if routed and first:
                        reached(pool, "var1_ready", 1)
                        pool.tensor_tensor(rstd_x1[:], var_x1[:], power[:], ALU.pow).then_inc(S["rstd1_ready"], 1)
                    if not routed and first:
                        reached(pool, "x1r_ready", 1)
                        pool.tensor_tensor(xn_all[:], xn_all[:], gm, ALU.mult).then_inc(S["xx_step"], 1)
                        reached(pool, "xx_step", 1)
                        pool.wait_ge(loaded_xx, 16)
                        pool.tensor_tensor(xx, xx, xn_all[:], ALU.add).then_inc(S["xx_step"], 1)

        @block.tensor
        def _(pe):
            for n in ("op_done", "down_done"):
                pe.sem_inc(S[n], CREDIT)
            pe.wait_ge(loaded_small[0], SMALL[0])

            def transposes(table, key, it, tile):
                pb = await_free(pe, table, key, it)
                for k in range(KH):
                    for c in range(2):
                        ins = pe.transpose(pb[:, 256 * k + P * c:256 * k + P * c + P], tile(c)[:, k * P:k * P + P], ident)
                is_full(ins, table, key)

            def transpose_xr(q):
                pe.wait_ge(v_step, V_XR[0 if q == 0 else 1])
                transposes(IN_SETUP, ("xr", q), 0, lambda c: xr_tile(2 * q + c))

            def project(dst, w, col, tokens):
                for k in range(KH):
                    ins = product(pe, dst, lambda s: w[:, s, k, col:col + P], lambda s: xrT[:, s, k, tokens],
                                  k == 0, k == KH - 1)
                return ins

            def project_x(unit, table, it, tokens):
                pb = await_free(pe, table, ("xp", unit), it)
                for jj in range(2 if unit < PAIRS else 1):
                    ins = project(pb[:, jj * SEQ:jj * SEQ + SEQ], wx_v, (2 * unit + jj) * P, tokens)
                is_full(ins, table, ("xp", unit))

            def project_first(n):
                unit = ORDER[n]
                c = min(unit // 2, NCH - 1)
                reached(pe, "wx_split", min(c + 1, 2))
                reached(pe, "wx_rest_split", max(c - 1, 0))
                project_x(unit, IN_FIRST, 0, slice(0, SEQ))

            transpose_xr(0)
            await_read(pe, IN_SETUP, ("xr", 0))
            project_first(0)
            project_first(1)
            for q in range(1, BATCH):
                transpose_xr(q)
            project_first(2)
            for q in range(1, BATCH):
                await_read(pe, IN_SETUP, ("xr", q))
            pe.wait_ge(v_step, V_WDT)
            for n in range(2):
                pb = await_free(pe, IN_SETUP, ("dt", n))
                for b in (2 * n, 2 * n + 1):
                    for k in range(KH):
                        ins = product(pe, pb[:, (b % 2) * SEQ:(b % 2) * SEQ + SEQ], lambda s: wdt_r[:, s, k, :],
                                      lambda s: xrT[:, s, k, b * SEQ:b * SEQ + SEQ], k == 0, k == KH - 1)
                is_full(ins, IN_SETUP, ("dt", n))
            for unit in (3, 4, 5):
                project_first(unit)
            pe.wait_ge(v_step, V_DT)
            pb = await_free(pe, IN_SETUP, ("dtt", 0))
            for c in range(2):
                ins = pe.transpose(pb[:, c * P:c * P + P], dtT[:, c * P:c * P + P], ident)
            is_full(ins, IN_SETUP, ("dtt", 0))
            for unit in (6, 7, 8):
                project_first(unit)
            pe.wait_ge(v_step, V_DECAY)

            def squares_sum(key, done, table, it):
                pb = await_free(pe, table, key, it)
                reached(pe, "gsq_ready", done)
                for c in range(2):
                    for jj in range(2):
                        ins = pe.matmul(pb[:, c:c + 1], gsq[:, jj * SEQ + c * P:jj * SEQ + c * P + P], ones[:],
                                        start=(jj == 0), stop=(jj == 1))
                is_full(ins, table, key)

            for b, table, it, prev, last in sequences(pe):
                toks = at(b, SEQ, SEQ)
                nxt = None if last else at(b + 1, SEQ, SEQ)
                for i in steps_of(last):
                    if i < PAIRS:
                        pb = await_free(pe, table, ("xtr", i), it)
                        if prev and i > 3:
                            reached(pe, "xs_ready", b * UNITS + place(i) + 1)
                        for c in range(2):
                            for jj in range(2):
                                ins = pe.transpose(pb[:, c * 256 + jj * P:c * 256 + jj * P + P],
                                                   xsT_v[:, 2 * i + jj, c * P:c * P + P], ident)
                        is_full(ins, table, ("xtr", i))
                        for n, name in enumerate(("bc0a", "bc0b")):
                            pb = await_free(pe, table, (name, i), it)
                            for hh in range(2):
                                h = 4 * i + 2 * n + hh
                                ins = pe.matmul(pb[:, hh * SEQ:hh * SEQ + SEQ], sel_head[:, h:h + 1].to_broadcast([SPLIT * HEADS, P]),
                                                decay0[:, toks], start=True, stop=True)
                            is_full(ins, table, (name, i))
                        pb = await_free(pe, table, ("bc1", i), it)
                        for hh in range(4):
                            h = 4 * i + hh
                            ins = pe.matmul(pb[:, hh * P:hh * P + P], sel_head[:, h:h + 1].to_broadcast([SPLIT * HEADS, P]),
                                            decay1[:, at(b, P, P)], start=True, stop=True)
                        is_full(ins, table, ("bc1", i))
                        if i % 2 == 0 and not prev:
                            reached(pe, "wzo_split", i // 2 + 1)
                        pb = await_free(pe, table, ("z", i), it)
                        for jj in range(2):
                            ins = project(pb[:, jj * SEQ:jj * SEQ + SEQ], wz_v, (2 * i + jj) * P, toks)
                        is_full(ins, table, ("z", i))
                    h = in_step(i, 1, prev)
                    if h is not None:
                        r = h % 2
                        pb = await_free(pe, table, ("y", h), it)
                        reached(pe, "xdt_ready", b * PAIRS + h + 1)
                        reached(pe, "m0_step", (b * PAIRS + h) * 2 + 2)
                        reached(pe, "m1_ready", b * PAIRS + h + 1)
                        for jj in range(2):
                            for hh in range(2):
                                n = 2 * jj + hh
                                rows = slice(HD * hh, HD * hh + HD)
                                pe.matmul(pb[rows, jj * SEQ:jj * SEQ + SEQ], xdt[:, r, 0, n * HD:n * HD + HD], m0[:, r, n, :],
                                          start=True, stop=False)
                                ins = pe.matmul(pb[rows, jj * SEQ + P:jj * SEQ + SEQ], xdt[:, r, 1, n * HD:n * HD + HD],
                                                m1[:, r, n, :], start=False, stop=True)
                        is_full(ins, table, ("y", h))
                    if i == 0:
                        reached(pe, "xs_ready", b * UNITS + (place(PAIRS) + 1 if prev else UNITS))
                        pb = await_free(pe, table, ("s", 0), it)
                        pe.matmul(pb[:, 0:SEQ], bT[:, 0:P], cT[:, :], start=True, stop=True)
                        ins = pe.matmul(pb[:, SEQ:SEQ + P], bT[:, P:SEQ], cT[:, P:SEQ], start=True, stop=True)
                        is_full(ins, table, ("s", 0))
                    if i == 2 and prev:
                        squares_sum(("ssq", -1), sums(b, -1), table, it)
                    for unit in units_at(i, prev, last):
                        project_x(unit, table, it, toks if i < 2 else nxt)
                    for q in XN_AT.get(i, ()) if last else ():
                        reached(pe, "xq_normed", q + 1)
                        transposes(table, ("xn", q), it, lambda c: acc[:, q % 2, c, :])
                    if last and i == ROUTE_STEP:
                        pb = await_free(pe, table, ("gate", 0), it)
                        for q in range(BATCH):
                            await_read(pe, table, ("xn", q), it)
                        for t in range(TT):
                            for k in range(KH):
                                ins = product(pe, pb[:, t * NE:t * NE + NE], lambda s: xnT[:, s, k, t * P:t * P + P],
                                              lambda s: wgate_r[:, s, k, :], k == 0, k == KH - 1)
                        is_full(ins, table, ("gate", 0))
                    if last and i == COMB_STEP:
                        pe.wait_ge(r_step, R_COMB)
                        for n in range(2):
                            pb = await_free(pe, table, ("comb", n), it)
                            for t in range(4):
                                ins = pe.transpose(pb[0:NR, t * P:t * P + P], combx[:, 4 * n + t, :], ident)
                            is_full(ins, table, ("comb", n))
                    h = in_step(i, 3, prev)
                    if h is not None:
                        if h == 0:
                            if prev:
                                await_read(pe, table, ("op", -1), it)
                            else:
                                await_read(pe, IN_SETUP, ("dtt", 0))
                        if h % 2 == 0 and not prev:
                            reached(pe, "wzo_split", NCH + h // 2 + 1)
                        reached(pe, "g_split", b * PAIRS + h + 1)
                        for jj in range(2):
                            for c in range(2):
                                gcol = jj * SEQ + c * P
                                for n, (s, s2) in enumerate(((0, 0), (0, 1), (1, 0))):
                                    ins = pe.matmul(bank[OPB][:, c * HID:c * HID + HID], g_r[:, s, h % 2, gcol:gcol + P],
                                                    wo_v[:, s2, 2 * (h % PAIRS) + jj, :],
                                                    start=(h == 0 and jj == 0 and c == 0 and n == 0),
                                                    stop=(h % PAIRS == PAIRS - 1 and jj == 1 and n == 2), skip_group_check=True)
                        ins.then_inc(S["op_done"], 1)
                        if h % PAIRS == PAIRS - 1:
                            reached(pe, "op_done", b * PAIRS + h + 1)
                            pe.sem_inc(bank_full[OPB], 1)
                    if i == PAIRS + 2:
                        squares_sum(("ssq", 0), sums(b, PAIRS - 1), table, it)

            def hidden(base, count, table, acc_table, routed):
                src = xnT if routed else x1T

                def down(m, r, u, first, last, n):
                    if u == 0:
                        reached(pe, "d_split", m + (base + 1))
                    if first:
                        for h in (2 * u, 2 * u + 1):
                            await_free(pe, acc_table, ("acc", h))
                    reached(pe, "h_split", n + 1)
                    for q in range(4 * u, 4 * u + 4):
                        for p, (s, s2) in enumerate(((0, 0), (0, 1), (1, 0))):
                            ins = pe.matmul(bank[ACC + q // 2][:, (q % 2) * HID:(q % 2) * HID + HID],
                                            hid[:, r, s, q * P:q * P + P], wd_r[:, r, s2, :],
                                            start=(first and q % 2 == 0 and p == 0), stop=(last and p == 2),
                                            skip_group_check=True)
                        if last and q % 2 == 1:
                            ins.then_inc(bank_full[ACC + q // 2], 1)
                    if not last:
                        ins.then_inc(S["down_done"], 1)
                    else:
                        pe.wait_ge(bank_full[ACC + 2 * u + 1], fills(acc_table, ("acc", 2 * u + 1))[1] + 1)
                        pe.sem_inc(S["down_done"], 1)

                for m, r, first, last in tiles(pe, count):
                    for u in range(2):
                        toks = slice(u * HALF, u * HALF + HALF)
                        if u == 0:
                            reached(pe, "gu_split", m + (base + 1))
                        for n, name in enumerate(("gate", "comb", "up")):
                            if name == "comb":
                                if routed:
                                    pb = await_free(pe, table, ("comb", u), m)
                                    ins = pe.matmul(pb[:, :], sel_exp[:, at(m, P, P)], comb_split[:, toks], start=True, stop=True)
                                    is_full(ins, table, ("comb", u))
                                continue
                            pb = await_free(pe, table, (name, u), m)
                            for k in range(KH):
                                ins = product(pe, pb[:, :], lambda s: wgu_r[:, r, s, k, n // 2, :], lambda s: src[:, s, k, toks],
                                              k == 0, k == KH - 1)
                            is_full(ins, table, (name, u))
                        if not first:
                            down(m - 1, 1 - r, u, isinstance(m, int) and m == 1, False, (m + (base - 1)) * 2 + u)
                    if last:
                        for u in range(2):
                            down(m, r, u, False, True, (m + base) * 2 + u)

            pe.wait_ge(r_step, R_SPLIT)
            pe.wait_ge(loaded_sel, 16)
            hidden(0, FT, IN_MOE, IN_MOE_ACC, True)
            reached(pe, "x1r_ready", 1)
            for q in range(4):
                transposes(IN_X1T, ("x1t", q), 0, lambda c: x1r[:, 2 * q + c, :])
            for q in range(4):
                await_read(pe, IN_X1T, ("x1t", q))
            hidden(FT, MT, IN_MLP, IN_MLP_ACC, False)


def kernel(**inputs):
    import numpy as np
    import concourse.bacc as bacc
    from concourse.bass_utils import run_bass_kernel_spmd
    import ml_dtypes

    a = {k: np.asarray(v) for k, v in inputs.items()}
    f32, bf16 = np.float32, ml_dtypes.bfloat16

    def rows(w, k):
        return w.reshape(k, P, -1).transpose(1, 0, 2)

    proj = a["L0_attn_in_proj_w"]
    gate_rows = np.concatenate([a["L0_ffn_exp_wg"].reshape(NE * FF, HID), a["L0_ffn_shared_wg"]])
    up_rows = np.concatenate([a["L0_ffn_exp_wu"].reshape(NE * FF, HID), a["L0_ffn_shared_wu"]])
    down_rows = np.concatenate([a["L0_ffn_exp_wd"].transpose(0, 2, 1).reshape(NE * FF, HID), a["L0_ffn_shared_wd"].T])
    pad = FFP - gate_rows.shape[0]
    gate_rows, up_rows, down_rows = (np.pad(w, ((0, pad), (0, 0))) for w in (gate_rows, up_rows, down_rows))
    owner = np.minimum(np.arange(FFP) // FF, NE)
    sel_exp = np.zeros((SPLIT * 32, FFP), bf16)
    sel_head = np.zeros((SPLIT * HEADS, HEADS), bf16)
    for s in range(SPLIT):
        sel_exp[32 * s + owner, np.arange(FFP)] = 1
        sel_head[HEADS * s + np.arange(HEADS), np.arange(HEADS)] = 1
    eye = np.zeros((P, 2, 512), f32)
    for h in range(2):
        eye[np.arange(P), 0, h * SEQ + np.arange(P)] = 1
    for h in range(4):
        eye[np.arange(P), 1, h * P + np.arange(P)] = 1
    wxT = rows(proj[DIN:2 * DIN + 2 * NST].T, KH)
    wzT = rows(proj[:DIN].T, KH)
    mlp = a["L0_attn_mlp_in_w"]
    gate_all, up_all = np.concatenate([gate_rows, mlp[:INTER]]), np.concatenate([up_rows, mlp[INTER:]])
    gu = np.stack([gate_all, up_all]).reshape(2, FT + MT, P, KH, P)
    small = {
        "ident": np.eye(P, dtype=f32),
        "ln1": a["L0_attn_ln1_w"].reshape(KH, P).T,
        "conv_w": a["L0_attn_conv_w"].reshape(CT + 1, P, TAPS).transpose(1, 0, 2),
        "conv_b": a["L0_attn_conv_b"].reshape(CT + 1, P).T,
        "wdt": np.tile(rows(proj[2 * DIN + 2 * NST:].T, KH), (1, 1, BATCH)),
        "wgate": rows(a["L0_ffn_gate_w"].T, KH),
        "iota": np.broadcast_to(np.arange(NE, dtype=f32), (P, TT, NE)),
        "d_col": np.repeat(a["L0_attn_D_param"], HD).reshape(CT, P).T,
        "mnorm": a["L0_attn_mnorm_w"].reshape(CT, P).T,
        "ln2": a["L0_attn_ln2_w"].reshape(KH, P).T,
        "dt_bias": np.tile(a["L0_attn_dt_bias"], BATCH),
        "a_log": np.tile(a["L0_attn_A_log"], BATCH),
    }
    arrays = {
        "x": a["L0_attn_x"].reshape(TT, P, HID).transpose(1, 0, 2),
        "wx": np.concatenate([wxT[:, :, c:c + n].reshape(P, -1) for c, n in WX_CHUNKS], 1),
        "wz": wzT.reshape(P, KH, NCH, -1).transpose(0, 2, 1, 3).reshape(P, -1),
        "wo": rows(a["L0_attn_out_proj_w"].T, CT).reshape(P, -1),
        "wgu": gu.transpose(1, 4, 3, 0, 2).reshape((FT + MT) * P, -1),
        "wd": np.concatenate([down_rows, a["L0_attn_mlp_out_w"].T]),
        "pack_a": np.concatenate([small[n].reshape(P, c) for n, c in PACK_A], 1),
        "pack_b": np.concatenate([small[n].reshape(P, c) for n, c in PACK_B], 1),
        "eye": eye,
        "sel_head": sel_head,
        "sel_exp": sel_exp,
    }
    nc = bacc.Bacc("TRN2", target_bir_lowering=False, num_devices=1)
    args, feed = [], {}
    for name, arr in arrays.items():
        arr = np.ascontiguousarray(arr)
        feed[f"in_{name}_dram"] = arr
        args.append(nc.dram_tensor(f"in_{name}_dram", arr.shape, mybir.dt.from_np(arr.dtype), kind="ExternalInput").ap())
    out = nc.dram_tensor("out_0_dram", (P, TT, HID), F32, kind="ExternalOutput").ap()
    build(nc, *args, out)
    r = run_bass_kernel_spmd(nc, [feed], core_ids=[0])
    got = r.results[0]["out_0_dram"]
    return np.ascontiguousarray(got.transpose(1, 0, 2).reshape(BATCH, SEQ, HID))
```

```python
from contextlib import ExitStack

import concourse.bass as bass
from concourse import mybir
from concourse.alu_op_type import AluOpType as ALU

ACT = mybir.ActivationFunctionType
F32 = mybir.dt.float32
F32R = mybir.dt.float32r
BF16 = mybir.dt.bfloat16
U32 = mybir.dt.uint32
AX_X = mybir.AxisListType.X

P = 128
BATCH, SEQ, HID = 4, 256, 256
TOK = BATCH * SEQ
TT = TOK // P
KH = HID // P
HEADS, HD, NST, TAPS = 32, 64, 64, 4
DIN = HEADS * HD
XCH = DIN + 2 * NST
CT = DIN // P
PAIRS = CT // 2
UNITS = PAIRS + 1
INTER = 1024
NE, FF, SFF = 8, 176, 352
FT = -(-(NE * FF + SFF) // P)
MT = INTER // P
FFP = FT * P
ROUTED_SCALE = 2.5
EPS = 1e-5
SPLIT = 3
NR = NE + 1
HALF = TOK // 2
CREDIT = 4
CONV = PAIRS * 4 + 2

RING = (0, 1, 2, 5)
BCA, BCB, YB, OPB = 3, 4, 6, 7
GATE, UP, COMB, ACC = 0, 2, 3, 4

WX_CHUNKS = [(0, 512), (512, 512), (1024, 512), (1536, XCH - 1536)]
NCH = 4
RAW_PLACE = (0, 1, 2, 3) + (0, 2, 3, 1) * 2
SLOT = KH * (XCH - 1536)

SETUP = [(("xr", 0), 6), (("xr", 1), 3), (("xr", 2), 4), (("xr", 3), 7), (("dt", 0), 6), (("dt", 1), 3),
         (("dtt", 0), 7)]


ROUTE_STEP, COMB_STEP = 6, 8
XN_AT = {3: (0, 1), 5: (2, 3)}
ORDER = (0, 1, 2, 3, PAIRS, 4, 5, 6, 7)


def place(unit):
    return ORDER.index(unit)


def units_at(i, last):
    if i < 2:
        return [PAIRS - 2 + i]
    if last or i >= PAIRS:
        return []
    return ([PAIRS] if i == PAIRS - 2 else []) + [i - 2]


def convolved_at(i, last):
    return [PAIRS - 3] if i == 0 else units_at(i - 1, last)


def in_step(i, lag, prev):
    h = i - lag
    return h if (0 <= h < PAIRS or (h < 0 and prev)) else None


def first_projection():
    return [(("xp", u), RING[(n + 1) % 4]) for n, u in enumerate(ORDER[:place(PAIRS - 3) + 1])]


def sequence_items(prev, last):
    keys, ys = [], []
    for i in range(PAIRS + 3 if last else PAIRS):
        if i < PAIRS:
            keys += [("xtr", i), ("z", i)]
        if i == 0:
            keys.append(("s", 0))
        if i == 2:
            keys += [("ssq", -1) if prev else None, None]
        keys += [("xp", u) for u in units_at(i, last)]
        if last:
            keys += [("xn", q) for q in XN_AT.get(i, ())]
        if last and i == ROUTE_STEP:
            keys += [("gate", 0), ("gate", 1)]
        if last and i == ROUTE_STEP + 1:
            keys.append(("prob", 0))
        if last and i == COMB_STEP:
            keys += [("comb", 0), ("comb", 1)]
        h = in_step(i, 1, prev)
        if h is not None:
            ys.append((("y", h), YB))
    items = [(k, RING[n % 4]) for n, k in enumerate(keys) if k]
    for i in range(PAIRS):
        items += [(("bca", i), BCA), (("bcb", i), BCB)]
    if last:
        items.append((("ssq", 0), BCA))
    return items + ys + ([(("op", -1), OPB)] if prev else []) + ([(("op", 0), OPB)] if last else [])


MOE_ITEMS = [(("gate", u), GATE + u) for u in range(2)] + [(("up", u), UP) for u in range(2)] + [
    (("comb", u), COMB) for u in range(2)]
MLP_ITEMS = MOE_ITEMS[:4]
EARLY = (("gate", 0), ("gate", 1), ("up", 0))


class Banks:

    def __init__(self):
        self.base = [0] * 8

    def phase(self, items, times=1, carried=None):
        base, seen, table = list(self.base), [0] * 8, {}
        for key, bank in items:
            table[key] = (bank, base[bank], seen[bank])
            seen[bank] += 1
        self.base = [b + times * n for b, n in zip(self.base, seen)]
        if carried is not None:
            key, bank = carried
            table[key] = (bank, base[bank], -1)
        return {k: (bank, b0, seen[bank], n) for k, (bank, b0, n) in table.items()}


BANKS = Banks()
IN_SETUP = BANKS.phase(SETUP)
IN_FIRST = BANKS.phase(first_projection())
CARRIED = (("carried", PAIRS - 3), RING[3])
assert all([k for k, b in items if b == RING[3]][-1] == ("xp", PAIRS - 3)
           for items in (first_projection(), sequence_items(False, False), sequence_items(True, False)))
IN_BEGIN = BANKS.phase(sequence_items(False, False), 1, CARRIED)
IN_SEQ = BANKS.phase(sequence_items(True, False), BATCH - 2, CARRIED)
IN_LAST = BANKS.phase(sequence_items(True, True), 1, CARRIED)
IN_MOE = BANKS.phase(MOE_ITEMS, FT)
IN_MOE_ACC = BANKS.phase([(("acc", n), ACC + n) for n in range(4)])
IN_X1T = BANKS.phase([(("x1t", n), n) for n in range(4)])
IN_MLP = BANKS.phase(MLP_ITEMS, MT)
IN_MLP_ACC = BANKS.phase([(("acc", n), ACC + n) for n in range(4)])


def fills(table, key, it=0):
    bank, base, per, n = table[key]
    return bank, it * per + (base + n)


LN_GROUPS = ((0, 2), (2, TT))
P_RSTD = 8
V_CENTRED = [1 + 2 + 2, 1 + 4 + TT]
V_XR = [V_CENTRED[1] + 2, V_CENTRED[1] + TT]
V_WDT = V_XR[1] + 1
V_NEG = V_WDT + BATCH + 1
V_U = V_NEG + 1
V_DT = V_U + 7
V_RESET = V_DT + 1
V_PART = V_RESET + 1
V_DECAY = V_PART + BATCH + 1 + 2 * BATCH
A_SQUARES = [2, TT]
A_NEGA = TT + 2
A_EXP = A_NEGA + 1
A_LN = A_EXP + 1
A_DEC = A_LN + 1
A_HI = A_DEC + 1
A_MID = A_HI + 1
A_XN = A_MID + TT

PACK_A = (("ident", P), ("ln1", KH), ("conv_w", (CT + 1) * TAPS), ("conv_b", CT + 1))
PACK_B = (("wdt", KH * P), ("wgate", KH * NE), ("iota", TT * NE), ("d_col", CT), ("mnorm", CT), ("ln2", KH),
          ("dt_bias", 1), ("a_log", 1))
R_COMB = 2 + 2 * TT + 4 + 7
R_PART = R_COMB + 1
R_SPLIT = R_PART + 1
RA_HI, RA_MID = 1, 3

def build(nc, x, wx, wz, wo, wgu, wd, pack_a_in, pack_b_in, eye_in, sel_head_in, sel_exp_in, out):
    with ExitStack() as ctx:
        def sb(name, shape, dt=F32):
            return ctx.enter_context(nc.sbuf_tensor(name, shape, dt))

        def sem(name):
            return ctx.enter_context(nc.semaphore(name))

        wx_r = sb("wx_r", [P, 2, KH * XCH], F32R)
        wz_r = sb("wz_r", [P, 2, KH * DIN], F32R)
        wo_r = sb("wo_r", [P, 2, CT * HID], F32R)
        xrT = sb("xrT", [P, 2, KH, TOK], F32R)
        g_r = sb("g_r", [P, 2, 2, 512], F32R)
        wdt_r = sb("wdt_r", [P, 2, KH, P], F32R)
        
        wx_v = wx_r[:, :, :].rearrange("p s (k n) -> p s k n", k=KH)
        wz_v = wz_r[:, :, :].rearrange("p s (k n) -> p s k n", k=KH)
        wo_v = wo_r[:, :, :].rearrange("p s (j n) -> p s j n", j=CT)
        flat_x = wx_r[:, :, :].rearrange("p s n -> p (s n)")
        flat_z = wz_r[:, :, :].rearrange("p s n -> p (s n)")
        xnT = flat_x[:, 0:2 * KH * TOK].rearrange("p (s k t) -> p s k t", s=2, k=KH)
        x1T = flat_x[:, 2 * KH * TOK:4 * KH * TOK].rearrange("p (s k t) -> p s k t", s=2, k=KH)
        wgate_r = flat_x[:, 4 * KH * TOK:4 * KH * TOK + 2 * KH * P].rearrange("p (s k n) -> p s k n", s=2, k=KH)
        hid = flat_z[:, 0:4096].rearrange("p (r s t) -> p r s t", r=2, s=2)
        wgu_r = flat_z[:, 4096:6144].rearrange("p (r s k g n) -> p r s k g n", r=2, s=2, k=KH, g=2)
        wd_r = flat_z[:, 6144:7168].rearrange("p (r s n) -> p r s n", r=2, s=2)
        pack_a = sb("pack_a", [P, sum(n for _, n in PACK_A)])
        pack_b = sb("pack_b", [P, sum(n for _, n in PACK_B)])
        small = {}
        for whole, parts in ((pack_a, PACK_A), (pack_b, PACK_B)):
            col = 0
            for name, n in parts:
                small[name] = whole[:, col:col + n]
                col += n
        ident, ln1_sb, cb = small["ident"], small["ln1"], small["conv_b"]
        cw = small["conv_w"].rearrange("p (j s) -> p j s", s=TAPS)
        wdt_sb = small["wdt"].rearrange("p (k n) -> p k n", k=KH)
        wgate_sb = small["wgate"].rearrange("p (k n) -> p k n", k=KH)
        iota = small["iota"].rearrange("p (t e) -> p t e", t=TT)
        dcol, mn, ln2_sb = small["d_col"], small["mnorm"], small["ln2"]
        dt_bias, neg_a = small["dt_bias"], small["a_log"]
        eye = sb("eye", [P, 2 * SEQ])
        sel_head = sb("sel_head", [SPLIT * HEADS, HEADS], BF16)
        ones = sb("ones", [P, 1])
        power = sb("power", [P, TT])
        st = sb("st", [P, 6, TT])
        xn_all = sb("xn_all", [P, TT, HID])
        dt_tok = sb("dt_tok", [P, 2, BATCH * HEADS])
        dt_seq = sb("dt_seq", [P, 2, HEADS])
        decay0 = sb("decay0", [SPLIT * HEADS, TOK], BF16)
        comb_split = sb("comb_split", [SPLIT * 32, TOK], BF16)
        rk = sb("rk", [P, 672])
        xsT = sb("xsT", [P, CT * SEQ])
        xsT_v = xsT[:, :].rearrange("p (j t) -> p j t", j=CT)
        bT = sb("bT", [NST, SEQ])
        cT = sb("cT", [NST, SEQ])
        acc = sb("acc", [P, 2, 2, SEQ])
        acc_bc = sb("acc_bc", [P, 1, SEQ])
        gsq = sb("gsq", [P, 512])
        s_sb = sb("s_sb", [P, SEQ + P])
        var_g = sb("var_g", [P, 2])
        rstd_g = sb("rstd_g", [P, 2])
        arena = sb("arena", [P, 8192])
        m0 = arena[:, 0:2048].rearrange("p (r h t) -> p r h t", r=2, h=4)
        m1 = arena[:, 2048:3072].rearrange("p (r h t) -> p r h t", r=2, h=4)
        sq = arena[:, 4096:5120].rearrange("p (r n) -> p r n", r=2)
        xdt = arena[:, 7168:8192].rearrange("p (r c n) -> p r c n", r=2, c=2)
        sz = arena[:, 5120:6144].rearrange("p (r n) -> p r n", r=2)
        y_sb = arena[:, 6144:7168].rearrange("p (r n) -> p r n", r=2)
        gm = arena[:, 0:2048].rearrange("p (q n) -> p q n", q=TT)
        xx = arena[:, 2048:4096].rearrange("p (q n) -> p q n", q=TT)
        x1r = arena[:, 4096:6144].rearrange("p (q n) -> p q n", q=TT)
        hraw = arena[:, 6144:7168].rearrange("p (r n) -> p r n", r=2)
        sg = arena[:, 7168:8192].rearrange("p (r n) -> p r n", r=2)
        ssq_x1 = sb("ssq_x1", [P, TT])
        var_x1 = sb("var_x1", [P, TT])
        rstd_x1 = sb("rstd_x1", [P, TT])
        raw = [arena[:, SLOT * n:SLOT * n + SLOT] for n in range(4)]
        v, q_, neg, e, u, lnu, d, c_, f, dtT, dec, part = (
            arena[:, 4 * SLOT + SEQ * n:4 * SLOT + SEQ * (n + 1)] for n in range(12))
        hi, mid, lo = (w.bitcast(BF16)[:, 0:SEQ] for w in (v, neg, e))
        xr_first = xsT[:, 3584:4096].rearrange("p (t n) -> p t n", t=2)
        xr_rest = xsT[:, 2048:3584].rearrange("p (t n) -> p t n", t=6)

        def xr_tile(t):
            return xr_first[:, t, :] if t < 2 else xr_rest[:, t - 2, :]

        junk = xsT[:, 0:2048].rearrange("p (t n) -> p t n", t=TT)
        wgate_all = wgate_sb.unsqueeze(2).to_broadcast([P, KH, P // NE, NE])
        _, score, top, mask0, mask1, wsc, topf = (rk[:, 64 * n:64 * n + 64].rearrange("p (t e) -> p t e", t=TT)
                                                     for n in range(7))
        topi = rk[:, 448:512].bitcast(U32).rearrange("p (t e) -> p t e", t=TT)
        combx = rk[:, 512:512 + TT * NR].rearrange("p (t e) -> p t e", t=TT)
        wsum = rk[:, 584:592]
        wnorm = rk[:, 592:600]
        combT = xsT[0:32, 0:1024]
        probT = xsT[0:NE, 0:1024]
        cpart = acc[0:32, :, :, :].rearrange("p a b c -> p (a b c)")
        cmid = xsT[0:32, 1024:1536].bitcast(BF16)
        raw_gu = xsT[:, 1536:2560].rearrange("p (r n) -> p r n", r=2)
        raw_d = xsT[:, 2560:3072].rearrange("p (r n) -> p r n", r=2)
        sel_exp = xsT[0:SPLIT * 32, 3072:3072 + FFP // 2].bitcast(BF16)

        bank = [ctx.enter_context(nc.psum_tensor(f"bank{n}", [P, 512], F32)) for n in range(8)]
        bank_full = [sem(f"bank_full{n}") for n in range(8)]
        bank_free = [sem(f"bank_free{n}") for n in range(8)]

        loaded_x = [sem(f"loaded_x{n}") for n in range(2)]
        loaded_small = [sem(f"loaded_small{n}") for n in range(2)]
        loaded_raw = [sem(f"loaded_raw{n}") for n in range(4)]
        loaded_xq = [sem(f"loaded_xq{n}") for n in range(2)]
        loaded_gu = [sem(f"loaded_gu{n}") for n in range(2)]
        loaded_d = [sem(f"loaded_d{n}") for n in range(2)]
        loaded_sel, loaded_xx = sem("loaded_sel"), sem("loaded_xx")
        v_step, a_step, p_step = sem("v_step"), sem("a_step"), sem("p_step")
        r_step, ra_step = sem("r_step"), sem("ra_step")
        names = ("chunk_hi", "small_hi", "wx_split", "wx_last_split", "wzo_split", "wo_scaled", "xr_hi",
                 "dt_ready", "xdt_ready", "m0_ready", "m_rest_ready", "g_ready", "g_hi", "g_split",
                 "sq_ready", "gsq_ready", "tap_ready", "conv_step", "xs_ready", "op_done", "rstd_ready",
                 "xq_normed", "xn_hi", "wgate_split",
                 "gu_hi", "gu_split", "d_hi", "d_split", "h_ready", "h_hi", "h_split", "down_done",
                 "t_step", "ssq_ready", "var1_ready", "rstd1_ready", "x1r_ready", "x1t_hi", "xx_step",
                 "out_step", "out_ready")
        S = {n: sem(n) for n in names}
        stored = sem("stored")
        block = ctx.enter_context(nc.Block())

        def await_full(eng, table, key, it=0):
            b, n = fills(table, key, it)
            eng.wait_ge(bank_full[b], n + 1)
            return bank[b]

        def await_free(eng, table, key, it=0):
            b, n = fills(table, key, it)
            if not (isinstance(n, int) and n == 0):
                eng.wait_ge(bank_free[b], n)
            return bank[b]

        def await_read(eng, table, key, it=0):
            b, n = fills(table, key, it)
            eng.wait_ge(bank_free[b], n + 1)

        def is_full(ins, table, key):
            ins.then_inc(bank_full[table[key][0]], 1)

        def is_free(ins, table, key):
            ins.then_inc(bank_free[table[key][0]], 1)

        def reached(eng, name, n):
            eng.wait_ge(S[name], n + CREDIT)

        def sequences(eng):
            yield 0, IN_BEGIN, 0, False, False
            with eng.Fori(0, BATCH - 2) as it:
                yield it + 1, IN_SEQ, it, True, False
            yield BATCH - 1, IN_LAST, 0, True, True

        def steps_of(last):
            return range(PAIRS + 3 if last else PAIRS)

        def slot_free(eng, table, i, it):
            if ("y", i - 1) in table:
                b6, f6 = fills(table, ("y", i - 1), it)
                eng.wait_ge(bank_full[b6], f6)

        def sums(b, h):
            return b * (PAIRS - 1) + (h if h >= 0 else h + 1)

        def conv_place(unit):
            return acc[:, unit % 2, :, :] if unit < PAIRS else acc_bc

        def tiles(eng, count):
            yield 0, 0, True, False
            yield 1, 1, False, False
            with eng.Fori(1, count // 2 - 1) as n:
                yield n * 2, 0, False, False
                yield n * 2 + 1, 1, False, False
            yield count - 2, 0, False, False
            yield count - 1, 1, False, True

        def at(b, n, size):
            return slice(b * n, b * n + size) if isinstance(b, int) else bass.ds(b * n, size)

        def product(pe, dst, lhs, rhs, first, last):
            for n, (a, c) in enumerate(((0, 0), (0, 1), (1, 0))):
                ins = pe.matmul(dst, lhs(a), rhs(c), start=first and n == 0, stop=last and n == 2)
            return ins

        @block.sync
        def _(sp):
            sp.dma_start(xn_all[:, 0:2, :], x[:, 0:2, :]).then_inc(loaded_x[0], 16)

            def chunk(n):
                w, c = divmod(n, NCH)
                if w == 0:
                    at0, size = WX_CHUNKS[c]
                    src = wx[:, KH * at0:KH * (at0 + size)]
                else:
                    src = (wz, wo)[w - 1][:, 1024 * c:1024 * c + 1024]
                sp.dma_start(raw[RAW_PLACE[n]][:, 0:src.shape[1]], src).then_inc(loaded_raw[RAW_PLACE[n]], 16)

            sp.dma_start(xn_all[:, 2:TT, :], x[:, 2:TT, :]).then_inc(loaded_x[1], 16)
            sp.dma_start(pack_a[:], pack_a_in).then_inc(loaded_small[0], 16)
            chunk(0)
            chunk(1)
            for n in range(2, 4):
                chunk(n)
            for dst, src in ((pack_b, pack_b_in), (eye, eye_in), (sel_head, sel_head_in)):
                sp.dma_start(dst[:], src).then_inc(loaded_small[1], 16)
            for n in range(4, 3 * NCH):
                if n < 2 * NCH:
                    c = RAW_PLACE[n]
                    reached(sp, "wx_split" if c < 3 else "wx_last_split", c + 1 if c < 3 else 1)
                else:
                    reached(sp, "wzo_split", n - 2 * NCH + 1)
                chunk(n)
            for q in range(BATCH):
                if q < 2:
                    reached(sp, "xs_ready", BATCH * UNITS)
                else:
                    await_read(sp, IN_LAST, ("xn", q - 2))
                sp.dma_start(acc[:, q % 2, :, :], x[:, 2 * q:2 * q + 2, :]).then_inc(loaded_xq[q % 2], 16)

            def weights(m, r):
                reached(sp, "gu_split", m - 1)
                sp.dma_start(raw_gu[:, r, :], wgu[at(m, P, P), :]).then_inc(loaded_gu[r], 16)
                reached(sp, "d_split", m - 1)
                sp.dma_start(raw_d[:, r, :], wd[at(m, P, P), :]).then_inc(loaded_d[r], 16)

            b6, n6 = fills(IN_LAST, ("y", 5))
            sp.wait_ge(bank_free[b6], n6 + 1)
            weights(0, 0)
            weights(1, 1)
            b6, n6 = fills(IN_LAST, ("y", 7))
            sp.wait_ge(bank_free[b6], n6 + 1)
            sp.dma_start(sel_exp, sel_exp_in).then_inc(loaded_sel, 16)
            await_read(sp, IN_LAST, ("op", 0))
            sp.dma_start(xx, x).then_inc(loaded_xx, 16)
            with sp.Fori(1, (FT + MT) // 2) as n:
                weights(n * 2, 0)
                weights(n * 2 + 1, 1)
            for n in range(4):
                reached(sp, "out_ready", n + 1)
                sp.dma_start(out[:, 2 * n:2 * n + 2, :], xx[:, 2 * n:2 * n + 2, :]).then_inc(stored, 16)
            sp.wait_ge(stored, 16 * 4)

        SMALL = (16, 3 * 16)

        def split_wx(eng, c, name):
            a, size = WX_CHUNKS[c]
            reached(eng, "chunk_hi", c + 1)
            ins = eng.tensor_tensor(wx_v[:, 1, :, a:a + size], raw[c][:, 0:KH * size].rearrange("p (k n) -> p k n", k=KH),
                                    wx_v[:, 0, :, a:a + size].bitcast(F32), ALU.subtract)
            ins.then_inc(S[name], 1)

        def split_gu(eng, n, r):
            reached(eng, "gu_hi", n + 1)
            hi, lo = (wgu_r[:, r, s].rearrange("p k g n -> p (k g n)") for s in (0, 1))
            eng.tensor_tensor(lo, raw_gu[:, r, :], hi.bitcast(F32), ALU.subtract).then_inc(S["gu_split"], 1)

        def split_chunk(eng, n):
            w, c = divmod(n, NCH)
            src = raw[RAW_PLACE[n]][:, 0:1024]
            reached(eng, "chunk_hi", n + 1)
            if w == 1:
                dst, hi = (wz_v[:, s, :, 512 * c:512 * c + 512] for s in (1, 0))
                src = src.rearrange("p (k n) -> p k n", k=KH)
            else:
                dst, hi = (wo_r[:, s, 1024 * c:1024 * c + 1024] for s in (1, 0))
            eng.tensor_tensor(dst, src, hi.bitcast(F32), ALU.subtract).then_inc(S["wzo_split"], 1)

        def add_squares(eng, b, h):
            reached(eng, "sq_ready", b * PAIRS + h + 1)
            if h != 1:
                reached(eng, "gsq_ready", sums(b, h) - 1)
            eng.tensor_tensor(gsq[:], gsq[:], sq[:, h % 2, :], ALU.add).then_inc(S["gsq_ready"], 1)

        @block.vector
        def _(dve):
            steps = [0]

            def step(ins):
                steps[0] += 1
                ins.then_inc(v_step, 1)
                dve.wait_ge(v_step, steps[0])

            def many(made):
                for ins in made:
                    steps[0] += 1
                    ins.then_inc(v_step, 1)
                dve.wait_ge(v_step, steps[0])

            for n in ("wx_split", "wgate_split", "m0_ready", "conv_step", "xq_normed", "h_ready", "h_split",
                      "t_step", "var1_ready", "x1r_ready", "out_step", "out_ready"):
                dve.sem_inc(S[n], CREDIT)
            dve.memset(power[:], -0.5)
            dve.memset(ones[:], 1.0)
            step(dve.memset(comb_split[:], 0.0))

            def centre(g):
                a, b = LN_GROUPS[g]
                dve.wait_ge(loaded_x[g], 16)
                step(dve.reduce_sum(st[:, 0, a:b], xn_all[:, a:b, :], AX_X))
                step(dve.tensor_scalar(st[:, 1, a:b], st[:, 0, a:b], 1.0 / HID, None, ALU.mult))
                many([dve.tensor_scalar(xn_all[:, t, :], xn_all[:, t, :], st[:, 1, t:t + 1], None, ALU.subtract)
                      for t in range(a, b)])
                assert steps[0] == V_CENTRED[g], steps

            def norm_xr(g):
                a, b = LN_GROUPS[g]
                dve.wait_ge(p_step, P_RSTD * (g + 1))
                many([dve.tensor_scalar(xr_tile(t), xn_all[:, t, :], st[:, 5, t:t + 1], None, ALU.mult)
                      for t in range(a, b)])
                assert steps[0] == V_XR[g], steps

            def split_xr(q):
                pb = await_full(dve, IN_SETUP, ("xr", q))
                reached(dve, "xr_hi", q + 1)
                for k in range(KH):
                    toks = slice(SEQ * q, SEQ * q + SEQ)
                    ins = dve.scalar_tensor_tensor(xrT[:, 1, k, toks], pb[:, 256 * k:256 * k + 256], ln1_sb[:, k:k + 1],
                                                   xrT[:, 0, k, toks].bitcast(F32), ALU.mult, ALU.subtract)
                is_free(ins, IN_SETUP, ("xr", q))

            def convolve(unit, table, it, turn, name="xp"):
                key = (name, unit)
                pb = await_full(dve, table, key, it)
                n = place(unit)
                reached(dve, "tap_ready", turn * UNITS + n + 1)
                n_tiles = 2 if unit < PAIRS else 1
                at0 = turn * CONV + n * 4 - (2 if n > place(PAIRS) else 0)
                for s in range(1, TAPS):
                    for jj in range(n_tiles):
                        if s > 1:
                            reached(dve, "conv_step", at0 + (s - 2) * n_tiles + jj + 1)
                        a = conv_place(unit)[:, jj, s:SEQ]
                        ins = dve.scalar_tensor_tensor(a, pb[:, jj * SEQ:jj * SEQ + SEQ - s],
                                                       cw[:, 2 * unit + jj, TAPS - 1 - s:TAPS - s], a, ALU.mult, ALU.add)
                        if s < TAPS - 1:
                            ins.then_inc(S["conv_step"], 1)
                is_free(ins, table, key)

            centre(0)
            centre(1)
            norm_xr(0)
            split_wx(dve, 0, "wx_split")
            split_xr(0)
            split_wx(dve, 1, "wx_split")
            split_wx(dve, 2, "wx_split")
            convolve(ORDER[0], IN_FIRST, 0, 0)
            convolve(ORDER[1], IN_FIRST, 0, 0)
            norm_xr(1)
            convolve(ORDER[2], IN_FIRST, 0, 0)
            for q in range(1, BATCH):
                split_xr(q)
            reached(dve, "small_hi", 1)
            many([dve.tensor_tensor(wdt_r[:, 1], wdt_sb, wdt_r[:, 0].bitcast(F32), ALU.subtract)])
            assert steps[0] == V_WDT, (steps, V_WDT)
            convolve(ORDER[3], IN_FIRST, 0, 0)
            made = []
            for b in range(BATCH):
                pb = await_full(dve, IN_SETUP, ("dt", b // 2))
                rows = slice(HEADS * b, HEADS * b + HEADS)
                made.append(dve.tensor_scalar(v[rows, :], pb[rows, (b % 2) * SEQ:(b % 2) * SEQ + SEQ], dt_bias[rows, :], None,
                                              ALU.add))
            many(made)
            for n in range(2):
                dve.sem_inc(bank_free[IN_SETUP[("dt", n)][0]], 1)
            step(dve.scalar_tensor_tensor(neg, v, -1.0, v, ALU.mult, ALU.min))
            assert steps[0] == V_NEG
            dve.wait_ge(a_step, A_EXP)
            step(dve.tensor_scalar(u, e, 1.0, None, ALU.add))
            assert steps[0] == V_U
            many([dve.tensor_scalar(d, u, -1.0, None, ALU.add), dve.tensor_scalar(f, e, -1.0, 1.0, ALU.mult, ALU.add),
                  dve.tensor_scalar(q_, v, 0.0, None, ALU.max)])
            step(dve.tensor_tensor(c_, e, d, ALU.subtract))
            step(dve.tensor_tensor(c_, c_, f, ALU.mult))
            dve.wait_ge(a_step, A_LN)
            step(dve.tensor_tensor(c_, c_, lnu, ALU.add))
            step(dve.tensor_tensor(dtT, q_, c_, ALU.add))
            assert steps[0] == V_DT
            convolve(ORDER[4], IN_FIRST, 0, 0)
            dve.wait_ge(a_step, A_DEC)
            step(dve.memset(dec[:, 0:1], 0.0))
            assert steps[0] == V_RESET
            dve.wait_ge(a_step, A_HI)
            step(dve.tensor_tensor(part, dec, hi, ALU.subtract))
            assert steps[0] == V_PART

            def by_head(s, whole):
                return [dve.tensor_copy(decay0[HEADS * s:HEADS * s + HEADS, SEQ * b:SEQ * b + SEQ],
                                        whole[HEADS * b:HEADS * b + HEADS, :]) for b in range(BATCH)]

            many(by_head(0, hi))
            dve.wait_ge(a_step, A_MID)
            step(dve.tensor_tensor(lo, part, mid, ALU.subtract))
            many(by_head(1, mid) + by_head(2, lo))
            assert steps[0] == V_DECAY, (steps, V_DECAY)

            convolve(ORDER[5], IN_FIRST, 0, 0)
            convolve(PAIRS - 3, IN_BEGIN, 0, 0, "carried")
            split_chunk(dve, 11)

            r_steps = [0]

            def route(made):
                for ins in made:
                    r_steps[0] += 1
                    ins.then_inc(r_step, 1)
                dve.wait_ge(r_step, r_steps[0])

            def variance(key, table, it):
                pb = await_full(dve, table, key, it)
                ins = dve.tensor_scalar(var_g[:], pb[:, 0:2], 1.0 / DIN, EPS, ALU.mult, ALU.add)
                is_free(ins, table, key)

            def residual(key, seq, table, it):
                pb = await_full(dve, table, key, it)
                reached(dve, "rstd_ready", seq + 1)
                dve.wait_ge(a_step, A_XN)
                for c in range(2):
                    xc = xn_all[:, at(seq, 2, 2), :][:, c, :]
                    ins = dve.scalar_tensor_tensor(xc, pb[:, c * HID:c * HID + HID], rstd_g[:, c:c + 1], xc,
                                                   ALU.mult, ALU.add)
                is_free(ins, table, key)

            for b, table, it, prev, last in sequences(dve):
                for i in steps_of(last):
                    h = in_step(i, 3, prev)
                    if h is not None and h % 2 == 1:
                        add_squares(dve, b, h)
                    for unit in convolved_at(i, last) if i > 0 or prev else ():
                        convolve(unit, table, it, b if i < 3 else b + 1, "xp" if i > 0 else "carried")
                    if i == 0 and not prev:
                        reached(dve, "wzo_split", 2 * NCH)
                    if i < PAIRS:
                        r = i % 2
                        slot_free(dve, table, i, it)
                        for n, name in enumerate(("bca", "bcb")):
                            pa = await_full(dve, table, (name, i), it)
                            dst = m0[:, r, 2 * n:2 * n + 2, :].rearrange("p h t -> p (h t)")
                            dve.tensor_tensor_scan(dst, pa[:, :], eye[:], 0.0, ALU.mult, ALU.add)
                            for hh in range(2):
                                ins = dve.tensor_tensor_scan(m1[:, r, 2 * n + hh, :], pa[:, hh * SEQ + P:hh * SEQ + SEQ],
                                                             ident, 0.0, ALU.mult, ALU.add)
                            is_free(ins, table, (name, i))
                        if i == 0:
                            await_read(dve, table, ("s", 0), it)
                        await_read(dve, table, ("bca", i), it)
                        mm = m0[:, r, 0:2, :]
                        dve.tensor_tensor(mm, mm, s_sb[:, 0:SEQ].unsqueeze(1).to_broadcast([P, 2, SEQ]), ALU.mult)\
                           .then_inc(S["m0_ready"], 1)
                    if last:
                        for q in XN_AT.get(i, ()):
                            dve.wait_ge(loaded_xq[q % 2], 16 * (q // 2 + 1))
                            for t in range(2):
                                tt = 2 * q + t
                                ins = dve.tensor_scalar(acc[:, q % 2, t, :], acc[:, q % 2, t, :], st[:, 1, tt:tt + 1],
                                                        st[:, 4, tt:tt + 1], ALU.subtract, ALU.mult)
                            ins.then_inc(S["xq_normed"], 1)
                    if i == 3 and prev:
                        residual(("op", -1), b - 1, table, it)
                    h = in_step(i, 1, prev)
                    if h is not None:
                        pb = await_full(dve, table, ("y", h), it)
                        reached(dve, "g_hi", b * PAIRS + h - 1)
                        reached(dve, "g_split", b * PAIRS + h - 1)
                        for jj in range(2):
                            j = 2 * (h % PAIRS) + jj
                            ins = dve.scalar_tensor_tensor(y_sb[:, h % 2, jj * SEQ:jj * SEQ + SEQ], xsT_v[:, j, :],
                                                           dcol[:, j:j + 1], pb[:, jj * SEQ:jj * SEQ + SEQ],
                                                           ALU.mult, ALU.add)
                        is_free(ins, table, ("y", h))
                    if i == 2 and prev:
                        variance(("ssq", -1), table, it)
                    if last and i == 4:
                        reached(dve, "small_hi", 2)
                        dve.tensor_tensor(wgate_r[:, 1].rearrange("p k (c e) -> p k c e", e=NE), wgate_all,
                                          wgate_r[:, 0].bitcast(F32).rearrange("p k (c e) -> p k c e", e=NE),
                                          ALU.subtract).then_inc(S["wgate_split"], 1)
                    if last:
                        for q in XN_AT.get(i, ()):
                            pb = await_full(dve, table, ("xn", q), it)
                            reached(dve, "xn_hi", q + 1)
                            toks = slice(SEQ * q, SEQ * q + SEQ)
                            ins = dve.tensor_tensor(xnT[:, 1, :, toks], pb[:, :].rearrange("p (k t) -> p k t", k=KH),
                                                    xnT[:, 0, :, toks].bitcast(F32), ALU.subtract)
                            is_free(ins, table, ("xn", q))
                    if last and i == ROUTE_STEP + 1:
                        split_gu(dve, 0, 0)
                        pb = await_full(dve, table, ("prob", 0), it)
                        route([dve.tensor_scalar(score, pb[:, 0:TT * NE].rearrange("p (t e) -> p t e", t=TT), 1.0, None, ALU.add)])
                        dve.sem_inc(bank_free[table[("prob", 0)][0]], 1)
                        route([dve.reciprocal(score, score)])
                        route([dve.max(top[:, t, :], score[:, t, :]) for t in range(TT)])
                        route([dve.max_index(topi[:, t, :], top[:, t, :], score[:, t, :]) for t in range(TT)])
                        route([dve.tensor_copy(topf, topi), dve.memset(combx, 1.0)])
                        route([dve.tensor_tensor(mask0, iota, topf[:, :, 0:1].to_broadcast([P, TT, NE]), ALU.is_equal),
                               dve.tensor_tensor(mask1, iota, topf[:, :, 1:2].to_broadcast([P, TT, NE]), ALU.is_equal)])
                        route([dve.tensor_tensor(mask0, mask0, mask1, ALU.add)])
                        route([dve.tensor_tensor(wsc, mask0, score, ALU.mult)])
                        route([dve.reduce_sum(wsum, wsc, AX_X)])
                        route([dve.tensor_scalar(wsum, wsum, 1e-20, None, ALU.add)])
                        route([dve.reciprocal(wnorm, wsum)])
                        route([dve.tensor_tensor(wsc, wsc, wnorm.unsqueeze(2).to_broadcast([P, TT, NE]), ALU.mult)])
                        route([dve.tensor_scalar(combx[:, :, 0:NE], wsc, ROUTED_SCALE, None, ALU.mult)])
                        assert r_steps[0] == R_COMB, r_steps
                    if last and i == COMB_STEP + 1:
                        dve.wait_ge(ra_step, RA_HI)
                        route([dve.tensor_tensor(cpart[0:NR, :], combT[0:NR, :], comb_split[0:NR, :], ALU.subtract)])
                        assert r_steps[0] == R_PART
                        dve.wait_ge(ra_step, RA_MID)
                        route([dve.tensor_tensor(comb_split[64:64 + NR, :], cpart[0:NR, :], cmid[0:NR, 0:TOK], ALU.subtract)])
                        assert r_steps[0] == R_SPLIT
                    if i == PAIRS + 2:
                        variance(("ssq", 0), table, it)

            def split_hidden(n):
                reached(dve, "h_hi", n["count"])
                u, r = n["u"], n["slot"]
                dve.tensor_tensor(hid[:, r, 1, u * HALF:u * HALF + HALF], hraw[:, u, :],
                                  hid[:, r, 0, u * HALF:u * HALF + HALF].bitcast(F32), ALU.subtract).then_inc(S["h_split"], 1)

            def hidden(base, count, table, routed):
                for m, r, first, last in tiles(dve, count):
                    for u in range(2):
                        n = (m + base) * 2 + u
                        if not (first and u == 0):
                            split_hidden({"count": n, "u": 1 - u, "slot": r if u else 1 - r})
                        if routed and first and u == 0:
                            reached(dve, "g_split", BATCH * PAIRS)
                            dve.wait_ge(loaded_sel, 16)
                        pb = await_full(dve, table, ("up", u), m)
                        await_read(dve, table, ("gate", u), m)
                        reached(dve, "h_split", n - 1)
                        if routed and first and u == 1:
                            residual(("op", 0), BATCH - 1, IN_LAST, 0)
                        dst = hraw[:, u, :]
                        ins = dve.tensor_tensor(dst, sg[:, u, :], pb[:, :], ALU.mult)
                        is_free(ins, table, ("up", u))
                        if routed:
                            pc = await_full(dve, table, ("comb", u), m)
                            await_read(dve, table, ("up", u), m)
                            ins = dve.tensor_tensor(dst, dst, pc[:, :], ALU.mult)
                            is_free(ins, table, ("comb", u))
                    if routed and isinstance(m, int) and m == 1:
                        reached(dve, "ssq_ready", 1)
                        dve.tensor_scalar(var_x1[:], ssq_x1[:], 1.0 / HID, EPS, ALU.mult, ALU.add).then_inc(S["var1_ready"], 1)
                    if last:
                        split_hidden({"count": n + 1, "u": 1, "slot": r})
                    if routed and isinstance(m, int) and m == FT - 2:
                        reached(dve, "rstd1_ready", 1)
                        for q in range(TT):
                            ins = dve.tensor_scalar(x1r[:, q, :], xn_all[:, q, :], rstd_x1[:, q:q + 1], None, ALU.mult)
                        ins.then_inc(S["x1r_ready"], 1)

            hidden(0, FT, IN_MOE, True)
            for q in range(4):
                pb = await_full(dve, IN_X1T, ("x1t", q))
                reached(dve, "x1t_hi", q + 1)
                for k in range(KH):
                    toks = slice(SEQ * q, SEQ * q + SEQ)
                    ins = dve.scalar_tensor_tensor(x1T[:, 1, k, toks], pb[:, 256 * k:256 * k + 256], ln2_sb[:, k:k + 1],
                                                   x1T[:, 0, k, toks].bitcast(F32), ALU.mult, ALU.subtract)
                is_free(ins, IN_X1T, ("x1t", q))
            hidden(FT, MT, IN_MLP, False)
            for n in range(4):
                pb = await_full(dve, IN_MLP_ACC, ("acc", n))
                prod = x1r[:, 2 * n:2 * n + 2, :]
                ins = dve.tensor_tensor(prod, gm[:, 2 * n:2 * n + 2, :], pb[:, :].rearrange("p (q n) -> p q n", q=2), ALU.mult)
                ins.then_inc(S["out_step"], 1)
                if n == 0:
                    reached(dve, "xx_step", 2)
                reached(dve, "out_step", n + 1)
                dst = xx[:, 2 * n:2 * n + 2, :]
                dve.tensor_tensor(dst, dst, prod, ALU.add).then_inc(S["out_ready"], 1)

        @block.scalar
        def _(act):
            for n in ("chunk_hi", "dt_ready", "xdt_ready", "small_hi", "xr_hi", "g_hi", "sq_ready", "tap_ready", "xs_ready", "xn_hi", "gu_hi", "d_hi", "h_hi",
                      "ssq_ready", "x1t_hi"):
                act.sem_inc(S[n], CREDIT)

            def squares(g):
                act.wait_ge(v_step, V_CENTRED[g])
                for t in range(*LN_GROUPS[g]):
                    ins = act.activation(junk[:, t, :], xn_all[:, t, :], ACT.Square, accum_out=st[:, 2, t:t + 1])
                    ins.then_inc(a_step, 1)

            def hi_xr(q):
                pb = await_full(act, IN_SETUP, ("xr", q))
                for k in range(KH):
                    ins = act.activation(xrT[:, 0, k, SEQ * q:SEQ * q + SEQ], pb[:, 256 * k:256 * k + 256], ACT.Copy,
                                         scale=ln1_sb[:, k:k + 1])
                ins.then_inc(S["xr_hi"], 1)

            def hi_chunk(n):
                w, c = divmod(n, NCH)
                act.wait_ge(loaded_raw[RAW_PLACE[n]], 16 * (n // 4 + 1))
                if w == 0:
                    a, size = WX_CHUNKS[c]
                    ins = act.activation(wx_v[:, 0, :, a:a + size], raw[c][:, 0:KH * size].rearrange("p (k n) -> p k n", k=KH),
                                         ACT.Copy)
                elif w == 1:
                    ins = act.activation(wz_v[:, 0, :, 512 * c:512 * c + 512],
                                         raw[RAW_PLACE[n]][:, 0:1024].rearrange("p (k n) -> p k n", k=KH), ACT.Copy)
                else:
                    reached(act, "wo_scaled", c + 1)
                    ins = act.activation(wo_r[:, 0, 1024 * c:1024 * c + 1024], raw[RAW_PLACE[n]][:, 0:1024], ACT.Copy)
                ins.then_inc(S["chunk_hi"], 1)

            def first_tap(unit, table, it, turn, name="xp"):
                pb = await_full(act, table, (name, unit), it)
                if unit == PAIRS:
                    gone = place(PAIRS) + 1 - UNITS
                else:
                    gone = place(unit - 2) + 1 if unit > 1 else unit - 1
                if not (isinstance(turn, int) and turn == 0 and gone <= 0):
                    reached(act, "xs_ready", turn * UNITS + gone)
                for jj in range(2 if unit < PAIRS else 1):
                    ins = act.activation(conv_place(unit)[:, jj, :], pb[:, jj * SEQ:jj * SEQ + SEQ], ACT.Identity,
                                         bias=cb[:, 2 * unit + jj:2 * unit + jj + 1],
                                         scale=cw[:, 2 * unit + jj, TAPS - 1:TAPS])
                ins.then_inc(S["tap_ready"], 1)

            def silu_conv(unit, table, it, name="xp"):
                await_read(act, table, (name, unit), it)
                if unit < PAIRS:
                    ins = act.activation(xsT_v[:, 2 * unit:2 * unit + 2, :], conv_place(unit), ACT.Silu)
                else:
                    act.activation(bT[:], acc_bc[0:NST, 0, :], ACT.Silu)
                    ins = act.activation(cT[:], acc_bc[NST:P, 0, :], ACT.Silu)
                ins.then_inc(S["xs_ready"], 1)

            squares(0)
            hi_chunk(0)
            act.wait_ge(loaded_small[0], SMALL[0])
            hi_xr(0)
            hi_chunk(1)
            hi_chunk(2)
            squares(1)
            first_tap(ORDER[0], IN_FIRST, 0, 0)
            hi_chunk(3)
            first_tap(ORDER[1], IN_FIRST, 0, 0)
            hi_chunk(4)
            hi_chunk(5)
            act.wait_ge(a_step, A_SQUARES[1])
            silu_conv(ORDER[0], IN_FIRST, 0)
            first_tap(ORDER[2], IN_FIRST, 0, 0)
            act.wait_ge(loaded_small[1], SMALL[1])
            act.activation(wdt_r[:, 0], wdt_sb, ACT.Copy).then_inc(S["small_hi"], 1)
            for q in range(1, BATCH):
                hi_xr(q)
            hi_chunk(6)
            silu_conv(ORDER[1], IN_FIRST, 0)
            first_tap(ORDER[3], IN_FIRST, 0, 0)
            hi_chunk(7)
            silu_conv(ORDER[2], IN_FIRST, 0)
            first_tap(ORDER[4], IN_FIRST, 0, 0)
            act.activation(neg_a, neg_a, ACT.Exp).then_inc(a_step, 1)
            act.wait_ge(a_step, A_SQUARES[1] + 1)
            act.mul(neg_a, neg_a, -1.0).then_inc(a_step, 1)
            act.wait_ge(v_step, V_NEG)
            act.activation(e, neg, ACT.Exp).then_inc(a_step, 1)
            act.wait_ge(v_step, V_U)
            act.activation(lnu, u, ACT.Ln).then_inc(a_step, 1)
            hi_chunk(8)
            act.wait_ge(v_step, V_DT)
            act.wait_ge(a_step, A_NEGA)
            act.activation(dec, dtT, ACT.Exp, scale=neg_a).then_inc(a_step, 1)
            act.wait_ge(v_step, V_RESET)
            act.activation(hi, dec, ACT.Copy).then_inc(a_step, 1)
            pb = await_full(act, IN_SETUP, ("dtt", 0))
            is_free(act.activation(dt_tok[:, :, :].rearrange("p c n -> p (c n)"), pb[:, 0:2 * P], ACT.Copy), IN_SETUP,
                    ("dtt", 0))
            act.wait_ge(v_step, V_PART)
            act.activation(mid, part, ACT.Copy).then_inc(a_step, 1)
            hi_chunk(9)
            first_tap(ORDER[5], IN_FIRST, 0, 0)
            silu_conv(ORDER[3], IN_FIRST, 0)
            first_tap(PAIRS - 3, IN_BEGIN, 0, 0, "carried")
            hi_chunk(10)
            hi_chunk(11)
            silu_conv(ORDER[4], IN_FIRST, 0)

            def hi_gu(m, r):
                act.wait_ge(loaded_gu[r], (m - r) * 8 + 16)
                act.activation(wgu_r[:, r, 0].rearrange("p k g n -> p (k g n)"), raw_gu[:, r, :], ACT.Copy)\
                   .then_inc(S["gu_hi"], 1)

            def hi_d(m, r):
                act.wait_ge(loaded_d[r], (m - r) * 8 + 16)
                act.activation(wd_r[:, r, 0, :], raw_d[:, r, :], ACT.Copy).then_inc(S["d_hi"], 1)

            for b, table, it, prev, last in sequences(act):
                for i in steps_of(last):
                    for unit in convolved_at(i, last) if i > 0 or prev else ():
                        first_tap(unit, table, it, b if i < 3 else b + 1, "xp" if i > 0 else "carried")
                    if i == 0 and not prev:
                        silu_conv(ORDER[5], IN_FIRST, 0)
                        act.wait_ge(v_step, V_DECAY)
                    if i < PAIRS:
                        pb = await_full(act, table, ("xtr", i), it)
                        slot_free(act, table, i, it)
                        if i == 0:
                            reached(act, "xdt_ready", b * PAIRS)
                            act.activation(dt_seq[:], dt_tok[:, :, at(b, HEADS, HEADS)], ACT.Copy).then_inc(S["dt_ready"], 1)
                            reached(act, "dt_ready", b + 1)
                        for c in range(2):
                            for n in range(4):
                                cols = slice(HD * n, HD * n + HD)
                                ins = act.activation(xdt[:, i % 2, c, cols], pb[:, c * 256 + HD * n:c * 256 + HD * n + HD],
                                                     ACT.Copy, scale=dt_seq[:, c, 4 * i + n:4 * i + n + 1])
                        ins.then_inc(S["xdt_ready"], 1)
                        reached(act, "xdt_ready", b * PAIRS + i + 1)
                        act.sem_inc(bank_free[table[("xtr", i)][0]], 1)
                        pb = await_full(act, table, ("z", i), it)
                        reached(act, "g_ready", b * PAIRS + i - 1)
                        ins = act.activation(sz[:, i % 2, :], pb[:, :], ACT.Silu)
                        is_free(ins, table, ("z", i))
                    if i == PAIRS - 1 and last:
                        hi_gu(0, 0)
                    if i == 0:
                        pb = await_full(act, table, ("s", 0), it)
                        reached(act, "m0_ready", b * PAIRS)
                        reached(act, "m_rest_ready", b * PAIRS)
                        ins = act.activation(s_sb[:], pb[:, 0:SEQ + P], ACT.Copy)
                        is_free(ins, table, ("s", 0))
                    for q in XN_AT.get(i, ()) if last else ():
                        pb = await_full(act, table, ("xn", q), it)
                        ins = act.activation(xnT[:, 0, :, SEQ * q:SEQ * q + SEQ], pb[:, :].rearrange("p (k t) -> p k t", k=KH),
                                             ACT.Copy)
                        ins.then_inc(S["xn_hi"], 1)
                    if last and i == 3:
                        act.activation(wgate_r[:, 0].rearrange("p k (c e) -> p k c e", e=NE), wgate_all, ACT.Copy)\
                           .then_inc(S["small_hi"], 1)
                    if last and i == ROUTE_STEP:
                        for n in range(2):
                            pb = await_full(act, table, ("gate", n), it)
                            ins = act.activation(probT[:, 512 * n:512 * n + 512], pb[0:NE, :], ACT.Exp, scale=-1.0)
                            is_free(ins, table, ("gate", n))
                    if not prev:
                        act.activation(xn_all[:, i, :], xn_all[:, i, :], ACT.Copy, scale=st[:, 4, i:i + 1]).then_inc(a_step, 1)
                    h = in_step(i, 2, prev)
                    if h is not None:
                        reached(act, "g_ready", b * PAIRS + h + 1)
                        if h == 0:
                            if prev:
                                await_full(act, table, ("ssq", -1), it)
                            dst = gsq[:, :]
                        else:
                            if h != 1 or prev:
                                reached(act, "gsq_ready", sums(b, h - 2 if h != 1 else -1))
                            dst = sq[:, h % 2, :]
                        act.activation(dst, y_sb[:, h % 2, :], ACT.Square).then_inc(S["sq_ready"], 1)
                        reached(act, "op_done", b * PAIRS + h - 1)
                        act.activation(g_r[:, 0, h % 2, :], y_sb[:, h % 2, :], ACT.Copy).then_inc(S["g_hi"], 1)
                    for unit in convolved_at(i, last):
                        own = i < 3
                        if unit < PAIRS and (prev or not own):
                            await_read(act, table, ("y", -1 if own else unit), it)
                        silu_conv(unit, table, it, "xp" if i > 0 else "carried")
                    if last and i == COMB_STEP:
                        for n in range(2):
                            pb = await_full(act, table, ("comb", n), it)
                            ins = act.activation(combT[0:NR, 512 * n:512 * n + 512], pb[0:NR, :], ACT.Copy)
                            is_free(ins, table, ("comb", n))
                        await_read(act, table, ("comb", 0), it)
                        await_read(act, table, ("comb", 1), it)
                        act.activation(comb_split[0:NR, :], combT[0:NR, :], ACT.Copy).then_inc(ra_step, 1)
                    if last and i == COMB_STEP + 1:
                        act.wait_ge(r_step, R_PART)
                        act.activation(cmid[0:NR, 0:TOK], cpart[0:NR, :], ACT.Copy).then_inc(ra_step, 1)
                        act.wait_ge(ra_step, RA_HI + 1)
                        act.activation(comb_split[32:32 + NR, :], cmid[0:NR, 0:TOK], ACT.Copy).then_inc(ra_step, 1)

            def hidden(base, count, table, routed):
                made = ("comb" if routed else "up")
                for m, r, first, last in tiles(act, count):
                    for u in range(2):
                        n = (m + base) * 2 + u
                        if not (first and u == 0):
                            high_half(table, made, m if u else m - 1, 1 - u, r if u else 1 - r, n)
                        pb = await_full(act, table, ("gate", u), m)
                        b2, n2 = fills(table, ("up", u), m)
                        act.wait_ge(bank_free[b2], n2 - 1)
                        if routed and first and u == 0:
                            reached(act, "gsq_ready", BATCH * (PAIRS - 1))
                        ins = act.activation(sg[:, u, :], pb[:, :], ACT.Silu)
                        is_free(ins, table, ("gate", u))
                        if u == 0:
                            if routed or not last:
                                hi_gu(m + (base + 1), 1 - r)
                            hi_d(m + base, r)
                    if routed and isinstance(m, int) and m == 1:
                        await_read(act, IN_LAST, ("op", 0))
                        for q in range(TT):
                            ins = act.activation(x1r[:, q, :], xn_all[:, q, :], ACT.Square, accum_out=ssq_x1[:, q:q + 1])
                        ins.then_inc(S["ssq_ready"], 1)
                    if not routed and first:
                        for q in range(4):
                            pb = await_full(act, IN_MOE_ACC, ("acc", q))
                            ins = act.activation(gm[:, 2 * q:2 * q + 2, :], pb[:, :].rearrange("p (q n) -> p q n", q=2), ACT.Silu)
                            is_free(ins, IN_MOE_ACC, ("acc", q))
                    if last:
                        high_half(table, made, m, 1, r, n + 1)

            def high_half(table, made, m, u, r, n):
                await_read(act, table, (made, u), m)
                reached(act, "down_done", n - 4)
                act.activation(hid[:, r, 0, u * HALF:u * HALF + HALF], hraw[:, u, :], ACT.Copy).then_inc(S["h_hi"], 1)

            hidden(0, FT, IN_MOE, True)
            for q in range(4):
                pb = await_full(act, IN_X1T, ("x1t", q))
                for k in range(KH):
                    ins = act.activation(x1T[:, 0, k, SEQ * q:SEQ * q + SEQ], pb[:, 256 * k:256 * k + 256], ACT.Copy,
                                         scale=ln2_sb[:, k:k + 1])
                ins.then_inc(S["x1t_hi"], 1)
            hidden(FT, MT, IN_MLP, False)

        @block.gpsimd
        def _(pool):
            for n in ("wx_last_split", "wo_scaled", "g_split", "wzo_split", "m_rest_ready", "g_ready", "gsq_ready",
                      "rstd_ready", "gu_split", "d_split", "rstd1_ready", "xx_step"):
                pool.sem_inc(S[n], CREDIT)
            steps = [0]

            def step(ins):
                steps[0] += 1
                ins.then_inc(p_step, 1)
                pool.wait_ge(p_step, steps[0])

            for g, (a, b) in enumerate(LN_GROUPS):
                pool.wait_ge(a_step, A_SQUARES[g])
                var, rstd, both = st[:, 2, a:b], st[:, 4, a:b], st[:, 5, a:b]
                step(pool.tensor_scalar(var, var, 1.0 / HID, None, ALU.mult))
                step(pool.tensor_scalar(rstd, var, EPS, None, ALU.add))
                step(pool.tensor_tensor(rstd, rstd, power[:, a:b], ALU.pow))
                step(pool.tensor_tensor(both, rstd, rstd, ALU.mult))
                step(pool.tensor_tensor(both, both, var, ALU.mult))
                step(pool.tensor_scalar(both, both, EPS, None, ALU.add))
                step(pool.tensor_tensor(both, both, power[:, a:b], ALU.pow))
                step(pool.tensor_tensor(both, both, rstd, ALU.mult))
                assert steps[0] == P_RSTD * (g + 1)
                if g == 0:
                    continue
                split_wx(pool, NCH - 1, "wx_last_split")
            pool.wait_ge(loaded_small[1], SMALL[1])

            def scale_wo(c):
                n = 2 * NCH + c
                pool.wait_ge(loaded_raw[RAW_PLACE[n]], 16 * (n // 4 + 1))
                rows = raw[RAW_PLACE[n]][:, 0:1024].rearrange("p (j n) -> p j n", j=4)
                pool.tensor_tensor(rows, rows, mn[:, 4 * c:4 * c + 4].unsqueeze(2).to_broadcast([P, 4, HID]), ALU.mult)\
                    .then_inc(S["wo_scaled"], 1)

            split_chunk(pool, 4)
            split_chunk(pool, 5)
            split_chunk(pool, 6)
            scale_wo(0)
            split_chunk(pool, 7)
            scale_wo(1)
            split_chunk(pool, 8)
            scale_wo(2)
            split_chunk(pool, 9)
            scale_wo(3)
            split_chunk(pool, 10)
            await_read(pool, IN_SETUP, ("dtt", 0))

            def split_d(n, r):
                reached(pool, "d_hi", n + 1)
                pool.tensor_tensor(wd_r[:, r, 1, :], raw_d[:, r, :], wd_r[:, r, 0, :].bitcast(F32), ALU.subtract)\
                    .then_inc(S["d_split"], 1)

            def root(key, table, it):
                await_read(pool, table, key, it)
                pool.tensor_tensor(rstd_g[:], var_g[:], power[:, 0:2], ALU.pow).then_inc(S["rstd_ready"], 1)

            for b, table, it, prev, last in sequences(pool):
                for i in steps_of(last):
                    if i < PAIRS:
                        r = i % 2
                        slot_free(pool, table, i, it)
                        await_read(pool, table, ("bcb", i), it)
                        if i == 0:
                            await_read(pool, table, ("s", 0), it)
                        mm = m0[:, r, 2:4, :]
                        pool.tensor_tensor(mm, mm, s_sb[:, 0:SEQ].unsqueeze(1).to_broadcast([P, 2, SEQ]), ALU.mult)
                        ins = pool.tensor_tensor(m1[:, r, :, :], m1[:, r, :, :],
                                                 s_sb[:, SEQ:SEQ + P].unsqueeze(1).to_broadcast([P, 4, P]), ALU.mult)
                        ins.then_inc(S["m_rest_ready"], 1)
                    if i == 2 and prev:
                        root(("ssq", -1), table, it)
                    h = in_step(i, 2, prev)
                    if h is not None:
                        reached(pool, "g_hi", b * PAIRS + h + 1)
                        pool.tensor_tensor(g_r[:, 1, h % 2, :], y_sb[:, h % 2, :], g_r[:, 0, h % 2, :].bitcast(F32),
                                           ALU.subtract).then_inc(S["g_split"], 1)
                    h = in_step(i, 1, prev)
                    if h is not None:
                        await_read(pool, table, ("y", h), it)
                        if h >= 0:
                            await_read(pool, table, ("z", h), it)
                        else:
                            reached(pool, "xdt_ready", b * PAIRS + 1)
                        yv = y_sb[:, h % 2, :]
                        pool.tensor_tensor(yv, yv, sz[:, h % 2, :], ALU.mult).then_inc(S["g_ready"], 1)
                    h = in_step(i, 2, prev)
                    if h is not None and h != 0 and h % 2 == 0:
                        add_squares(pool, b, h)
                    if i == PAIRS + 2:
                        root(("ssq", 0), table, it)

            for base, count, routed in ((0, FT, True), (FT, MT, False)):
                for m, r, first, last in tiles(pool, count):
                    if routed or not last:
                        split_gu(pool, m + (base + 1), 1 - r)
                    split_d(m + base, r)
                    if routed and isinstance(m, int) and m == 1:
                        reached(pool, "var1_ready", 1)
                        pool.tensor_tensor(rstd_x1[:], var_x1[:], power[:], ALU.pow).then_inc(S["rstd1_ready"], 1)
                    if not routed and first:
                        for n in range(4):
                            await_read(pool, IN_MOE_ACC, ("acc", n))
                        reached(pool, "x1r_ready", 1)
                        pool.tensor_tensor(xn_all[:], xn_all[:], gm, ALU.mult).then_inc(S["xx_step"], 1)
                    if not routed and isinstance(m, int) and m == 1:
                        reached(pool, "xx_step", 1)
                        pool.wait_ge(loaded_xx, 16)
                        pool.tensor_tensor(xx, xx, xn_all[:], ALU.add).then_inc(S["xx_step"], 1)

        @block.tensor
        def _(pe):
            for n in ("op_done", "down_done"):
                pe.sem_inc(S[n], CREDIT)
            pe.wait_ge(loaded_small[0], SMALL[0])

            def transposes(table, key, it, tile):
                pb = await_free(pe, table, key, it)
                for k in range(KH):
                    for c in range(2):
                        ins = pe.transpose(pb[:, 256 * k + P * c:256 * k + P * c + P], tile(c)[:, k * P:k * P + P], ident)
                is_full(ins, table, key)

            def transpose_xr(q):
                pe.wait_ge(v_step, V_XR[0 if q == 0 else 1])
                transposes(IN_SETUP, ("xr", q), 0, lambda c: xr_tile(2 * q + c))

            def project(dst, w, col, tokens):
                for k in range(KH):
                    ins = product(pe, dst, lambda s: w[:, s, k, col:col + P], lambda s: xrT[:, s, k, tokens],
                                  k == 0, k == KH - 1)
                return ins

            def project_x(unit, table, it, tokens):
                pb = await_free(pe, table, ("xp", unit), it)
                for jj in range(2 if unit < PAIRS else 1):
                    ins = project(pb[:, jj * SEQ:jj * SEQ + SEQ], wx_v, (2 * unit + jj) * P, tokens)
                is_full(ins, table, ("xp", unit))

            def project_first(n):
                unit = ORDER[n]
                c = min(unit // 2, NCH - 1)
                reached(pe, "wx_split", min(c + 1, 3))
                reached(pe, "wx_last_split", max(c - 2, 0))
                project_x(unit, IN_FIRST, 0, slice(0, SEQ))

            transpose_xr(0)
            await_read(pe, IN_SETUP, ("xr", 0))
            project_first(0)
            project_first(1)
            project_first(2)
            for q in range(1, BATCH):
                transpose_xr(q)
            project_first(3)
            for q in range(1, BATCH):
                await_read(pe, IN_SETUP, ("xr", q))
            pe.wait_ge(v_step, V_WDT)
            for n in range(2):
                pb = await_free(pe, IN_SETUP, ("dt", n))
                for b in (2 * n, 2 * n + 1):
                    for k in range(KH):
                        ins = product(pe, pb[:, (b % 2) * SEQ:(b % 2) * SEQ + SEQ], lambda s: wdt_r[:, s, k, :],
                                      lambda s: xrT[:, s, k, b * SEQ:b * SEQ + SEQ], k == 0, k == KH - 1)
                is_full(ins, IN_SETUP, ("dt", n))
            for unit in (4, 5):
                project_first(unit)
            pe.wait_ge(v_step, V_DT)
            pb = await_free(pe, IN_SETUP, ("dtt", 0))
            for c in range(2):
                ins = pe.transpose(pb[:, c * P:c * P + P], dtT[:, c * P:c * P + P], ident)
            is_full(ins, IN_SETUP, ("dtt", 0))
            project_first(6)
            pe.wait_ge(v_step, V_DECAY)

            def squares_sum(key, done, table, it):
                pb = await_free(pe, table, key, it)
                reached(pe, "gsq_ready", done)
                for c in range(2):
                    for jj in range(2):
                        ins = pe.matmul(pb[:, c:c + 1], gsq[:, jj * SEQ + c * P:jj * SEQ + c * P + P], ones[:],
                                        start=(jj == 0), stop=(jj == 1))
                is_full(ins, table, key)

            def product_of(name, m, r, u, table, src, base):
                toks = slice(u * HALF, u * HALF + HALF)
                pb = await_free(pe, table, (name, u), m)
                if name == "comb":
                    ins = pe.matmul(pb[:, :], sel_exp[:, at(m, P, P)], comb_split[:, toks], start=True, stop=True)
                else:
                    if u == 0 and name == "gate":
                        reached(pe, "gu_split", m + (base + 1))
                    g = 0 if name == "gate" else 1
                    for k in range(KH):
                        ins = product(pe, pb[:, :], lambda s: wgu_r[:, r, s, k, g, :], lambda s: src[:, s, k, toks],
                                      k == 0, k == KH - 1)
                is_full(ins, table, (name, u))

            for b, table, it, prev, last in sequences(pe):
                toks = at(b, SEQ, SEQ)
                nxt = None if last else at(b + 1, SEQ, SEQ)
                for i in steps_of(last):
                    if i < PAIRS:
                        pb = await_free(pe, table, ("xtr", i), it)
                        if i > 3:
                            reached(pe, "xs_ready", b * UNITS + place(i) + 1)
                        for c in range(2):
                            for jj in range(2):
                                ins = pe.transpose(pb[:, c * 256 + jj * P:c * 256 + jj * P + P],
                                                   xsT_v[:, 2 * i + jj, c * P:c * P + P], ident)
                        is_full(ins, table, ("xtr", i))
                        for n, name in enumerate(("bca", "bcb")):
                            pb = await_free(pe, table, (name, i), it)
                            for hh in range(2):
                                h = 4 * i + 2 * n + hh
                                ins = pe.matmul(pb[:, hh * SEQ:hh * SEQ + SEQ], sel_head[:, h:h + 1].to_broadcast([SPLIT * HEADS, P]),
                                                decay0[:, toks], start=True, stop=True)
                            is_full(ins, table, (name, i))
                        if i % 2 == 0 and not prev:
                            reached(pe, "wzo_split", i // 2 + 1)
                        pb = await_free(pe, table, ("z", i), it)
                        for jj in range(2):
                            ins = project(pb[:, jj * SEQ:jj * SEQ + SEQ], wz_v, (2 * i + jj) * P, toks)
                        is_full(ins, table, ("z", i))
                    h = in_step(i, 1, prev)
                    if h is not None:
                        r = h % 2
                        pb = await_free(pe, table, ("y", h), it)
                        reached(pe, "xdt_ready", b * PAIRS + h + 1)
                        reached(pe, "m0_ready", b * PAIRS + h + 1)
                        reached(pe, "m_rest_ready", b * PAIRS + h + 1)
                        for jj in range(2):
                            for hh in range(2):
                                n = 2 * jj + hh
                                rows = slice(HD * hh, HD * hh + HD)
                                pe.matmul(pb[rows, jj * SEQ:jj * SEQ + SEQ], xdt[:, r, 0, n * HD:n * HD + HD], m0[:, r, n, :],
                                          start=True, stop=False)
                                ins = pe.matmul(pb[rows, jj * SEQ + P:jj * SEQ + SEQ], xdt[:, r, 1, n * HD:n * HD + HD],
                                                m1[:, r, n, :], start=False, stop=True)
                        is_full(ins, table, ("y", h))
                    if i == 0:
                        reached(pe, "xs_ready", b * UNITS + place(PAIRS) + 1)
                        pb = await_free(pe, table, ("s", 0), it)
                        pe.matmul(pb[:, 0:SEQ], bT[:, 0:P], cT[:, :], start=True, stop=True)
                        ins = pe.matmul(pb[:, SEQ:SEQ + P], bT[:, P:SEQ], cT[:, P:SEQ], start=True, stop=True)
                        is_full(ins, table, ("s", 0))
                    if i == 2 and prev:
                        squares_sum(("ssq", -1), sums(b, -1), table, it)
                    for unit in units_at(i, last):
                        project_x(unit, table, it, toks if i < 2 else nxt)
                    for q in XN_AT.get(i, ()) if last else ():
                        reached(pe, "xq_normed", q + 1)
                        transposes(table, ("xn", q), it, lambda c: acc[:, q % 2, c, :])
                    if last and i == ROUTE_STEP:
                        reached(pe, "wgate_split", 1)
                        for q in range(BATCH):
                            await_read(pe, table, ("xn", q), it)
                        for n in range(2):
                            pb = await_free(pe, table, ("gate", n), it)
                            for k in range(KH):
                                ins = product(pe, pb[:, :], lambda s: wgate_r[:, s, k, :],
                                              lambda s: xnT[:, s, k, HALF * n:HALF * n + HALF], k == 0, k == KH - 1)
                            is_full(ins, table, ("gate", n))
                    if last and i == ROUTE_STEP + 1:
                        pb = await_free(pe, table, ("prob", 0), it)
                        for n in range(2):
                            await_read(pe, table, ("gate", n), it)
                        for t in range(TT):
                            ins = pe.transpose(pb[:, t * NE:t * NE + NE], probT[:, t * P:t * P + P], ident[0:NE, 0:NE])
                        is_full(ins, table, ("prob", 0))
                    h = in_step(i, 3, prev)
                    if h is not None:
                        if h == 0:
                            if prev:
                                await_read(pe, table, ("op", -1), it)
                            else:
                                await_read(pe, IN_SETUP, ("dtt", 0))
                        if h == 0 and not prev:
                            reached(pe, "wzo_split", 2 * NCH)
                        reached(pe, "g_split", b * PAIRS + h + 1)
                        for jj in range(2):
                            for c in range(2):
                                gcol = jj * SEQ + c * P
                                for n, (s, s2) in enumerate(((0, 0), (0, 1), (1, 0))):
                                    ins = pe.matmul(bank[OPB][:, c * HID:c * HID + HID], g_r[:, s, h % 2, gcol:gcol + P],
                                                    wo_v[:, s2, 2 * (h % PAIRS) + jj, :],
                                                    start=(h == 0 and jj == 0 and c == 0 and n == 0),
                                                    stop=(h % PAIRS == PAIRS - 1 and jj == 1 and n == 2), skip_group_check=True)
                        ins.then_inc(S["op_done"], 1)
                        if h % PAIRS == PAIRS - 1:
                            reached(pe, "op_done", b * PAIRS + h + 1)
                            pe.sem_inc(bank_full[OPB], 1)
                    if last and i == COMB_STEP:
                        pe.wait_ge(r_step, R_COMB)
                        for n in range(2):
                            pb = await_free(pe, table, ("comb", n), it)
                            for t in range(4):
                                ins = pe.transpose(pb[0:NR, t * P:t * P + P], combx[:, 4 * n + t, :], ident)
                            is_full(ins, table, ("comb", n))
                    if i == PAIRS + 1:
                        for name, u in EARLY:
                            product_of(name, 0, 0, u, IN_MOE, xnT, 0)
                    if i == PAIRS + 2:
                        squares_sum(("ssq", 0), sums(b, PAIRS - 1), table, it)

            def hidden(base, count, table, acc_table, routed):
                src = xnT if routed else x1T

                def down(m, r, u, first, last, n):
                    if u == 0:
                        reached(pe, "d_split", m + (base + 1))
                    if first:
                        for h in (2 * u, 2 * u + 1):
                            await_free(pe, acc_table, ("acc", h))
                    reached(pe, "h_split", n + 1)
                    for q in range(4 * u, 4 * u + 4):
                        for p, (s, s2) in enumerate(((0, 0), (0, 1), (1, 0))):
                            ins = pe.matmul(bank[ACC + q // 2][:, (q % 2) * HID:(q % 2) * HID + HID],
                                            hid[:, r, s, q * P:q * P + P], wd_r[:, r, s2, :],
                                            start=(first and q % 2 == 0 and p == 0), stop=(last and p == 2),
                                            skip_group_check=True)
                        if last and q % 2 == 1:
                            ins.then_inc(bank_full[ACC + q // 2], 1)
                    if not last:
                        ins.then_inc(S["down_done"], 1)
                    else:
                        pe.wait_ge(bank_full[ACC + 2 * u + 1], fills(acc_table, ("acc", 2 * u + 1))[1] + 1)
                        pe.sem_inc(S["down_done"], 1)

                for m, r, first, last in tiles(pe, count):
                    if routed and first:
                        pe.wait_ge(r_step, R_SPLIT)
                        pe.wait_ge(loaded_sel, 16)
                        for name, u in (("comb", 0), ("up", 1), ("comb", 1)):
                            product_of(name, m, r, u, table, src, base)
                        continue
                    for u in range(2):
                        if not routed and first:
                            for q in (2 * u, 2 * u + 1):
                                await_read(pe, IN_X1T, ("x1t", q))
                        for name in ("gate", "comb", "up") if routed else ("gate", "up"):
                            product_of(name, m, r, u, table, src, base)
                        if not first:
                            down(m - 1, 1 - r, u, isinstance(m, int) and m == 1, False, (m + (base - 1)) * 2 + u)
                    if last:
                        for u in range(2):
                            if routed:
                                if u == 0:
                                    reached(pe, "x1r_ready", 1)
                                for q in (2 * u, 2 * u + 1):
                                    transposes(IN_X1T, ("x1t", q), 0, lambda c: x1r[:, 2 * q + c, :])
                            down(m, r, u, False, True, (m + base) * 2 + u)

            hidden(0, FT, IN_MOE, IN_MOE_ACC, True)
            hidden(FT, MT, IN_MLP, IN_MLP_ACC, False)


def kernel(**inputs):
    import numpy as np
    import concourse.bacc as bacc
    from concourse.bass_utils import run_bass_kernel_spmd
    import ml_dtypes

    a = {k: np.asarray(v) for k, v in inputs.items()}
    f32, bf16 = np.float32, ml_dtypes.bfloat16

    def rows(w, k):
        return w.reshape(k, P, -1).transpose(1, 0, 2)

    proj = a["L0_attn_in_proj_w"]
    gate_rows = np.concatenate([a["L0_ffn_exp_wg"].reshape(NE * FF, HID), a["L0_ffn_shared_wg"]])
    up_rows = np.concatenate([a["L0_ffn_exp_wu"].reshape(NE * FF, HID), a["L0_ffn_shared_wu"]])
    down_rows = np.concatenate([a["L0_ffn_exp_wd"].transpose(0, 2, 1).reshape(NE * FF, HID), a["L0_ffn_shared_wd"].T])
    pad = FFP - gate_rows.shape[0]
    gate_rows, up_rows, down_rows = (np.pad(w, ((0, pad), (0, 0))) for w in (gate_rows, up_rows, down_rows))
    owner = np.minimum(np.arange(FFP) // FF, NE)
    sel_exp = np.zeros((SPLIT * 32, FFP), bf16)
    sel_head = np.zeros((SPLIT * HEADS, HEADS), bf16)
    for s in range(SPLIT):
        sel_exp[32 * s + owner, np.arange(FFP)] = 1
        sel_head[HEADS * s + np.arange(HEADS), np.arange(HEADS)] = 1
    eye = np.zeros((P, 2 * SEQ), f32)
    for h in range(2):
        eye[np.arange(P), h * SEQ + np.arange(P)] = 1
    wxT = rows(proj[DIN:2 * DIN + 2 * NST].T, KH)
    wzT = rows(proj[:DIN].T, KH)
    mlp = a["L0_attn_mlp_in_w"]
    gate_all, up_all = np.concatenate([gate_rows, mlp[:INTER]]), np.concatenate([up_rows, mlp[INTER:]])
    gu = np.stack([gate_all, up_all]).reshape(2, FT + MT, P, KH, P)
    small = {
        "ident": np.eye(P, dtype=f32),
        "ln1": a["L0_attn_ln1_w"].reshape(KH, P).T,
        "conv_w": a["L0_attn_conv_w"].reshape(CT + 1, P, TAPS).transpose(1, 0, 2),
        "conv_b": a["L0_attn_conv_b"].reshape(CT + 1, P).T,
        "wdt": np.tile(rows(proj[2 * DIN + 2 * NST:].T, KH), (1, 1, BATCH)),
        "wgate": rows(a["L0_ffn_gate_w"].T, KH),
        "iota": np.broadcast_to(np.arange(NE, dtype=f32), (P, TT, NE)),
        "d_col": np.repeat(a["L0_attn_D_param"], HD).reshape(CT, P).T,
        "mnorm": a["L0_attn_mnorm_w"].reshape(CT, P).T,
        "ln2": a["L0_attn_ln2_w"].reshape(KH, P).T,
        "dt_bias": np.tile(a["L0_attn_dt_bias"], BATCH),
        "a_log": np.tile(a["L0_attn_A_log"], BATCH),
    }
    arrays = {
        "x": a["L0_attn_x"].reshape(TT, P, HID).transpose(1, 0, 2),
        "wx": np.concatenate([wxT[:, :, c:c + n].reshape(P, -1) for c, n in WX_CHUNKS], 1),
        "wz": wzT.reshape(P, KH, NCH, -1).transpose(0, 2, 1, 3).reshape(P, -1),
        "wo": rows(a["L0_attn_out_proj_w"].T, CT).reshape(P, -1),
        "wgu": gu.transpose(1, 4, 3, 0, 2).reshape((FT + MT) * P, -1),
        "wd": np.concatenate([down_rows, a["L0_attn_mlp_out_w"].T]),
        "pack_a": np.concatenate([small[n].reshape(P, c) for n, c in PACK_A], 1),
        "pack_b": np.concatenate([small[n].reshape(P, c) for n, c in PACK_B], 1),
        "eye": eye,
        "sel_head": sel_head,
        "sel_exp": sel_exp,
    }
    nc = bacc.Bacc("TRN2", target_bir_lowering=False, num_devices=1)
    args, feed = [], {}
    for name, arr in arrays.items():
        arr = np.ascontiguousarray(arr)
        feed[f"in_{name}_dram"] = arr
        args.append(nc.dram_tensor(f"in_{name}_dram", arr.shape, mybir.dt.from_np(arr.dtype), kind="ExternalInput").ap())
    out = nc.dram_tensor("out_0_dram", (P, TT, HID), F32, kind="ExternalOutput").ap()
    build(nc, *args, out)
    r = run_bass_kernel_spmd(nc, [feed], core_ids=[0])
    got = r.results[0]["out_0_dram"]
    return np.ascontiguousarray(got.transpose(1, 0, 2).reshape(BATCH, SEQ, HID))
```
